# Optimizing a Trainium2 kernel written in Bass

```python
import numpy as np
import jax
import jax.numpy as jnp

def _softmax(x, axis=-1):
    return jax.nn.softmax(x, axis=axis)

def _gelu(x):
    return jax.nn.gelu(x, approximate=True)

def _silu(x):
    return jax.nn.silu(x)

def _sigmoid(x):
    return jax.nn.sigmoid(x)

def _layernorm(x, axis=-1, eps=1e-05):
    m = jnp.mean(x, axis=axis, keepdims=True)
    v = jnp.var(x, axis=axis, keepdims=True)
    return (x - m) / jnp.sqrt(v + eps)

def _scatter_add(tgt, idx, src, axis=0):
    return tgt.at[idx].add(src)

def _segment_sum(src, seg, n):
    return jax.ops.segment_sum(src, seg, n)
kernel_name = 'mk_xattn_ffn_d4_seqx_r4_e9e46a'

def setup_inputs(seed: int=0):
    np.random.seed(seed)
    _w = jnp.asarray

    def _rec_inputs():
        import jax
        import jax.numpy as jnp
        _rk = jax.random.key(seed)
        x = 7.22e-05 + 1 * jax.random.normal(jax.random.fold_in(_rk, 1), (16, 112, 256), jnp.float32)
        _lenS = 112 - jax.random.randint(jax.random.fold_in(_rk, 7), (16,), 0, max(1, 112 // 4) + 1, jnp.int32)
        _lenS2 = 375 - jax.random.randint(jax.random.fold_in(_rk, 8), (16,), 0, max(1, 375 // 4) + 1, jnp.int32)
        _ctx_1024P = jax.random.normal(jax.random.fold_in(_rk, 11), (16, 16, 256), jnp.float32)
        _ctx_1024c = jax.random.dirichlet(jax.random.fold_in(_rk, 511), 0.3 * jnp.ones((16,), jnp.float32), (16, 375))
        _ctx_1024t = jnp.einsum('bsk,bkd->bsd', _ctx_1024c, _ctx_1024P)
        _ctx_1024t = _ctx_1024t * jax.lax.rsqrt(jnp.mean(jnp.square(_ctx_1024t)) + 1e-12) * 0.953939
        ctx_1024 = -0.000514642 + 1.00011 * (_ctx_1024t + 0.3 * jax.random.normal(jax.random.fold_in(_rk, 611), (16, 375, 256), jnp.float32))
        _validS = jnp.arange(112)[None, :] < _lenS[:, None]
        _validS2 = jnp.arange(375)[None, :] < _lenS2[:, None]
        _causal = jnp.tril(jnp.ones((112, 112), dtype=bool))
        mask_BxS_ik0 = jnp.where(jnp.broadcast_to(_validS[:, :], (16, 112)), 0, 1).astype(jnp.int32)
        mask_1xSxS2_ff0 = jnp.where(jnp.ones((1, 112, 375), dtype=bool), 0.0, -1000000000.0).astype(jnp.float32)
        return (x, ctx_1024, mask_BxS_ik0, mask_1xSxS2_ff0)
    x, ctx_1024, mask_BxS_ik0, mask_1xSxS2_ff0 = _rec_inputs()

    def _L0_xattn_setup():
        import jax, jax.numpy as jnp
        import numpy as np
        B, S, P, D, H = (2, 1024, 256, 256, 16)
        key = jax.random.key(seed)
        ks = jax.random.split(key, 8)
        init = 0.02
        queries = jax.random.normal(ks[0], (B, S, D), dtype=jnp.float32)
        patch_representations = jax.random.normal(ks[1], (B, P, D), dtype=jnp.float32)
        patch_boundaries = jax.random.randint(ks[2], (B, S), 0, 2, dtype=jnp.int32)
        wq = jax.random.normal(ks[3], (D, D), dtype=jnp.float32) * init
        wk = jax.random.normal(ks[4], (D, D), dtype=jnp.float32) * init
        wv = jax.random.normal(ks[5], (D, D), dtype=jnp.float32) * init
        wo = jax.random.normal(ks[6], (D, D), dtype=jnp.float32) * init
        bq = jnp.zeros((D,), jnp.float32)
        bk = jnp.zeros((D,), jnp.float32)
        bv = jnp.zeros((D,), jnp.float32)
        bo = jnp.zeros((D,), jnp.float32)
        return {'queries': queries, 'patch_representations': patch_representations, 'patch_boundaries': patch_boundaries, 'wq': wq, 'wk': wk, 'wv': wv, 'wo': wo, 'bq': bq, 'bk': bk, 'bv': bv, 'bo': bo}
    _L0_xattn_all = _L0_xattn_setup()
    _L0_xattn_in = {k: v for k, v in _L0_xattn_all.items() if k in ('wq', 'wk', 'wv', 'wo', 'bq', 'bk', 'bv', 'bo')}
    del _L0_xattn_all

    def _L0_ffn_setup():
        import jax, jax.numpy as jnp
        import numpy as np
        D_MODEL, D_FF, N_EXPERTS, TOP_K = (256, 1024, 8, 2)
        key = jax.random.key(seed)
        k0, k1, k2, k3 = jax.random.split(key, 4)
        x = jax.random.normal(k0, (2, 512, D_MODEL), dtype=jnp.float32)
        Wg = jax.random.normal(k1, (D_MODEL, N_EXPERTS), dtype=jnp.float32) * 0.02
        W1 = jax.random.normal(k2, (N_EXPERTS, D_MODEL, D_FF), dtype=jnp.float32) * 0.02
        b1 = jnp.zeros((N_EXPERTS, D_FF), dtype=jnp.float32)
        W2 = jax.random.normal(k3, (N_EXPERTS, D_FF, D_MODEL), dtype=jnp.float32) * 0.02
        b2 = jnp.zeros((N_EXPERTS, D_MODEL), dtype=jnp.float32)
        return {'x': x, 'Wg': Wg, 'W1': W1, 'b1': b1, 'W2': W2, 'b2': b2}
    _L0_ffn_all = _L0_ffn_setup()
    _L0_ffn_in = {k: v for k, v in _L0_ffn_all.items() if k in ('Wg', 'W1', 'b1', 'W2', 'b2')}
    del _L0_ffn_all

    def _L1_xattn_setup():
        import jax, jax.numpy as jnp
        import numpy as np
        B, S, D_IN, D_MODEL = (4, 512, 256, 256)
        key = jax.random.key(seed)
        ks = jax.random.split(key, 8)
        glorot = np.sqrt(6.0 / (D_IN + D_MODEL))
        inp = {'q': jax.random.normal(ks[0], (B, S, D_IN), dtype=jnp.float32), 'k': jax.random.normal(ks[1], (B, S, D_IN), dtype=jnp.float32), 'v': jax.random.normal(ks[2], (B, S, D_IN), dtype=jnp.float32), 'mask': jnp.zeros((1, S, S), dtype=jnp.float32), 'kernel_q': jax.random.uniform(ks[3], (1, 1, D_IN, D_MODEL), jnp.float32, -glorot, glorot), 'kernel_k': jax.random.uniform(ks[4], (1, 1, D_IN, D_MODEL), jnp.float32, -glorot, glorot), 'kernel_v': jax.random.uniform(ks[5], (1, 1, D_IN, D_MODEL), jnp.float32, -glorot, glorot), 'bias_q': 0.05 * jax.random.normal(ks[6], (D_MODEL,), dtype=jnp.float32), 'bias_k': 0.05 * jax.random.normal(ks[7], (D_MODEL,), dtype=jnp.float32), 'bias_v': 0.05 * jax.random.normal(jax.random.fold_in(key, 7), (D_MODEL,), dtype=jnp.float32)}
        return inp
    _L1_xattn_all = _L1_xattn_setup()
    _L1_xattn_in = {k: v for k, v in _L1_xattn_all.items() if k in ('kernel_q', 'kernel_k', 'kernel_v', 'bias_q', 'bias_k', 'bias_v')}
    del _L1_xattn_all

    def _L1_ffn_setup():
        import jax, jax.numpy as jnp
        import numpy as np
        import math
        B, T, D, H, E, TOPK, CAPF = (4, 512, 256, 16, 8, 2, 2.0)
        HD = D // H

        def layernorm(x, g, b, eps=1e-05):
            m = jnp.mean(x, -1, keepdims=True)
            v = jnp.mean(jnp.square(x - m), -1, keepdims=True)
            return (x - m) * jax.lax.rsqrt(v + eps) * g + b

        def block_forward(x, ln1_g, ln1_b, Wqkv, Wproj, ln2_g, ln2_b, Wgate, W1, b1, W2, b2):
            Bb, Tt, d = x.shape
            hd = HD
            half = hd // 2
            h = layernorm(x, ln1_g, ln1_b)
            qkv = (h @ Wqkv).reshape(Bb, Tt, H, 3 * hd)
            q, k, v = (qkv[..., :hd], qkv[..., hd:2 * hd], qkv[..., 2 * hd:])
            inv_freq = 1.0 / 10000.0 ** (jnp.arange(0, hd, 2, dtype=jnp.float32) / hd)
            ang = jnp.arange(Tt, dtype=jnp.float32)[:, None] * inv_freq
            sin = jnp.sin(ang)[None, :, None, :].astype(x.dtype)
            cos = jnp.cos(ang)[None, :, None, :].astype(x.dtype)

            def rope(t):
                t1, t2 = (t[..., :half], t[..., half:])
                return jnp.concatenate([t1 * cos - t2 * sin, t1 * sin + t2 * cos], -1)
            q, k = (rope(q), rope(k))
            scores = jnp.einsum('bqhd,bkhd->bhqk', q, k) / math.sqrt(hd)
            causal = jnp.tril(jnp.ones((Tt, Tt), dtype=bool))
            scores = jnp.where(causal, scores, jnp.asarray(-1000000000.0, scores.dtype))
            probs = jax.nn.softmax(scores, axis=-1)
            attn = jnp.einsum('bhqk,bkhd->bqhd', probs, v).reshape(Bb, Tt, d) @ Wproj
            x = x + attn
            h2 = layernorm(x, ln2_g, ln2_b)
            flat = h2.reshape(-1, d)
            N = flat.shape[0]
            capacity = int(math.ceil(CAPF * N / E))
            gates = jax.nn.softmax((flat @ Wgate).astype(jnp.float32), -1).astype(flat.dtype)
            _, top_inds = jax.lax.top_k(gates, TOPK)
            mask = jnp.zeros((N, E), dtype=bool).at[jnp.arange(N)[:, None], top_inds].set(True)
            pos = jnp.cumsum(mask.astype(jnp.int32), axis=0) * mask - 1
            keep = (pos < capacity) & mask
            t_flat = jnp.repeat(jnp.arange(N), TOPK)
            e_flat = top_inds.reshape(-1)
            p = pos[t_flat, e_flat]
            kp = keep[t_flat, e_flat]
            p_eff = jnp.where(kp, p, capacity)
            exp_in = jnp.zeros((E, capacity, d), flat.dtype).at[e_flat, p_eff].set(flat[t_flat], mode='drop')
            hmid = jax.nn.gelu(jnp.einsum('ecd,edf->ecf', exp_in, W1) + b1[:, None, :], approximate=False)
            exp_out = jnp.einsum('ecf,efd->ecd', hmid, W2) + b2[:, None, :]
            gate = gates[t_flat, e_flat] * kp.astype(flat.dtype)
            p_g = jnp.minimum(p_eff, capacity - 1)
            moe = jnp.zeros((N, d), flat.dtype).at[t_flat].add(exp_out[e_flat, p_g] * gate[:, None])
            return x + moe.reshape(Bb, Tt, d)
        key = jax.random.key(seed)
        ks = jax.random.split(key, 8)
        s = 0.02
        return {'x': jax.random.normal(ks[0], (B, T, D), jnp.float32), 'ln1_g': jnp.ones((D,), jnp.float32), 'ln1_b': jnp.zeros((D,), jnp.float32), 'Wqkv': jax.random.normal(ks[1], (D, 3 * D), jnp.float32) * s, 'Wproj': jax.random.normal(ks[2], (D, D), jnp.float32) * s, 'ln2_g': jnp.ones((D,), jnp.float32), 'ln2_b': jnp.zeros((D,), jnp.float32), 'Wgate': jax.random.normal(ks[3], (D, E), jnp.float32) * s, 'W1': jax.random.normal(ks[4], (E, D, 4 * D), jnp.float32) * s, 'b1': jnp.zeros((E, 4 * D), jnp.float32), 'W2': jax.random.normal(ks[5], (E, 4 * D, D), jnp.float32) * s, 'b2': jnp.zeros((E, D), jnp.float32)}
    _L1_ffn_all = _L1_ffn_setup()
    _L1_ffn_in = {k: v for k, v in _L1_ffn_all.items() if k in ('ln1_g', 'ln1_b', 'Wqkv', 'Wproj', 'ln2_g', 'ln2_b', 'Wgate', 'W1', 'b1', 'W2', 'b2')}
    del _L1_ffn_all

    def _L2_xattn_setup():
        import jax, jax.numpy as jnp
        import numpy as np
        D_MODEL = 256
        N_HEAD = 16
        D_K = 64
        D_V = 64
        B, S = (4, 512)
        key = jax.random.key(seed)
        ks = jax.random.split(key, 7)
        scale = 1.0 / np.sqrt(D_MODEL)
        return {'q': jax.random.normal(ks[0], (B, S, D_MODEL), jnp.float32), 'k': jax.random.normal(ks[1], (B, S, D_MODEL), jnp.float32), 'v': jax.random.normal(ks[2], (B, S, D_MODEL), jnp.float32), 'Wq': jax.random.normal(ks[3], (D_MODEL, N_HEAD * D_K), jnp.float32) * scale, 'Wk': jax.random.normal(ks[4], (D_MODEL, N_HEAD * D_K), jnp.float32) * scale, 'Wv': jax.random.normal(ks[5], (D_MODEL, N_HEAD * D_V), jnp.float32) * scale, 'Wo': jax.random.normal(ks[6], (N_HEAD * D_V, D_MODEL), jnp.float32) * scale}
    _L2_xattn_all = _L2_xattn_setup()
    _L2_xattn_in = {k: v for k, v in _L2_xattn_all.items() if k in ('Wq', 'Wk', 'Wv', 'Wo')}
    del _L2_xattn_all

    def _L2_ffn_setup():
        import jax, jax.numpy as jnp
        import numpy as np
        D_MODEL = 256
        MLP_DIM = 1024
        N_EXPERTS = 8
        B, T = (4, 256)
        key = jax.random.key(seed)
        ks = jax.random.split(key, 7)
        scale_in = (1.0 / D_MODEL) ** 0.5
        scale_out = (1.0 / MLP_DIM) ** 0.5
        bound_g = (1.0 / D_MODEL) ** 0.5
        w_gate = jax.random.uniform(ks[0], (D_MODEL, N_EXPERTS), minval=-bound_g, maxval=bound_g, dtype=jnp.float32)
        b_gate = jax.random.uniform(ks[1], (N_EXPERTS,), minval=-bound_g, maxval=bound_g, dtype=jnp.float32)
        W1 = jax.random.uniform(ks[2], (N_EXPERTS, D_MODEL, MLP_DIM), minval=-scale_in, maxval=scale_in, dtype=jnp.float32)
        b1 = jnp.zeros((N_EXPERTS, MLP_DIM), dtype=jnp.float32)
        W2 = jax.random.uniform(ks[3], (N_EXPERTS, MLP_DIM, D_MODEL), minval=-scale_out, maxval=scale_out, dtype=jnp.float32)
        b2 = jnp.zeros((N_EXPERTS, D_MODEL), dtype=jnp.float32)
        x = jax.random.normal(ks[4], (B, T, D_MODEL), dtype=jnp.float32)
        return {'x': x, 'w_gate': w_gate, 'b_gate': b_gate, 'W1': W1, 'b1': b1, 'W2': W2, 'b2': b2}
    _L2_ffn_all = _L2_ffn_setup()
    _L2_ffn_in = {k: v for k, v in _L2_ffn_all.items() if k in ('w_gate', 'b_gate', 'W1', 'b1', 'W2', 'b2')}
    del _L2_ffn_all

    def _L3_xattn_setup():
        import jax, jax.numpy as jnp
        import numpy as np
        HEAD_NUM = 16
        KEY_DIM = 64
        EMBED = 256
        KV_OUT = HEAD_NUM * KEY_DIM
        key = jax.random.key(seed)
        ks = jax.random.split(key, 11)
        B, L, E = (2, 512, EMBED)
        scale = 0.02
        return {'query': jax.random.normal(ks[0], (B, L, E), jnp.float32), 'key': jax.random.normal(ks[1], (B, L, E), jnp.float32), 'value': jax.random.normal(ks[2], (B, L, E), jnp.float32), 'W_Query': jax.random.normal(ks[3], (E, KV_OUT), jnp.float32) * scale, 'W_Key': jax.random.normal(ks[4], (E, KV_OUT), jnp.float32) * scale, 'W_Value': jax.random.normal(ks[5], (E, KV_OUT), jnp.float32) * scale, 'W_Output': jax.random.normal(ks[6], (KV_OUT, E), jnp.float32) * scale, 'B_Query': jnp.zeros((KV_OUT,), jnp.float32), 'B_Key': jnp.zeros((KV_OUT,), jnp.float32), 'B_Value': jnp.zeros((KV_OUT,), jnp.float32), 'B_Output': jnp.zeros((E,), jnp.float32)}
    _L3_xattn_all = _L3_xattn_setup()
    _L3_xattn_in = {k: v for k, v in _L3_xattn_all.items() if k in ('W_Query', 'W_Key', 'W_Value', 'W_Output', 'B_Query', 'B_Key', 'B_Value', 'B_Output')}
    del _L3_xattn_all

    def _L3_ffn_setup():
        import jax, jax.numpy as jnp
        import numpy as np
        DIM = 256
        EXPERT_DIM = 128
        N_EXPERTS = 16
        TOPK = 2
        SHARED_HIDDEN = EXPERT_DIM * TOPK
        B, T = (4, 256)

        def _moe_forward(x, router_w, router_bias, up_proj, gate_proj, down_proj, sh_gate, sh_up, sh_down):
            Bb, Tt, D = x.shape
            flat = x.reshape(Bb * Tt, D)
            N = flat.shape[0]
            logits = flat @ router_w.T
            topk_scores, topk_idx = jax.lax.top_k(logits + router_bias, TOPK)
            topk_scores = jax.nn.softmax(topk_scores, axis=-1)
            combine = jnp.zeros((N, N_EXPERTS), flat.dtype)
            combine = combine.at[jnp.arange(N)[:, None], topk_idx].add(topk_scores)
            up_all = jnp.einsum('nd,kde->nke', flat, up_proj)
            gate_all = jnp.einsum('nd,kde->nke', flat, gate_proj)
            hidden = jax.nn.silu(gate_all) * up_all
            down_all = jnp.einsum('nke,ked->nkd', hidden, down_proj)
            out = jnp.einsum('nk,nkd->nd', combine, down_all)
            sh_hidden = jax.nn.silu(flat @ sh_gate.T) * (flat @ sh_up.T)
            out = out + sh_hidden @ sh_down.T
            return out.reshape(Bb, Tt, D)
        key = jax.random.key(seed)
        ks = jax.random.split(key, 9)
        std = 0.02
        return {'x': jax.random.normal(ks[0], (B, T, DIM), jnp.float32), 'router_w': jax.random.normal(ks[1], (N_EXPERTS, DIM), jnp.float32) * std, 'router_bias': jnp.zeros((N_EXPERTS,), jnp.float32), 'up_proj': jax.random.normal(ks[2], (N_EXPERTS, DIM, EXPERT_DIM), jnp.float32) * std, 'gate_proj': jax.random.normal(ks[3], (N_EXPERTS, DIM, EXPERT_DIM), jnp.float32) * std, 'down_proj': jax.random.normal(ks[4], (N_EXPERTS, EXPERT_DIM, DIM), jnp.float32) * std, 'sh_gate': jax.random.normal(ks[5], (SHARED_HIDDEN, DIM), jnp.float32) * std, 'sh_up': jax.random.normal(ks[6], (SHARED_HIDDEN, DIM), jnp.float32) * std, 'sh_down': jax.random.normal(ks[7], (DIM, SHARED_HIDDEN), jnp.float32) * std}
    _L3_ffn_all = _L3_ffn_setup()
    _L3_ffn_in = {k: v for k, v in _L3_ffn_all.items() if k in ('router_w', 'router_bias', 'up_proj', 'gate_proj', 'down_proj', 'sh_gate', 'sh_up', 'sh_down')}
    del _L3_ffn_all
    return {'x': x, 'ctx_1024': ctx_1024, 'mask_BxS_ik0': mask_BxS_ik0, 'mask_1xSxS2_ff0': mask_1xSxS2_ff0, 'L0_xattn_wq': _L0_xattn_in['wq'], 'L0_xattn_wk': _L0_xattn_in['wk'], 'L0_xattn_wv': _L0_xattn_in['wv'], 'L0_xattn_wo': _L0_xattn_in['wo'], 'L0_xattn_bq': _L0_xattn_in['bq'], 'L0_xattn_bk': _L0_xattn_in['bk'], 'L0_xattn_bv': _L0_xattn_in['bv'], 'L0_xattn_bo': _L0_xattn_in['bo'], 'L0_ffn_Wg': _L0_ffn_in['Wg'], 'L0_ffn_W1': _L0_ffn_in['W1'], 'L0_ffn_b1': _L0_ffn_in['b1'], 'L0_ffn_W2': _L0_ffn_in['W2'], 'L0_ffn_b2': _L0_ffn_in['b2'], 'L1_xattn_kernel_q': _L1_xattn_in['kernel_q'], 'L1_xattn_kernel_k': _L1_xattn_in['kernel_k'], 'L1_xattn_kernel_v': _L1_xattn_in['kernel_v'], 'L1_xattn_bias_q': _L1_xattn_in['bias_q'], 'L1_xattn_bias_k': _L1_xattn_in['bias_k'], 'L1_xattn_bias_v': _L1_xattn_in['bias_v'], 'L1_ffn_ln1_g': _L1_ffn_in['ln1_g'], 'L1_ffn_ln1_b': _L1_ffn_in['ln1_b'], 'L1_ffn_Wqkv': _L1_ffn_in['Wqkv'], 'L1_ffn_Wproj': _L1_ffn_in['Wproj'], 'L1_ffn_ln2_g': _L1_ffn_in['ln2_g'], 'L1_ffn_ln2_b': _L1_ffn_in['ln2_b'], 'L1_ffn_Wgate': _L1_ffn_in['Wgate'], 'L1_ffn_W1': _L1_ffn_in['W1'], 'L1_ffn_b1': _L1_ffn_in['b1'], 'L1_ffn_W2': _L1_ffn_in['W2'], 'L1_ffn_b2': _L1_ffn_in['b2'], 'L2_xattn_Wq': _L2_xattn_in['Wq'], 'L2_xattn_Wk': _L2_xattn_in['Wk'], 'L2_xattn_Wv': _L2_xattn_in['Wv'], 'L2_xattn_Wo': _L2_xattn_in['Wo'], 'L2_ffn_w_gate': _L2_ffn_in['w_gate'], 'L2_ffn_b_gate': _L2_ffn_in['b_gate'], 'L2_ffn_W1': _L2_ffn_in['W1'], 'L2_ffn_b1': _L2_ffn_in['b1'], 'L2_ffn_W2': _L2_ffn_in['W2'], 'L2_ffn_b2': _L2_ffn_in['b2'], 'L3_xattn_W_Query': _L3_xattn_in['W_Query'], 'L3_xattn_W_Key': _L3_xattn_in['W_Key'], 'L3_xattn_W_Value': _L3_xattn_in['W_Value'], 'L3_xattn_W_Output': _L3_xattn_in['W_Output'], 'L3_xattn_B_Query': _L3_xattn_in['B_Query'], 'L3_xattn_B_Key': _L3_xattn_in['B_Key'], 'L3_xattn_B_Value': _L3_xattn_in['B_Value'], 'L3_xattn_B_Output': _L3_xattn_in['B_Output'], 'L3_ffn_router_w': _L3_ffn_in['router_w'], 'L3_ffn_router_bias': _L3_ffn_in['router_bias'], 'L3_ffn_up_proj': _L3_ffn_in['up_proj'], 'L3_ffn_gate_proj': _L3_ffn_in['gate_proj'], 'L3_ffn_down_proj': _L3_ffn_in['down_proj'], 'L3_ffn_sh_gate': _L3_ffn_in['sh_gate'], 'L3_ffn_sh_up': _L3_ffn_in['sh_up'], 'L3_ffn_sh_down': _L3_ffn_in['sh_down']}

def reference(x, ctx_1024, mask_BxS_ik0, mask_1xSxS2_ff0, L0_xattn_wq, L0_xattn_wk, L0_xattn_wv, L0_xattn_wo, L0_xattn_bq, L0_xattn_bk, L0_xattn_bv, L0_xattn_bo, L0_ffn_Wg, L0_ffn_W1, L0_ffn_b1, L0_ffn_W2, L0_ffn_b2, L1_xattn_kernel_q, L1_xattn_kernel_k, L1_xattn_kernel_v, L1_xattn_bias_q, L1_xattn_bias_k, L1_xattn_bias_v, L1_ffn_ln1_g, L1_ffn_ln1_b, L1_ffn_Wqkv, L1_ffn_Wproj, L1_ffn_ln2_g, L1_ffn_ln2_b, L1_ffn_Wgate, L1_ffn_W1, L1_ffn_b1, L1_ffn_W2, L1_ffn_b2, L2_xattn_Wq, L2_xattn_Wk, L2_xattn_Wv, L2_xattn_Wo, L2_ffn_w_gate, L2_ffn_b_gate, L2_ffn_W1, L2_ffn_b1, L2_ffn_W2, L2_ffn_b2, L3_xattn_W_Query, L3_xattn_W_Key, L3_xattn_W_Value, L3_xattn_W_Output, L3_xattn_B_Query, L3_xattn_B_Key, L3_xattn_B_Value, L3_xattn_B_Output, L3_ffn_router_w, L3_ffn_router_bias, L3_ffn_up_proj, L3_ffn_gate_proj, L3_ffn_down_proj, L3_ffn_sh_gate, L3_ffn_sh_up, L3_ffn_sh_down):
    import jax
    import jax.numpy as jnp

    def _L0_xattn_ref(queries, patch_representations, patch_boundaries, wq, wk, wv, wo, bq, bk, bv, bo):
        import jax, jax.numpy as jnp
        import numpy as np
        B, S, P, D, H = (2, 1024, 256, 256, 16)
        b, s, d = queries.shape
        p = patch_representations.shape[1]
        h = H
        dh = d // h
        scale = 1.0 / jnp.sqrt(jnp.asarray(dh, queries.dtype))
        q = (queries @ wq.T + bq).reshape(b, s, h, dh)
        k = (patch_representations @ wk.T + bk).reshape(b, p, h, dh)
        v = (patch_representations @ wv.T + bv).reshape(b, p, h, dh)
        scores = jnp.einsum('bqhd,bkhd->bhqk', q, k) * scale
        patch_idx = jnp.cumsum(patch_boundaries, axis=1)
        mask = jnp.arange(p)[None, None, :] > patch_idx[:, :, None]
        scores = jnp.where(mask[:, None, :, :], jnp.finfo(scores.dtype).min, scores)
        attn = jax.nn.softmax(scores, axis=-1)
        out = jnp.einsum('bhqk,bkhd->bqhd', attn, v).reshape(b, s, d)
        return out @ wo.T + bo

    def _L0_ffn_ref(x, Wg, W1, b1, W2, b2):
        import jax, jax.numpy as jnp
        import numpy as np
        D_MODEL, D_FF, N_EXPERTS, TOP_K = (256, 1024, 8, 2)
        B = x.shape[:-1]
        xs = x.reshape(-1, x.shape[-1])
        T = xs.shape[0]
        gate_logits = xs @ Wg
        weights, sel = jax.lax.top_k(gate_logits, TOP_K)
        weights = jax.nn.softmax(weights.astype(jnp.float32), axis=1).astype(x.dtype)
        h = jax.nn.relu(jnp.einsum('td,edf->etf', xs, W1) + b1[:, None, :])
        out_e = jnp.einsum('etf,efd->etd', h, W2) + b2[:, None, :]
        tok = jnp.arange(T)
        picked = out_e[sel, tok[:, None]]
        out = jnp.einsum('tk,tkd->td', weights, picked)
        return out.reshape(*B, x.shape[-1])

    def _L1_xattn_ref(q, k, v, mask, kernel_q, kernel_k, kernel_v, bias_q, bias_k, bias_v):
        import jax, jax.numpy as jnp
        import numpy as np
        B, S, D_IN, D_MODEL = (4, 512, 256, 256)
        Wq, Wk, Wv = (kernel_q[0, 0], kernel_k[0, 0], kernel_v[0, 0])
        qp = jax.nn.relu(jnp.einsum('bsd,de->bse', q, Wq) + bias_q)
        kp = jax.nn.relu(jnp.einsum('bsd,de->bse', k, Wk) + bias_k)
        vp = jax.nn.relu(jnp.einsum('bsd,de->bse', v, Wv) + bias_v)
        scores = jax.nn.relu(jnp.einsum('bqe,bke->bqk', qp, kp))
        dk = jnp.asarray(kp.shape[-1], dtype=scores.dtype)
        logits = scores / jnp.sqrt(dk) + mask
        out = jax.nn.relu(jnp.einsum('bqk,bke->bqe', logits, vp))
        return out

    def _L1_ffn_ref(x, ln1_g, ln1_b, Wqkv, Wproj, ln2_g, ln2_b, Wgate, W1, b1, W2, b2):
        import jax, jax.numpy as jnp
        import numpy as np
        import math
        B, T, D, H, E, TOPK, CAPF = (4, 512, 256, 16, 8, 2, 2.0)
        HD = D // H

        def layernorm(x, g, b, eps=1e-05):
            m = jnp.mean(x, -1, keepdims=True)
            v = jnp.mean(jnp.square(x - m), -1, keepdims=True)
            return (x - m) * jax.lax.rsqrt(v + eps) * g + b

        def block_forward(x, ln1_g, ln1_b, Wqkv, Wproj, ln2_g, ln2_b, Wgate, W1, b1, W2, b2):
            Bb, Tt, d = x.shape
            hd = HD
            half = hd // 2
            h = layernorm(x, ln1_g, ln1_b)
            qkv = (h @ Wqkv).reshape(Bb, Tt, H, 3 * hd)
            q, k, v = (qkv[..., :hd], qkv[..., hd:2 * hd], qkv[..., 2 * hd:])
            inv_freq = 1.0 / 10000.0 ** (jnp.arange(0, hd, 2, dtype=jnp.float32) / hd)
            ang = jnp.arange(Tt, dtype=jnp.float32)[:, None] * inv_freq
            sin = jnp.sin(ang)[None, :, None, :].astype(x.dtype)
            cos = jnp.cos(ang)[None, :, None, :].astype(x.dtype)

            def rope(t):
                t1, t2 = (t[..., :half], t[..., half:])
                return jnp.concatenate([t1 * cos - t2 * sin, t1 * sin + t2 * cos], -1)
            q, k = (rope(q), rope(k))
            scores = jnp.einsum('bqhd,bkhd->bhqk', q, k) / math.sqrt(hd)
            causal = jnp.tril(jnp.ones((Tt, Tt), dtype=bool))
            scores = jnp.where(causal, scores, jnp.asarray(-1000000000.0, scores.dtype))
            probs = jax.nn.softmax(scores, axis=-1)
            attn = jnp.einsum('bhqk,bkhd->bqhd', probs, v).reshape(Bb, Tt, d) @ Wproj
            x = x + attn
            h2 = layernorm(x, ln2_g, ln2_b)
            flat = h2.reshape(-1, d)
            N = flat.shape[0]
            capacity = int(math.ceil(CAPF * N / E))
            gates = jax.nn.softmax((flat @ Wgate).astype(jnp.float32), -1).astype(flat.dtype)
            _, top_inds = jax.lax.top_k(gates, TOPK)
            mask = jnp.zeros((N, E), dtype=bool).at[jnp.arange(N)[:, None], top_inds].set(True)
            pos = jnp.cumsum(mask.astype(jnp.int32), axis=0) * mask - 1
            keep = (pos < capacity) & mask
            t_flat = jnp.repeat(jnp.arange(N), TOPK)
            e_flat = top_inds.reshape(-1)
            p = pos[t_flat, e_flat]
            kp = keep[t_flat, e_flat]
            p_eff = jnp.where(kp, p, capacity)
            exp_in = jnp.zeros((E, capacity, d), flat.dtype).at[e_flat, p_eff].set(flat[t_flat], mode='drop')
            hmid = jax.nn.gelu(jnp.einsum('ecd,edf->ecf', exp_in, W1) + b1[:, None, :], approximate=False)
            exp_out = jnp.einsum('ecf,efd->ecd', hmid, W2) + b2[:, None, :]
            gate = gates[t_flat, e_flat] * kp.astype(flat.dtype)
            p_g = jnp.minimum(p_eff, capacity - 1)
            moe = jnp.zeros((N, d), flat.dtype).at[t_flat].add(exp_out[e_flat, p_g] * gate[:, None])
            return x + moe.reshape(Bb, Tt, d)
        return block_forward(x, ln1_g, ln1_b, Wqkv, Wproj, ln2_g, ln2_b, Wgate, W1, b1, W2, b2)

    def _L2_xattn_ref(q, k, v, Wq, Wk, Wv, Wo):
        import jax, jax.numpy as jnp
        import numpy as np
        D_MODEL = 256
        N_HEAD = 16
        D_K = 64
        D_V = 64
        B, S = (4, 512)
        B_, Sq, _ = q.shape
        Sk = k.shape[1]
        qh = (q @ Wq).reshape(B_, Sq, N_HEAD, D_K).transpose(0, 2, 1, 3)
        kh = (k @ Wk).reshape(B_, Sk, N_HEAD, D_K).transpose(0, 2, 1, 3)
        vh = (v @ Wv).reshape(B_, Sk, N_HEAD, D_V).transpose(0, 2, 1, 3)
        scores = jnp.einsum('bhqd,bhkd->bhqk', qh, kh) / jnp.sqrt(jnp.float32(D_K))
        attn = jax.nn.softmax(scores, axis=-1)
        ctx = jnp.einsum('bhqk,bhkd->bhqd', attn, vh)
        ctx = ctx.transpose(0, 2, 1, 3).reshape(B_, Sq, N_HEAD * D_V)
        return ctx @ Wo

    def _L2_ffn_ref(x, w_gate, b_gate, W1, b1, W2, b2):
        import jax, jax.numpy as jnp
        import numpy as np
        D_MODEL = 256
        MLP_DIM = 1024
        N_EXPERTS = 8
        B, T = (4, 256)
        b, t, d = x.shape
        x_flat = x.reshape(b * t, d)
        logits = x_flat @ w_gate + b_gate
        probs = jax.nn.softmax(logits, axis=-1)
        route_p = jnp.max(probs, axis=-1)
        route_idx = jnp.argmax(probs, axis=-1)
        h = jnp.einsum('nd,edm->enm', x_flat, W1) + b1[:, None, :]
        h = jax.nn.relu(h)
        y = jnp.einsum('enm,emd->end', h, W2) + b2[:, None, :]
        n = b * t
        out = y[route_idx, jnp.arange(n)] * route_p[:, None]
        return out.reshape(b, t, d)

    def _L3_xattn_ref(query, key, value, W_Query, W_Key, W_Value, W_Output, B_Query, B_Key, B_Value, B_Output):
        import jax, jax.numpy as jnp
        import numpy as np
        HEAD_NUM = 16
        KEY_DIM = 64
        EMBED = 256
        KV_OUT = HEAD_NUM * KEY_DIM
        B, Lq, E = query.shape
        Lk = key.shape[1]
        H, D = (HEAD_NUM, KEY_DIM)
        q = query @ W_Query + B_Query
        k = key @ W_Key + B_Key
        v = value @ W_Value + B_Value
        q = q.reshape(B, Lq, H, D)
        k = k.reshape(B, Lk, H, D)
        v = v.reshape(B, Lk, H, D)
        scores = jnp.einsum('bqhd,bkhd->bhqk', q, k) / D ** 0.5
        probs = jax.nn.softmax(scores, axis=-1)
        out = jnp.einsum('bhqk,bkhd->bqhd', probs, v)
        out = out.reshape(B, Lq, H * D)
        return out @ W_Output + B_Output

    def _L3_ffn_ref(x, router_w, router_bias, up_proj, gate_proj, down_proj, sh_gate, sh_up, sh_down):
        import jax, jax.numpy as jnp
        import numpy as np
        DIM = 256
        EXPERT_DIM = 128
        N_EXPERTS = 16
        TOPK = 2
        SHARED_HIDDEN = EXPERT_DIM * TOPK
        B, T = (4, 256)

        def _moe_forward(x, router_w, router_bias, up_proj, gate_proj, down_proj, sh_gate, sh_up, sh_down):
            Bb, Tt, D = x.shape
            flat = x.reshape(Bb * Tt, D)
            N = flat.shape[0]
            logits = flat @ router_w.T
            topk_scores, topk_idx = jax.lax.top_k(logits + router_bias, TOPK)
            topk_scores = jax.nn.softmax(topk_scores, axis=-1)
            combine = jnp.zeros((N, N_EXPERTS), flat.dtype)
            combine = combine.at[jnp.arange(N)[:, None], topk_idx].add(topk_scores)
            up_all = jnp.einsum('nd,kde->nke', flat, up_proj)
            gate_all = jnp.einsum('nd,kde->nke', flat, gate_proj)
            hidden = jax.nn.silu(gate_all) * up_all
            down_all = jnp.einsum('nke,ked->nkd', hidden, down_proj)
            out = jnp.einsum('nk,nkd->nd', combine, down_all)
            sh_hidden = jax.nn.silu(flat @ sh_gate.T) * (flat @ sh_up.T)
            out = out + sh_hidden @ sh_down.T
            return out.reshape(Bb, Tt, D)
        return _moe_forward(x, router_w, router_bias, up_proj, gate_proj, down_proj, sh_gate, sh_up, sh_down)
    x = x + _L0_xattn_ref(_layernorm(x, axis=-1), ctx_1024, mask_BxS_ik0, L0_xattn_wq, L0_xattn_wk, L0_xattn_wv, L0_xattn_wo, L0_xattn_bq, L0_xattn_bk, L0_xattn_bv, L0_xattn_bo)
    x = x + _L0_ffn_ref(_layernorm(x, axis=-1), L0_ffn_Wg, L0_ffn_W1, L0_ffn_b1, L0_ffn_W2, L0_ffn_b2)
    x = x + _L1_xattn_ref(_layernorm(x, axis=-1), ctx_1024, ctx_1024, mask_1xSxS2_ff0, L1_xattn_kernel_q, L1_xattn_kernel_k, L1_xattn_kernel_v, L1_xattn_bias_q, L1_xattn_bias_k, L1_xattn_bias_v)
    x = x + _L1_ffn_ref(_layernorm(x, axis=-1), L1_ffn_ln1_g, L1_ffn_ln1_b, L1_ffn_Wqkv, L1_ffn_Wproj, L1_ffn_ln2_g, L1_ffn_ln2_b, L1_ffn_Wgate, L1_ffn_W1, L1_ffn_b1, L1_ffn_W2, L1_ffn_b2)
    x = x + _L2_xattn_ref(_layernorm(x, axis=-1), ctx_1024, ctx_1024, L2_xattn_Wq, L2_xattn_Wk, L2_xattn_Wv, L2_xattn_Wo)
    x = x + _L2_ffn_ref(_layernorm(x, axis=-1), L2_ffn_w_gate, L2_ffn_b_gate, L2_ffn_W1, L2_ffn_b1, L2_ffn_W2, L2_ffn_b2)
    x = x + _L3_xattn_ref(_layernorm(x, axis=-1), ctx_1024, ctx_1024, L3_xattn_W_Query, L3_xattn_W_Key, L3_xattn_W_Value, L3_xattn_W_Output, L3_xattn_B_Query, L3_xattn_B_Key, L3_xattn_B_Value, L3_xattn_B_Output)
    x = x + _L3_ffn_ref(_layernorm(x, axis=-1), L3_ffn_router_w, L3_ffn_router_bias, L3_ffn_up_proj, L3_ffn_gate_proj, L3_ffn_down_proj, L3_ffn_sh_gate, L3_ffn_sh_up, L3_ffn_sh_down)
    return x

_drawn_inputs = setup_inputs


def setup_inputs(seed=0):
    import zlib

    import numpy as np

    out = dict(_drawn_inputs(seed))
    spreads = {'L0_xattn_bq': (0.0, 2.0),
     'L0_xattn_bk': (0.0, 2.0),
     'L0_xattn_bv': (0.0, 0.8),
     'L0_xattn_bo': (0.0, 0.662),
     'L0_ffn_b1': (0.0, 0.8),
     'L0_ffn_b2': (0.0, 2.0),
     'L1_ffn_ln1_g': (1.0, 0.6),
     'L1_ffn_ln1_b': (0.0, 0.8),
     'L1_ffn_ln2_g': (1.0, 0.6),
     'L1_ffn_ln2_b': (0.0, 0.8),
     'L1_ffn_b1': (0.0, 2.0),
     'L1_ffn_b2': (0.0, 2.0),
     'L2_ffn_b1': (0.0, 2.0),
     'L2_ffn_b2': (0.0, 2.0),
     'L3_xattn_B_Query': (0.0, 2.0),
     'L3_xattn_B_Key': (0.0, 2.0),
     'L3_xattn_B_Value': (0.0, 2.0),
     'L3_xattn_B_Output': (0.0, 2.0),
     'L3_ffn_router_bias': (0.0, 2.0)}
    factors = {'L0_xattn_wq': 8.0,
     'L0_xattn_wk': 8.0,
     'L0_xattn_wv': 3.675,
     'L0_xattn_wo': 3.658,
     'L0_ffn_Wg': 4.014,
     'L0_ffn_W1': 4.917,
     'L0_ffn_W2': 4.05,
     'L1_xattn_bias_q': 8.0,
     'L1_xattn_bias_k': 8.0,
     'L1_ffn_Wqkv': 8.0,
     'L1_ffn_Wproj': 8.0,
     'L1_ffn_Wgate': 8.0,
     'L1_ffn_W1': 8.0,
     'L1_ffn_W2': 8.0,
     'L2_xattn_Wq': 8.0,
     'L2_xattn_Wk': 8.0,
     'L2_xattn_Wv': 8.0,
     'L2_xattn_Wo': 8.0,
     'L2_ffn_w_gate': 21.698,
     'L2_ffn_b_gate': 64.0,
     'L2_ffn_W1': 22.866,
     'L2_ffn_W2': 8.0,
     'L3_xattn_W_Query': 8.0,
     'L3_xattn_W_Key': 8.0,
     'L3_xattn_W_Value': 8.0,
     'L3_xattn_W_Output': 8.0,
     'L3_ffn_router_w': 45.352,
     'L3_ffn_up_proj': 38.541,
     'L3_ffn_gate_proj': 46.38,
     'L3_ffn_down_proj': 39.256,
     'L3_ffn_sh_gate': 21.912,
     'L3_ffn_sh_up': 8.0,
     'L3_ffn_sh_down': 8.0}
    for name, (base, spread) in spreads.items():
        noise = np.random.default_rng([zlib.crc32(name.encode()), seed]).standard_normal(out[name].shape)
        drawn = base * np.exp(spread * noise) if base else spread * noise
        out[name] = jnp.asarray(drawn.astype(out[name].dtype))
    for name, factor in factors.items():
        out[name] = (out[name] * factor).astype(out[name].dtype)
    return out
```

```python
from contextlib import ExitStack

import concourse.bass as bass
from concourse import mybir

F32 = mybir.dt.float32
I32 = mybir.dt.int32
U32 = mybir.dt.uint32
ALU = mybir.AluOpType
ACT = mybir.ActivationFunctionType
AX = mybir.AxisListType.X

B, T, D = 16, 112, 256
S, SJ, J = 375, 125, 3
P = 128
DC = D // P
H = 16
HALF = 512
CREDIT = 64
NEG = -1e30
LAYERS = 99


class Counter:

    def __init__(self, sem, start):
        self.sem, self.start = sem, start

    def at(self, n):
        return n + self.start

    def stage_over(self, n):
        self.start += n


class Batch:

    def __init__(self, i, k):
        self.n = 2 * i + k
        self.half = i + k // 2
        self.par = k % 2
        self.i, self.k = i, k

    def __add__(self, d):
        return Batch(self.i, self.k + d)


def before(b, h, d):
    return (b, h - d) if h >= d else (b + -1, h - d + H)


class Core:

    def __init__(self, nc, ctx):
        self.nc, self.ctx, self.counters = nc, ctx, {}
        self.bank = [ctx.enter_context(nc.psum_tensor(f"bank{i}", [P, HALF], F32)) for i in range(8)]

    def keep(self, name, shape, dt=F32):
        return self.ctx.enter_context(self.nc.sbuf_tensor(name, shape, dt))

    def counter(self, name):
        if name not in self.counters:
            start = 0 if name in BY_POOL_DMA else CREDIT
            self.counters[name] = Counter(self.ctx.enter_context(self.nc.semaphore(name)), start)
        return self.counters[name]


def load_start(nc, core, x_in, ident_in):
    loaded = core.counter("start_loaded")
    with nc.Block() as block:

        @block.gpsimd
        def _(pool):
            for s in core.counters.values():
                if s.start:
                    pool.sem_inc(s.sem, s.start)
            pool.memset(core.neg_half[:, :], -0.5)
            pool.memset(core.ones[:, :], 1.0)
            pool.memset(core.h_all[:, :, :], 0.0).then_inc(core.filled_sem, 1)

        @block.sync
        def _(sp):
            sp.dma_start(core.ident[:, :], ident_in).then_inc(core.start_sem, 16)
            sp.dma_start(core.x[:, :, :], x_in.rearrange("b t d -> t b d")).then_inc(core.start_sem, 16)
            sp.wait_ge(core.filled_sem, 1)
            for r in range(core.slots_in.shape[0] // (B * T)):
                sp.dma_start(core.slots_in[r * B * T:(r + 1) * B * T, :].rearrange("(t b) d -> t b d", b=B),
                             core.h_all[:, :, :]).then_inc(core.zeroed_sem, 16)
            sp.wait_ge(core.start_sem, 32)


def store_end(nc, core, out):
    stored = core.counter("stored")
    with nc.Block() as block:

        @block.sync
        def _(sp):
            sp.dma_start(out.rearrange("b t d -> t b d"), core.x[:, :, :]).then_inc(stored.sem, 16)
            sp.wait_ge(stored.sem, stored.at(16))


def cross_attention(nc, core, name, ctx_in, w, dh, mask=None):
    E = H * dh
    EC = E // P
    NQ = -(-EC // 4)
    VW = min(E, HALF)
    NV = J * E // VW
    NOT = -(-EC // 4)
    NY = 2 if EC > 2 else 1
    YW = D // NY
    G = min(H, HALF // dh)
    NG = H // G
    scale = float(dh) ** -0.5
    biased = "bk" in w
    if EC > 2:
        order = {0: ["K0"], 1: ["K1"], 2: ["K2"], 3: ["K3"], 4: ["K4"], 5: ["K5", "O0", "O1"],
                 7: ["Y0", "Y1", "L0", "L1"], 8: ["K6"], 9: ["K7"], 10: ["Q0"], 11: ["Q1", "V0"],
                 12: ["V1"], 13: ["V2"], 14: ["V3"], 15: ["V4", "V5"]}
    else:
        order = {0: ["K0"], 2: ["K1"], 5: ["O0"], 7: ["Y0", "L0", "L1"], 9: ["Q0"], 10: ["V0"],
                 12: ["V1"], 14: ["V2"]}
    first_pieces = ["L0", "L1", "Q0", "Q1", "K0", "K1", "K2", "K3", "K4", "K5", "K6", "K7",
                    "V0", "V1", "V2", "V3", "V4", "V5"]
    every = [p for ps in order.values() for p in ps]
    first_pieces = [p for p in first_pieces if p in every]
    per_batch = {"L": 2, "Q": NQ, "K": EC, "V": NV, "O": NOT, "Y": NY}

    ctx = ExitStack()
    with ctx:
        def sb(n, shape, dt=F32):
            return ctx.enter_context(nc.sbuf_tensor(f"{name}_{n}", shape, dt))

        wq, wk, wv = (sb(n, [P, DC, E]) for n in ("wq", "wk", "wv"))
        wo = sb("wo", [P, EC, D])
        ctxT = [sb(f"ctxT{i}", [P, DC, S]) for i in range(2)]
        stats = sb("stats", [T, 16])
        normed = sb("normed", [T, D])
        hT = sb("hT", [P, DC, T])
        q = [sb(f"q{i}", [P, EC, T] if EC > 2 else [P, H, T]) for i in range(2)]
        kT = [sb(f"kT{i}", [P, EC, S]) for i in range(2)]
        v = [sb(f"v{i}", [SJ, J, E]) for i in range(2)]
        probs = [sb(f"probs{i}", [T, S]) for i in range(2)]
        probsT = [sb(f"probsT{i}", [SJ, J, T]) for i in range(2)]
        negmax = [sb(f"negmax{i}", [T, H]) for i in range(2)]
        sums = [sb(f"sums{i}", [T, H]) for i in range(2)]
        inverse = sb("inverse", [T, H])
        o = sb("o", [T, E])
        oT = sb("oT", [P, EC, T])
        if biased:
            bq, bk, bv = (sb(n, [P, EC]) for n in ("bq", "bk", "bv"))
            bo = sb("bo", [1, D])
        if mask:
            steps = sb("steps", [T, B], I32)
            stepsf = sb("stepsf", [T, B])
            upto = sb("upto", [T, T])
            last_key = sb("last_key", [T, B])
            keys = sb("keys", [T, S])
            headmask = sb("headmask", [P, P // dh])
            barred = [sb(f"barred{i}", [T, S]) for i in range(2)]
            masked = [sb(f"masked{i}", [T, S]) for i in range(2)]
        weights = core.counter("weights")
        ctx_here = [core.counter(f"ctx_here{i}") for i in range(2)]
        var_ready = core.counter("var_ready")
        rstd_ready = core.counter("rstd_ready")
        normed_ready = core.counter("normed_ready")
        scored = core.counter("scored")
        maxed = core.counter("maxed")
        exped = core.counter("exped")
        turned = core.counter("turned")
        probsT_ready = core.counter("probsT_ready")
        pv_done = core.counter("pv_done")
        o_ready = core.counter("o_ready")
        setup_done = core.counter("setup_done")
        cums = core.counter("cums")
        made = {c: core.counter(f"made_{c}") for c in "LQKVOY"}
        taken = {c: core.counter(f"taken_{c}") for c in "LQKVOY"}
        nweights = 4 + (4 if biased else 0) + (4 if mask else 0)
        psS, psT, psO, ring = core.bank[0:2], core.bank[2:4], core.bank[4:6], core.bank[6:8]

        def count(piece, b):
            n = per_batch[piece[0]]
            return b.n * n + (int(piece[1]) + 1)

        def pieces_at(h, b_first, b_last):
            for p in order.get(h, []):
                if p[0] in "OY":
                    if not b_first:
                        yield p, -1
                elif not b_last:
                    yield p, 1

        def slots(b_first):
            before_ = [("V%d" % (NV - 2), 0), ("V%d" % (NV - 1), 0)]
            if NV == 1:
                raise ValueError
            out, n = {}, 0
            for h in range(H):
                for p, d in pieces_at(h, b_first, False):
                    out[p] = (n % 2, before_[n % 2])
                    before_[n % 2] = (p, d)
                    n += 1
            assert n % 2 == 0
            return out

        def first_slots():
            out, before_ = {}, [None, None]
            for n, p in enumerate(first_pieces):
                out[p] = (n % 2, before_[n % 2])
                before_[n % 2] = (p, 0)
            assert len(first_pieces) % 2 == 0
            return out

        def last_slots():
            tail = [p for p in every if p[0] in "OY"]
            lasts = [p for p in every if p[0] in "OY"]
            before_ = [(lasts[-2], -1), (lasts[-1], -1)]
            out = {}
            for n, p in enumerate(tail):
                out[p] = (n % 2, before_[n % 2])
                before_[n % 2] = (p, 0)
            return out

        def run(heads, first, last, tail, engine):
            first(Batch(0, 0))
            heads(Batch(0, 0), True, False)
            with engine.Fori(0, (B - 2) // 2) as i:
                heads(Batch(i, 1), False, False)
                heads(Batch(i, 2), False, False)
            heads(Batch(0, B - 1), False, True)
            tail(Batch(0, B - 1))

        with nc.Block() as block:

            @block.sync
            def _(sp):
                for dst, src in ((wq, w["wq"]), (wk, w["wk"]), (wv, w["wv"]), (wo, w["wo"])):
                    sp.dma_start(dst[:, :, :], src).then_inc(weights.sem, 16)
                if biased:
                    for dst, src in ((bq, w["bq"]), (bk, w["bk"]), (bv, w["bv"]), (bo, w["bo"])):
                        sp.dma_start(dst[:, :], src).then_inc(weights.sem, 16)
                if mask:
                    sp.dma_start(steps[:, :], mask["steps"]).then_inc(weights.sem, 16)
                    sp.dma_start(upto[:, :], mask["upto"]).then_inc(weights.sem, 16)
                    sp.dma_start(keys[:, :], mask["keys"].partition_broadcast(T)).then_inc(weights.sem, 16)
                    sp.dma_start(headmask[:, :], mask["headmask"]).then_inc(weights.sem, 16)

                def load(b):
                    sp.dma_start(ctxT[b.par][:, :, :], ctx_in[bass.ds(b.n, 1)].rearrange("a p c s -> p (a c) s"))\
                        .then_inc(ctx_here[b.par].sem, 16)

                load(Batch(0, 0))
                load(Batch(0, 1))
                with sp.Fori(0, (B - 2) // 2) as i:
                    for k in (2, 3):
                        b = Batch(i, k)
                        sp.wait_ge(made["V"].sem, made["V"].at(count("V%d" % (NV - 1), b + -2)))
                        load(b)

            @block.tensor
            def _(pe):
                def piece(p, b, slot):
                    at, prior = slot
                    if prior:
                        kind = prior[0]
                        pe.wait_ge(taken[kind[0]].sem, taken[kind[0]].at(count(kind, prior[1])))
                    bank, m = ring[at], int(p[1])
                    if p[0] == "L":
                        pe.wait_ge(normed_ready.sem, normed_ready.at(b.n + 1))
                        ins = pe.transpose(bank[:, 0:T], normed[:, m * P:(m + 1) * P], core.ident[0:T, 0:T])
                    elif p[0] == "Q":
                        pe.wait_ge(taken["L"].sem, taken["L"].at(count("L1", b)))
                        cs = range(4 * m, min(4 * m + 4, EC))
                        for c in cs:
                            for k in range(DC):
                                ins = pe.matmul(bank[:, (c - 4 * m) * T:(c - 4 * m + 1) * T],
                                                wq[:, k, c * P:(c + 1) * P], hT[:, k, :],
                                                start=(k == 0), stop=(k == DC - 1))
                    elif p[0] == "K":
                        pe.wait_ge(ctx_here[b.par].sem, ctx_here[b.par].at(16 * b.half + 16))
                        for k in range(DC):
                            ins = pe.matmul(bank[:, 0:S], wk[:, k, m * P:(m + 1) * P], ctxT[b.par][:, k, :],
                                            start=(k == 0), stop=(k == DC - 1))
                    elif p[0] == "V":
                        pe.wait_ge(ctx_here[b.par].sem, ctx_here[b.par].at(16 * b.half + 16))
                        j, n = m // (E // VW), m % (E // VW)
                        for k in range(DC):
                            ins = pe.matmul(bank[0:SJ, 0:VW], ctxT[b.par][:, k, j * SJ:(j + 1) * SJ],
                                            wv[:, k, n * VW:(n + 1) * VW], start=(k == 0), stop=(k == DC - 1))
                    elif p[0] == "O":
                        pe.wait_ge(o_ready.sem, o_ready.at(NG * b.n + NG))
                        cs = range(4 * m, min(4 * m + 4, EC))
                        for c in cs:
                            ins = pe.transpose(bank[:, (c - 4 * m) * T:(c - 4 * m + 1) * T],
                                               o[:, c * P:(c + 1) * P], core.ident[0:T, 0:T])
                    else:
                        pe.wait_ge(taken["O"].sem, taken["O"].at(count("O%d" % (NOT - 1), b)))
                        for c in range(EC):
                            ins = pe.matmul(bank[0:T, 0:YW], oT[:, c, :], wo[:, c, m * YW:(m + 1) * YW],
                                            start=(c == 0), stop=(c == EC - 1 and not biased))
                        if biased:
                            ins = pe.matmul(bank[0:T, 0:YW], core.ones[0:1, 0:T], bo[0:1, m * YW:(m + 1) * YW],
                                            start=False, stop=True)
                    ins.then_inc(made[p[0]].sem, 1)

                def scores(b, h):
                    if h == 0:
                        pe.wait_ge(taken["Q"].sem, taken["Q"].at(NQ * b.n + NQ))
                        pe.wait_ge(taken["K"].sem, taken["K"].at(EC * b.n + EC))
                    if EC > 2:
                        at = h * dh % P
                        pe.matmul(psS[h % 2][0:T, 0:S], q[b.par][at:at + dh, h * dh // P, :],
                                  kT[b.par][at:at + dh, h * dh // P, :], start=True, stop=True)\
                            .then_inc(scored.sem, 1)
                    else:
                        pe.matmul(psS[h % 2][0:T, 0:S], q[b.par][:, h, :], kT[b.par][:, h * dh // P, :],
                                  start=True, stop=True).then_inc(scored.sem, 1)

                def turn(b, h):
                    pe.wait_ge(exped.sem, exped.at(H * b.n + h + 1))
                    for j in range(J):
                        ins = pe.transpose(psT[h % 2][0:SJ, j * T:(j + 1) * T],
                                           probs[h % 2][:, j * SJ:(j + 1) * SJ], core.ident[0:T, 0:T])
                    ins.then_inc(turned.sem, 1)

                def values(b, h):
                    pe.wait_ge(probsT_ready.sem, probsT_ready.at(H * b.n + h + 1))
                    if h == 0:
                        pe.wait_ge(taken["V"].sem, taken["V"].at(NV * b.n + NV))
                    if h % G == 0:
                        pe.wait_ge(o_ready.sem, o_ready.at(NG * b.n + h // G - 1))
                    bank = psO[(b.par * NG + h // G) % 2]
                    for j in range(J):
                        ins = pe.matmul(bank[0:T, h % G * dh:(h % G + 1) * dh], probsT[h % 2][:, j, :],
                                        v[b.par][:, j, h * dh:(h + 1) * dh], start=(j == 0), stop=(j == J - 1))
                    ins.then_inc(pv_done.sem, 1)

                def heads(b, b_first, b_last):
                    where = slots(b_first)
                    for h in range(H):
                        scores(b, h)
                        if not (b_first and h < 1):
                            turn(*before(b, h, 1))
                        if not (b_first and h < 2):
                            values(*before(b, h, 2))
                        for p, d in pieces_at(h, b_first, b_last):
                            at, (prior, pd) = where[p] if not b_last else last_where[p]
                            piece(p, b + d, (at, (prior, b + pd)))

                def first(b):
                    where = first_slots()
                    for p in first_pieces:
                        at, prior = where[p]
                        piece(p, b, (at, prior and (prior[0], b)))

                def tail(b):
                    turn(b, H - 1)
                    values(b, H - 2)
                    values(b, H - 1)
                    where = last_slots()
                    for p in [p for p in every if p[0] in "OY"]:
                        at, (prior, d) = where[p]
                        piece(p, b, (at, (prior, b + d)))

                last_where, prior_ = {}, [("V%d" % (NV - 2), 0), ("V%d" % (NV - 1), 0)]
                for n, p in enumerate([p for p in every if p[0] in "OY"]):
                    last_where[p] = (n % 2, prior_[n % 2])
                    prior_[n % 2] = (p, -1)

                pe.wait_ge(weights.sem, weights.at(16 * nweights))
                if mask:
                    pe.wait_ge(setup_done.sem, setup_done.at(1))
                    pe.matmul(psS[0][0:T, 0:B], upto[:, :], stepsf[:, :], start=True, stop=True)\
                        .then_inc(cums.sem, 1)
                    pe.wait_ge(setup_done.sem, setup_done.at(2))
                run(heads, first, lambda *_: None, tail, pe)

            @block.scalar
            def _(act):
                act.preload_act_table(ACT.Exp)
                act.wait_ge(weights.sem, weights.at(16 * nweights))

                def take(p, b, at):
                    bank, m = ring[at], int(p[1])
                    if p[0] in "YQ":
                        return
                    act.wait_ge(made[p[0]].sem, made[p[0]].at(count(p, b)))
                    if p[0] == "L":
                        ins = act.activation(hT[:, m, :], bank[:, 0:T], ACT.Copy)
                    elif p[0] == "K":
                        if biased:
                            ins = act.activation(kT[b.par][:, m, :], bank[:, 0:S], ACT.Identity, bias=bk[:, m:m + 1])
                        else:
                            ins = act.activation(kT[b.par][:, m, :], bank[:, 0:S], ACT.Copy)
                    elif p[0] == "V":
                        j, n = m // (E // VW), m % (E // VW)
                        ins = act.activation(v[b.par][:, j, n * VW:(n + 1) * VW], bank[0:SJ, 0:VW], ACT.Copy)
                    else:
                        cs = range(4 * m, min(4 * m + 4, EC))
                        if biased:
                            for c in cs:
                                ins = act.activation(oT[:, c, :], bank[:, (c - 4 * m) * T:(c - 4 * m + 1) * T],
                                                     ACT.Identity, bias=bv[:, c:c + 1])
                        else:
                            ins = act.activation(oT[:, cs[0]:cs[-1] + 1, :],
                                                 bank[:, 0:len(cs) * T].rearrange("p (c t) -> p c t", t=T), ACT.Copy)
                    ins.then_inc(taken[p[0]].sem, 1)

                def heads(b, b_first, b_last):
                    where = slots(b_first)
                    tails = [p for p in every if p[0] in "OY"]
                    for h in range(H):
                        act.wait_ge(maxed.sem, maxed.at(H * b.n + h + 1))
                        act.activation(probs[h % 2][:, :], masked[h % 2][:, :] if mask else psS[h % 2][0:T, 0:S],
                                       ACT.Exp, bias=negmax[b.par][:, h:h + 1],
                                       accum_out=sums[b.par][:, h:h + 1]).then_inc(exped.sem, 1)
                        for p, d in pieces_at(h, b_first, b_last):
                            take(p, b + d, where[p][0] if not b_last else tails.index(p) % 2)

                def first(b):
                    where = first_slots()
                    for p in first_pieces:
                        take(p, b, where[p][0])

                def tail(b):
                    where = last_slots()
                    for p in [p for p in every if p[0] in "OY"]:
                        take(p, b, where[p][0])

                run(heads, first, None, tail, act)

            @block.gpsimd
            def _(pool):
                def rstd(b):
                    pool.wait_ge(var_ready.sem, var_ready.at(b.n + 1))
                    pool.tensor_tensor(stats[:, 9:10], stats[:, 8:9], core.neg_half[0:T, :], ALU.pow)\
                        .then_inc(rstd_ready.sem, 1)

                rstd(Batch(0, 0))
                with pool.Fori(0, B - 1) as i:
                    pool.wait_ge(var_ready.sem, var_ready.at(i + 2))
                    pool.tensor_tensor(stats[:, 9:10], stats[:, 8:9], core.neg_half[0:T, :], ALU.pow)\
                        .then_inc(rstd_ready.sem, 1)

            @block.vector
            def _(dve):
                def x_of(b):
                    return core.x[:, bass.ds(b.n, 1), :].rearrange("t a d -> t (a d)")

                def normalise_start(b):
                    dve.bn_stats(stats[:, 0:6], x_of(b))
                    dve.drain()
                    dve.bn_aggr(stats[:, 6:8], stats[:, 0:6])
                    dve.drain()
                    dve.tensor_scalar(stats[:, 8:9], stats[:, 7:8], 1e-5, None, ALU.add).then_inc(var_ready.sem, 1)

                def normalise_end(b):
                    dve.wait_ge(rstd_ready.sem, rstd_ready.at(b.n + 1))
                    dve.tensor_scalar(normed[:, :], x_of(b), stats[:, 6:7], stats[:, 9:10], ALU.subtract, ALU.mult)\
                        .then_inc(normed_ready.sem, 1)

                def bar(b):
                    dve.tensor_scalar(barred[b.par][:, :], keys[:, :], last_key[:, bass.ds(b.n, 1)], NEG,
                                      ALU.is_gt, ALU.mult)
                    dve.drain()

                def take(p, b, at):
                    bank, m = ring[at], int(p[1])
                    if p[0] not in "YQ":
                        return
                    dve.wait_ge(made[p[0]].sem, made[p[0]].at(count(p, b)))
                    if p[0] == "Y":
                        xb = core.x[:, bass.ds(b.n, 1), m * YW:(m + 1) * YW].rearrange("t a d -> t (a d)")
                        ins = dve.tensor_tensor(xb, bank[0:T, 0:YW], xb, ALU.add)
                    elif EC > 2:
                        cs = range(4 * m, min(4 * m + 4, EC))
                        src = bank[:, 0:len(cs) * T].rearrange("p (c t) -> p c t", t=T)
                        dst = q[b.par][:, cs[0]:cs[-1] + 1, :]
                        if biased:
                            ins = dve.scalar_tensor_tensor(
                                out=dst, in0=src, scalar=scale,
                                in1=bq[:, cs[0]:cs[-1] + 1].unsqueeze(2).broadcast_to([P, len(cs), T]),
                                op0=ALU.mult, op1=ALU.add)
                        else:
                            ins = dve.tensor_scalar(dst, src, scale, None, ALU.mult)
                    else:
                        HC = P // dh
                        for c in range(EC):
                            ins = dve.scalar_tensor_tensor(
                                out=q[b.par][:, c * HC:(c + 1) * HC, :],
                                in0=bank[:, c * T:(c + 1) * T].unsqueeze(1).broadcast_to([P, HC, T]),
                                scalar=bq[:, c:c + 1], in1=headmask[:, :].unsqueeze(2).broadcast_to([P, HC, T]),
                                op0=ALU.add, op1=ALU.mult)
                    ins.then_inc(taken[p[0]].sem, 1)

                def head_max(b, h):
                    dve.wait_ge(scored.sem, scored.at(H * b.n + h + 1))
                    if mask:
                        dve.tensor_tensor(masked[h % 2][:, :], psS[h % 2][0:T, 0:S], barred[b.par][:, :], ALU.add)
                        dve.drain()
                        dve.tensor_reduce(negmax[b.par][:, h:h + 1], masked[h % 2][:, :], AX, ALU.max,
                                          negate=True).then_inc(maxed.sem, 1)
                    else:
                        dve.tensor_reduce(negmax[b.par][:, h:h + 1], psS[h % 2][0:T, 0:S], AX, ALU.max,
                                          negate=True).then_inc(maxed.sem, 1)

                def take_probsT(b, h):
                    dve.wait_ge(turned.sem, turned.at(H * b.n + h + 1))
                    dve.tensor_copy(probsT[h % 2][:, :, :],
                                    psT[h % 2][0:SJ, 0:J * T].rearrange("p (j t) -> p j t", t=T))\
                        .then_inc(probsT_ready.sem, 1)

                def divide(b, g):
                    dve.wait_ge(pv_done.sem, pv_done.at(H * b.n + (g + 1) * G))
                    dve.reciprocal(inverse[:, g * G:(g + 1) * G], sums[b.par][:, g * G:(g + 1) * G])
                    dve.drain()
                    bank = psO[(b.par * NG + g) % 2]
                    dve.tensor_tensor(o[:, g * G * dh:(g + 1) * G * dh].rearrange("t (h e) -> t h e", e=dh),
                                      bank[0:T, 0:G * dh].rearrange("t (h e) -> t h e", e=dh),
                                      inverse[:, g * G:(g + 1) * G].unsqueeze(2).broadcast_to([T, G, dh]),
                                      ALU.mult).then_inc(o_ready.sem, 1)

                def heads(b, b_first, b_last):
                    where = slots(b_first)
                    tails = [p for p in every if p[0] in "OY"]
                    for h in range(H):
                        if h == 0 and mask:
                            bar(b)
                        head_max(b, h)
                        if not (b_first and h < 1):
                            take_probsT(*before(b, h, 1))
                        if h == 1 and not b_last:
                            normalise_start(b + 1)
                        if h == 3 and not b_first:
                            divide(b + -1, NG - 1)
                        if h == 4 and not b_last:
                            normalise_end(b + 1)
                        if NG == 2 and h == 11:
                            divide(b, 0)
                        for p, d in pieces_at(h, b_first, b_last):
                            take(p, b + d, where[p][0] if not b_last else tails.index(p) % 2)

                def first(b):
                    normalise_start(b)
                    normalise_end(b)
                    where = first_slots()
                    for p in first_pieces:
                        take(p, b, where[p][0])

                def tail(b):
                    take_probsT(b, H - 1)
                    divide(b, NG - 1)
                    where = last_slots()
                    for p in [p for p in every if p[0] in "OY"]:
                        take(p, b, where[p][0])

                dve.wait_ge(weights.sem, weights.at(16 * nweights))
                if biased and EC > 2:
                    dve.tensor_scalar(bq[:, :], bq[:, :], scale, None, ALU.mult)
                if mask:
                    dve.tensor_copy(stepsf[:, :], steps[:, :]).then_inc(setup_done.sem, 1)
                    dve.wait_ge(cums.sem, cums.at(1))
                    dve.tensor_copy(last_key[:, :], psS[0][0:T, 0:B]).then_inc(setup_done.sem, 1)
                dve.drain()
                run(heads, first, None, tail, dve)

        weights.stage_over(16 * nweights)
        for s in ctx_here:
            s.stage_over(16 * B // 2)
        for s in (var_ready, rstd_ready, normed_ready):
            s.stage_over(B)
        for s in (scored, maxed, exped, turned, probsT_ready, pv_done):
            s.stage_over(B * H)
        o_ready.stage_over(B * NG)
        if mask:
            setup_done.stage_over(2)
            cums.stage_over(1)
        for c in "LQKVOY":
            made[c].stage_over(B * per_batch[c])
            taken[c].stage_over(B * per_batch[c])


def normalise_start(dve, stats, src, var_ready):
    dve.bn_stats(stats[:, 0:6], src)
    dve.drain()
    dve.bn_aggr(stats[:, 6:8], stats[:, 0:6])
    dve.drain()
    dve.tensor_scalar(stats[:, 8:9], stats[:, 7:8], 1e-5, None, ALU.add).then_inc(var_ready.sem, 1)


def batch_row(t, b):
    return t[:, bass.ds(b.n, 1), :].rearrange("t a d -> t (a d)")


def pair_loop(engine, body, n):
    with engine.Fori(0, n // 2) as i:
        body(Batch(i, 0))
        body(Batch(i, 1))


def route(nc, core, name, w, E, topk, how, tile):
    affine = "g" in w
    src = core.y if affine else core.x
    biased = "bg" in w
    BE = B * E
    NT = core.tiles[name] if tile else 0
    M = -(-B * T // tile) if tile else 0
    slots = core.slots_in

    ctx = ExitStack()
    with ctx:
        def sb(n, shape, dt=F32):
            return ctx.enter_context(nc.sbuf_tensor(f"{name}_route_{n}", shape, dt))

        wg = sb("wg", [P, DC, E])
        stats = sb("stats", [T, 16])
        normed = [sb(f"normed{i}", [T, D]) for i in range(2)]
        hT = [sb(f"hT{i}", [P, DC, T]) for i in range(2)]
        logits, logits2, eq1, eq2, both, scratch = (sb(n, [T, B, E]) for n in
                                                    ("logits", "logits2", "eq1", "eq2", "both", "scratch"))
        at_expert = sb("at_expert", [T, E])
        m1, m2, i1, i2, total, kept, place = (sb(n, [T, B]) for n in ("m1", "m2", "i1", "i2", "total", "kept", "place"))
        if affine:
            gain, shift = sb("gain", [T, D]), sb("shift", [T, D])
        if biased:
            bg = sb("bg", [T, E])
        if tile:
            upto = sb("upto", [T, T])
            sums_eb, scan, keepgoing = (sb(n, [T, E, B]) for n in ("sums_eb", "scan", "keepgoing"))
            base = sb("base", [T, E, B])
            steps = sb("steps", [T, E, M])
            over = sb("over", [T, E, M])
            ntiles, ends, starts = (sb(n, [T, E]) for n in ("ntiles", "ends", "starts"))
            tiles = sb("tiles", [1, NT, E])
            tiles_cmp = sb("tiles_cmp", [1, NT, E])
            eidf = sb("eidf", [1, NT])
            spare = sb("spare", [T, topk, B])
        weights = core.counter("weights")
        var_ready = core.counter("var_ready")
        rstd_ready = core.counter("rstd_ready")
        normed_ready = core.counter("normed_ready")
        made_L, taken_L = core.counter("made_L"), core.counter("taken_L")
        made_G, taken_G = core.counter("made_G"), core.counter("taken_G")
        kept_copy = core.counter("kept_copy")
        to_exp, exped = core.counter("maxed"), core.counter("exped")
        to_count, counted = core.counter("setup_done"), core.counter("cums")
        slots_ready = core.counter("o_ready")
        scattered = core.counter("scattered")
        loads = [(wg, w["wg"])]
        if affine:
            loads += [(gain, w["g"].partition_broadcast(T)), (shift, w["b"].partition_broadcast(T))]
        if biased:
            loads += [(bg, w["bg"].partition_broadcast(T))]
        loads += [(at_expert, core.consts["at_expert%d" % E].partition_broadcast(T))]
        if tile:
            loads += [(upto, core.consts["upto"]), (keepgoing, core.consts["keepgoing"].partition_broadcast(T)),
                      (spare, core.consts["spare"][:, 0:topk, :])]
            if how == "cap":
                loads += [(starts, core.consts["cap_starts"].partition_broadcast(T))]
            else:
                loads += [(steps, core.consts[f"steps_{name}"].partition_broadcast(T)),
                          (tiles, core.consts[f"tiles_{name}"].unsqueeze(0))]
        psL, psG = core.bank[0:2], core.bank[2:4]
        pos, tot = core.bank[4], core.bank[5]

        with nc.Block() as block:

            @block.sync
            def _(sp):
                for dst, s in loads:
                    sp.dma_start(dst[tuple([slice(None)] * len(dst.shape))], s).then_inc(weights.sem, 16)

            @block.gpsimd
            def _(pool):
                with pool.Fori(0, B) as i:
                    pool.wait_ge(var_ready.sem, var_ready.at(i + 1))
                    pool.tensor_tensor(stats[:, 9:10], stats[:, 8:9], core.neg_half[0:T, :], ALU.pow)\
                        .then_inc(rstd_ready.sem, 1)
                if tile:
                    pool.wait_ge(slots_ready.sem, slots_ready.at(1))
                    for b in range(B):
                        for k in range(topk):
                            pool.indirect_dma_start(
                                out=slots[:, :],
                                out_offset=bass.IndirectOffsetOnAxis(ap=core.slot_in[:, k, b:b + 1], axis=0),
                                in_=core.h_all[:, b, :], in_offset=None).then_inc(scattered.sem, 16)
                    pool.wait_ge(scattered.sem, scattered.at(16 * B * topk))

            @block.tensor
            def _(pe):
                pe.wait_ge(weights.sem, weights.at(16 * len(loads)))

                def body(b):
                    pe.wait_ge(normed_ready.sem, normed_ready.at(b.n + 1))
                    pe.wait_ge(taken_L.sem, taken_L.at(b.n - 1))
                    for k in range(DC):
                        ins = pe.transpose(psL[b.par][:, k * T:(k + 1) * T], normed[b.par][:, k * P:(k + 1) * P],
                                           core.ident[0:T, 0:T])
                    ins.then_inc(made_L.sem, 1)
                    pe.wait_ge(taken_L.sem, taken_L.at(b.n + 1))
                    pe.wait_ge(taken_G.sem, taken_G.at(b.n - 1))
                    for k in range(DC):
                        ins = pe.matmul(psG[b.par][0:T, 0:E], hT[b.par][:, k, :], wg[:, k, :],
                                        start=(k == 0), stop=(k == DC - 1))
                    ins.then_inc(made_G.sem, 1)

                pair_loop(pe, body, B)
                if tile:
                    pe.wait_ge(to_count.sem, to_count.at(1))
                    pe.matmul(pos[0:T, 0:BE], upto[:, :], both[:, :, :].rearrange("t b e -> t (b e)"),
                              start=True, stop=True)
                    pe.matmul(tot[0:T, 0:BE], core.ones[0:T, 0:T], both[:, :, :].rearrange("t b e -> t (b e)"),
                              start=True, stop=True).then_inc(counted.sem, 1)

            @block.scalar
            def _(act):
                act.preload_act_table(ACT.Exp)

                def body(b):
                    act.wait_ge(made_L.sem, made_L.at(b.n + 1))
                    src_ = psL[b.par][:, 0:DC * T].rearrange("p (k t) -> p k t", t=T)
                    act.activation(hT[b.par][:, :, :], src_, ACT.Copy).then_inc(taken_L.sem, 1)
                    if tile:
                        act.activation(batch_row(core.h_all, b), normed[b.par][:, :], ACT.Copy).then_inc(kept_copy.sem, 1)
                    else:
                        act.activation(core.hT_all[:, :, bass.ds(b.n * T, T)], src_, ACT.Copy).then_inc(kept_copy.sem, 1)

                act.wait_ge(core.zeroed_sem, 16 * (slots.shape[0] // (B * T)))
                pair_loop(act, body, B)
                act.wait_ge(to_exp.sem, to_exp.at(1))
                act.activation(scratch[:, :, :], scratch[:, :, :], ACT.Exp).then_inc(exped.sem, 1)

            @block.vector
            def _(dve):
                v = dve
                v.wait_ge(weights.sem, weights.at(16 * len(loads)))

                def take_logits(b):
                    v.wait_ge(made_G.sem, made_G.at(b.n + 1))
                    dst = logits[:, bass.ds(b.n, 1), :].rearrange("t a e -> t (a e)")
                    if biased:
                        v.tensor_tensor(dst, psG[b.par][0:T, 0:E], bg[:, :], ALU.add).then_inc(taken_G.sem, 1)
                    else:
                        v.tensor_copy(dst, psG[b.par][0:T, 0:E]).then_inc(taken_G.sem, 1)

                def body(b):
                    normalise_start(v, stats, batch_row(src, b), var_ready)
                    v.wait_ge(kept_copy.sem, kept_copy.at(b.n - 1))
                    v.wait_ge(rstd_ready.sem, rstd_ready.at(b.n + 1))
                    n = normed[b.par][:, :]
                    ins = v.tensor_scalar(n, batch_row(src, b), stats[:, 6:7], stats[:, 9:10], ALU.subtract, ALU.mult)
                    if affine:
                        v.drain()
                        v.tensor_tensor(n, n, gain[:, :], ALU.mult)
                        v.drain()
                        ins = v.tensor_tensor(n, n, shift[:, :], ALU.add)
                    ins.then_inc(normed_ready.sem, 1)
                    take_logits(b)

                pair_loop(v, body, B)

                def over_e(t):
                    return t[:, :].unsqueeze(2).broadcast_to([T, B, E])

                def over_b(t):
                    return t[:, :].unsqueeze(1).broadcast_to([T, B, E])

                v.drain()

                def first_best(l, m, i, eq):
                    v.tensor_reduce(m[:, :], l[:, :, :], AX, ALU.max)
                    v.drain()
                    v.tensor_tensor(eq[:, :, :], l[:, :, :], over_e(m), ALU.is_equal)
                    v.drain()
                    v.tensor_tensor(eq[:, :, :], eq[:, :, :], over_b(at_expert), ALU.mult)
                    v.drain()
                    v.tensor_reduce(i[:, :], eq[:, :, :], AX, ALU.min)
                    v.drain()
                    v.tensor_tensor(eq[:, :, :], over_b(at_expert), over_e(i), ALU.is_equal)
                    v.drain()

                first_best(logits, m1, i1, eq1)
                v.tensor_tensor(scratch[:, :, :], logits[:, :, :], over_e(m1), ALU.subtract).then_inc(to_exp.sem, 1)
                if topk == 2:
                    v.scalar_tensor_tensor(out=logits2[:, :, :], in0=eq1[:, :, :], scalar=NEG, in1=logits[:, :, :],
                                           op0=ALU.mult, op1=ALU.add)
                    v.drain()
                    first_best(logits2, m2, i2, eq2)
                    v.tensor_tensor(both[:, :, :], eq1[:, :, :], eq2[:, :, :], ALU.add).then_inc(to_count.sem, 1)
                else:
                    v.tensor_copy(both[:, :, :], eq1[:, :, :]).then_inc(to_count.sem, 1)
                v.wait_ge(exped.sem, exped.at(1))
                v.drain()
                if how in ("pair", "dense"):
                    v.tensor_tensor(scratch[:, :, :], scratch[:, :, :], both[:, :, :], ALU.mult)
                    v.drain()
                v.tensor_reduce(total[:, :], scratch[:, :, :], AX, ALU.add)
                v.drain()
                v.reciprocal(total[:, :], total[:, :])
                v.drain()
                if how == "dense":
                    v.memset(core.comb[:, :, E:], 1.0)
                    v.tensor_tensor(core.comb[:, :, 0:E], scratch[:, :, :], over_e(total), ALU.mult)
                    v.drain()
                if tile:
                    gate = core.gate
                    for k, eq in enumerate((eq1, eq2)[:topk]):
                        v.tensor_tensor(logits2[:, :, :], scratch[:, :, :], eq[:, :, :], ALU.mult)
                        v.drain()
                        v.tensor_reduce(m1[:, :], logits2[:, :, :], AX, ALU.add)
                        v.drain()
                        v.tensor_tensor(gate[:, k, :], m1[:, :], total[:, :], ALU.mult)
                        v.drain()
                    v.wait_ge(counted.sem, counted.at(1))
                    v.tensor_copy(sums_eb[:, :, :].rearrange("t e b -> t b e"),
                                  tot[0:T, 0:BE].rearrange("t (b e) -> t b e", e=E))
                    v.drain()
                    flat = "t e b -> t (e b)"
                    v.tensor_tensor_scan(scan[:, :, :].rearrange(flat), keepgoing[:, :, :].rearrange(flat),
                                         sums_eb[:, :, :].rearrange(flat), 0.0, ALU.mult, ALU.add)
                    v.drain()
                    if how != "cap":
                        v.tensor_tensor(over[:, :, :], scan[:, :, B - 1:B].broadcast_to([T, E, M]), steps[:, :, :], ALU.is_gt)
                        v.drain()
                        v.tensor_reduce(ntiles[:, :], over[:, :, :], AX, ALU.add)
                        v.drain()
                        v.tensor_tensor_scan(ends[:, :], core.ones[0:T, 0:E], ntiles[:, :], 0.0, ALU.mult, ALU.add)
                        v.drain()
                        v.tensor_tensor(starts[:, :], ends[:, :], ntiles[:, :], ALU.subtract)
                        v.drain()
                        v.tensor_scalar(starts[:, :], starts[:, :], float(tile), None, ALU.mult)
                        v.drain()
                        v.tensor_tensor(tiles_cmp[:, :, :], tiles[:, :, :],
                                        ends[0:1, :].unsqueeze(1).broadcast_to([1, NT, E]), ALU.is_ge)
                        v.drain()
                        v.tensor_reduce(eidf[:, :], tiles_cmp[:, :, :], AX, ALU.add)
                        v.drain()
                        v.tensor_scalar(eidf[:, :], eidf[:, :], float(E - 1), None, ALU.min)
                        v.drain()
                        v.tensor_copy(core.eid[0:1, 0:NT], eidf[:, :])
                    v.tensor_tensor(base[:, :, :], scan[:, :, :], sums_eb[:, :, :], ALU.subtract)
                    v.drain()
                    v.tensor_tensor(both[:, :, :], pos[0:T, 0:BE].rearrange("t (b e) -> t b e", e=E),
                                    base[:, :, :].rearrange("t e b -> t b e"), ALU.add)
                    v.drain()
                    for k, eq in enumerate((eq1, eq2)[:topk]):
                        v.tensor_tensor(scratch[:, :, :], both[:, :, :], eq[:, :, :], ALU.mult)
                        v.tensor_tensor(logits2[:, :, :], over_b(starts), eq[:, :, :], ALU.mult)
                        v.drain()
                        v.tensor_reduce(m1[:, :], scratch[:, :, :], AX, ALU.add)
                        v.tensor_reduce(m2[:, :], logits2[:, :, :], AX, ALU.add)
                        v.drain()
                        v.tensor_tensor(place[:, :], m1[:, :], m2[:, :], ALU.add)
                        v.drain()
                        v.tensor_scalar(place[:, :], place[:, :], -1.0, None, ALU.add)
                        v.drain()
                        if how == "cap":
                            v.tensor_scalar(kept[:, :], m1[:, :], float(tile), None, ALU.is_le)
                            v.drain()
                            v.tensor_tensor(gate[:, k, :], gate[:, k, :], kept[:, :], ALU.mult)
                            v.tensor_tensor(place[:, :], place[:, :], kept[:, :], ALU.mult)
                            v.tensor_tensor(m2[:, :], spare[:, k, :], kept[:, :], ALU.mult)
                            v.drain()
                            v.tensor_copy(core.slot_out[:, k, :], place[:, :])
                            v.tensor_tensor(m2[:, :], spare[:, k, :], m2[:, :], ALU.subtract)
                            v.drain()
                            v.tensor_tensor(place[:, :], place[:, :], m2[:, :], ALU.add)
                            v.drain()
                        else:
                            v.tensor_copy(core.slot_out[:, k, :], place[:, :])
                        v.tensor_copy(core.slot_in[:, k, :], place[:, :])
                        v.drain()
                    v.wait_ge(kept_copy.sem, kept_copy.at(B))
                    v.tensor_copy(place[:, :], m1[:, :]).then_inc(slots_ready.sem, 1)

        weights.stage_over(16 * len(loads))
        for s in (var_ready, rstd_ready, normed_ready, made_L, taken_L, made_G, taken_G, kept_copy):
            s.stage_over(B)
        to_exp.stage_over(1)
        exped.stage_over(1)
        to_count.stage_over(1)
        if tile:
            counted.stage_over(1)
            slots_ready.stage_over(1)
            scattered.stage_over(16 * B * topk)


def expert_tiles(nc, core, name, w, tile, NT, func, dynamic):
    CH = -(-tile // P)
    CW = tile // CH
    F = w["w1"].shape[3] // P
    ctx = ExitStack()
    with ctx:
        def sb(n, shape, dt=F32):
            return ctx.enter_context(nc.sbuf_tensor(f"{name}_{n}", shape, dt))

        w1 = [sb(f"w1_{i}", [P, DC, F * P]) for i in range(2)]
        w2 = [sb(f"w2_{i}", [P, F, D]) for i in range(2)]
        b1 = [sb(f"b1_{i}", [P, F]) for i in range(2)]
        b2 = [sb(f"b2_{i}", [CW, D]) for i in range(2)]
        xs = [sb(f"xs{i}", [CW, CH, D]) for i in range(2)]
        xT = sb("xT", [P, DC, tile])
        hidden = sb("hidden", [P, F, tile])
        ys = [sb(f"ys{i}", [CW, CH, D]) for i in range(2)]
        x_here = [core.counter(f"ctx_here{i}") for i in range(2)]
        w_here = [core.counter(f"w_here{i}") for i in range(2)]
        xT_made, xT_taken = core.counter("made_L"), core.counter("taken_L")
        h_made, h_taken = core.counter("made_H"), core.counter("taken_H")
        y_made, y_taken = core.counter("made_Y"), core.counter("taken_Y")
        stored = [core.counter(f"y_stored{i}") for i in range(2)]
        slots_in, slots_out = core.slots_in, core.slots_out
        psX, psH, psY = core.bank[0:2], core.bank[2:6], core.bank[6:8]
        eid = core.eid

        def rows(dram, t):
            return dram[bass.ds(t.n * tile, tile), :].rearrange("(c p) d -> p c d", p=CW)

        with nc.Block() as block:

            @block.sync
            def _(sp):
                def store(t):
                    sp.dma_start(rows(slots_out, t), ys[t.par][:, :, :]).then_inc(stored[t.par].sem, 16)

                def load(t, wait):
                    if wait:
                        sp.wait_ge(xT_made.sem, xT_made.at(t.n - 1))
                    sp.dma_start(xs[t.par][:, :, :], rows(slots_in, t)).then_inc(x_here[t.par].sem, 16)
                    if dynamic:
                        e = sp.value_load(eid[0:1, bass.ds(t.n, 1)], min_val=0, max_val=w["w1"].shape[0] - 1)
                    else:
                        e = t.n
                    if wait:
                        sp.wait_ge(h_taken.sem, h_taken.at(F * (t.n - 1)))
                    sp.dma_start(w1[t.par][:, :, :], w["w1"][bass.ds(e, 1)].rearrange("a p k f -> p (a k) f"))\
                        .then_inc(w_here[t.par].sem, 16)
                    sp.dma_start(b1[t.par][:, :], w["b1"][bass.ds(e, 1)].rearrange("a p f -> p (a f)"))\
                        .then_inc(w_here[t.par].sem, 16)
                    if wait:
                        sp.wait_ge(y_taken.sem, y_taken.at(CH * (t.n - 1)))
                        store(t + -2)
                    sp.dma_start(w2[t.par][:, :, :], w["w2"][bass.ds(e, 1)].rearrange("a p f d -> p (a f) d"))\
                        .then_inc(w_here[t.par].sem, 16)
                    sp.dma_start(b2[t.par][:, :], w["b2"][bass.ds(e, 1)].rearrange("a d -> (a d)").partition_broadcast(CW))\
                        .then_inc(w_here[t.par].sem, 16)

                load(Batch(0, 0), False)
                load(Batch(0, 1), False)
                with sp.Fori(0, (NT - 2) // 2) as i:
                    load(Batch(i, 2), True)
                    load(Batch(i, 3), True)
                if NT % 2:
                    load(Batch(0, NT - 1), True)
                for t in (NT - 2, NT - 1):
                    sp.wait_ge(y_taken.sem, y_taken.at(CH * (t + 1)))
                    store(Batch(0, t))
                for i in range(2):
                    sp.wait_ge(stored[i].sem, stored[i].at(16 * ((NT + 1 - i) // 2)))

            def run(engine, body):
                n = (NT - 1) // 2
                with engine.Fori(0, n) as i:
                    body(Batch(i, 0), False)
                    body(Batch(i, 1), False)
                for t in range(2 * n, NT):
                    body(Batch(0, t), t == NT - 1)

            @block.tensor
            def _(pe):
                def turn(t):
                    pe.wait_ge(x_here[t.par].sem, x_here[t.par].at(16 * t.half + 16))
                    pe.wait_ge(xT_taken.sem, xT_taken.at(t.n))
                    for k in range(DC):
                        for c in range(CH):
                            ins = pe.transpose(psX[k][:, c * CW:(c + 1) * CW], xs[t.par][:, c, k * P:(k + 1) * P],
                                               core.ident[0:CW, 0:CW])
                    ins.then_inc(xT_made.sem, 1)

                def body(t, last):
                    pe.wait_ge(w_here[t.par].sem, w_here[t.par].at(64 * t.half + 64))
                    pe.wait_ge(xT_taken.sem, xT_taken.at(t.n + 1))
                    for f in range(F):
                        pe.wait_ge(h_taken.sem, h_taken.at(F * t.n + (f - 3)))
                        for k in range(DC):
                            ins = pe.matmul(psH[f % 4][:, 0:tile], w1[t.par][:, k, f * P:(f + 1) * P], xT[:, k, :],
                                            start=(k == 0), stop=(k == DC - 1))
                        ins.then_inc(h_made.sem, 1)
                    if not last:
                        turn(t + 1)
                    for c in range(CH):
                        pe.wait_ge(y_taken.sem, y_taken.at(CH * t.n + (c - 1)))
                        for f in range(F):
                            if c == 0:
                                pe.wait_ge(h_taken.sem, h_taken.at(F * t.n + (f + 1)))
                            ins = pe.matmul(psY[c % 2][0:CW, 0:D], hidden[:, f, c * CW:(c + 1) * CW], w2[t.par][:, f, :],
                                            start=(f == 0), stop=(f == F - 1))
                        ins.then_inc(y_made.sem, 1)

                turn(Batch(0, 0))
                run(pe, body)

            @block.scalar
            def _(act):
                act.preload_act_table(func)

                def take_xT(t):
                    act.wait_ge(xT_made.sem, xT_made.at(t.n + 1))
                    act.activation(xT[:, 0, :], psX[0][:, 0:tile], ACT.Copy)
                    act.activation(xT[:, 1, :], psX[1][:, 0:tile], ACT.Copy).then_inc(xT_taken.sem, 1)

                def body(t, last):
                    act.wait_ge(w_here[t.par].sem, w_here[t.par].at(64 * t.half + 64))
                    for f in range(F):
                        act.wait_ge(h_made.sem, h_made.at(F * t.n + (f + 1)))
                        act.activation(hidden[:, f, :], psH[f % 4][:, 0:tile], func, bias=b1[t.par][:, f:f + 1])\
                            .then_inc(h_taken.sem, 1)
                    if not last:
                        take_xT(t + 1)

                take_xT(Batch(0, 0))
                run(act, body)

            @block.vector
            def _(dve):
                def body(t, last):
                    dve.wait_ge(w_here[t.par].sem, w_here[t.par].at(64 * t.half + 64))
                    dve.wait_ge(stored[t.par].sem, stored[t.par].at(16 * t.half))
                    for c in range(CH):
                        dve.wait_ge(y_made.sem, y_made.at(CH * t.n + (c + 1)))
                        dve.tensor_tensor(ys[t.par][:, c, :], psY[c % 2][0:CW, 0:D], b2[t.par][:, :], ALU.add)\
                            .then_inc(y_taken.sem, 1)

                run(dve, body)

        for i in range(2):
            x_here[i].stage_over(16 * ((NT + 1 - i) // 2))
            w_here[i].stage_over(64 * ((NT + 1 - i) // 2))
            stored[i].stage_over(16 * ((NT + 1 - i) // 2))
        xT_made.stage_over(NT)
        xT_taken.stage_over(NT)
        h_made.stage_over(F * NT)
        h_taken.stage_over(F * NT)
        y_made.stage_over(CH * NT)
        y_taken.stage_over(CH * NT)


def combine(nc, core, name, topk):
    R = 8
    with ExitStack() as ctx:
        got = [ctx.enter_context(nc.sbuf_tensor(f"{name}_got{r}", [T, topk, D], F32)) for r in range(R)]
        gathered = [core.counter(f"gathered{r}") for r in range(R)]
        added = core.counter("taken_Y")
        with nc.Block() as block:

            @block.gpsimd
            def _(pool):
                for b in range(B):
                    if b >= R:
                        pool.wait_ge(added.sem, added.at(b - R + 1))
                    for k in range(topk):
                        pool.indirect_dma_start(
                            out=got[b % R][:, k, :], out_offset=None, in_=core.slots_out[:, :],
                            in_offset=bass.IndirectOffsetOnAxis(ap=core.slot_out[:, k, b:b + 1], axis=0))\
                            .then_inc(gathered[b % R].sem, 16)

            @block.vector
            def _(dve):
                for b in range(B):
                    dve.wait_ge(gathered[b % R].sem, gathered[b % R].at(16 * topk * (b // R + 1)))
                    for k in range(topk):
                        ins = dve.scalar_tensor_tensor(out=core.x[:, b, :], in0=got[b % R][:, k, :],
                                                       scalar=core.gate[:, k, b:b + 1], in1=core.x[:, b, :],
                                                       op0=ALU.mult, op1=ALU.add)
                        if k < topk - 1:
                            dve.drain()
                    ins.then_inc(added.sem, 1)

        for r in range(R):
            gathered[r].stage_over(16 * topk * (B // R))
        added.stage_over(B)


def dense_experts(nc, core, name, w, NE):
    GT, GB = 4 * T, 4
    NG = B // GB
    ctx = ExitStack()
    with ctx:
        def sb(n, shape, dt=F32):
            return ctx.enter_context(nc.sbuf_tensor(f"{name}_{n}", shape, dt))

        wu = [sb(f"wu{i}", [P, DC, P]) for i in range(2)]
        wg = [sb(f"wg{i}", [P, DC, P]) for i in range(2)]
        wd = [sb(f"wd{i}", [P, D]) for i in range(2)]
        silu = [sb(f"silu{i}", [P, GT]) for i in range(2)]
        hidden = [sb(f"hidden{i}", [P, GT]) for i in range(2)]
        comb = [sb(f"comb{i}", [T, B]) for i in range(2)]
        w_here = [core.counter(f"w_here{i}") for i in range(2)]
        g_made, g_taken = core.counter("made_G"), core.counter("taken_G")
        u_made, u_taken = core.counter("made_H"), core.counter("taken_H")
        y_made, y_taken = core.counter("made_Y"), core.counter("taken_Y")
        psG, psU, psY = core.bank[0:2], core.bank[2:4], core.bank[4:8]

        with nc.Block() as block:

            @block.sync
            def _(sp):
                def load(e, wait):
                    if wait:
                        sp.wait_ge(y_made.sem, y_made.at(B * (e.n - 1)))
                    for dst, src in ((wg, "wg"), (wu, "wu")):
                        sp.dma_start(dst[e.par][:, :, :], w[src][bass.ds(e.n, 1)].rearrange("a p k f -> p (a k) f"))\
                            .then_inc(w_here[e.par].sem, 16)
                    sp.dma_start(wd[e.par][:, :], w["wd"][bass.ds(e.n, 1)].rearrange("a p d -> p (a d)"))\
                        .then_inc(w_here[e.par].sem, 16)

                load(Batch(0, 0), False)
                load(Batch(0, 1), False)
                with sp.Fori(0, (NE - 2) // 2) as i:
                    load(Batch(i, 2), True)
                    load(Batch(i, 3), True)

            @block.tensor
            def _(pe):
                def up(e, g):
                    n = NG * e.n + g
                    if g == 0:
                        pe.wait_ge(w_here[e.par].sem, w_here[e.par].at(48 * e.half + 48))
                    h = core.hT_all[:, :, g * GT:(g + 1) * GT]
                    pe.wait_ge(g_taken.sem, g_taken.at(n - 1))
                    for k in range(DC):
                        ins = pe.matmul(psG[g % 2][:, 0:GT], wg[e.par][:, k, :], h[:, k, :],
                                        start=(k == 0), stop=(k == DC - 1))
                    ins.then_inc(g_made.sem, 1)
                    pe.wait_ge(u_taken.sem, u_taken.at(n - 1))
                    for k in range(DC):
                        ins = pe.matmul(psU[g % 2][:, 0:GT], wu[e.par][:, k, :], h[:, k, :],
                                        start=(k == 0), stop=(k == DC - 1))
                    ins.then_inc(u_made.sem, 1)

                def down(e, g):
                    pe.wait_ge(u_taken.sem, u_taken.at(NG * e.n + (g + 1)))
                    for c in range(GB):
                        pe.wait_ge(y_taken.sem, y_taken.at(B * e.n + (GB * g + c - 3)))
                        pe.matmul(psY[c][0:T, 0:D], hidden[g % 2][:, c * T:(c + 1) * T], wd[e.par][:, :],
                                  start=True, stop=True).then_inc(y_made.sem, 1)

                def body(e):
                    for g in range(NG):
                        up(e, g)
                        if g:
                            down(e, g - 1)
                    down(e, NG - 1)

                pair_loop(pe, body, NE)

            @block.scalar
            def _(act):
                act.preload_act_table(ACT.Silu)

                def body(e):
                    for g in range(NG):
                        act.wait_ge(g_made.sem, g_made.at(NG * e.n + (g + 1)))
                        act.wait_ge(u_taken.sem, u_taken.at(NG * e.n + (g - 1)))
                        act.activation(silu[g % 2][:, :], psG[g % 2][:, 0:GT], ACT.Silu).then_inc(g_taken.sem, 1)

                pair_loop(act, body, NE)

            @block.vector
            def _(dve):
                def mix(e, g):
                    dve.wait_ge(g_taken.sem, g_taken.at(NG * e.n + (g + 1)))
                    dve.wait_ge(u_made.sem, u_made.at(NG * e.n + (g + 1)))
                    dve.tensor_tensor(hidden[g % 2][:, :], silu[g % 2][:, :], psU[g % 2][:, 0:GT], ALU.mult)\
                        .then_inc(u_taken.sem, 1)

                def add(e, g):
                    for c in range(GB):
                        b = GB * g + c
                        dve.wait_ge(y_made.sem, y_made.at(B * e.n + (b + 1)))
                        dve.scalar_tensor_tensor(out=core.x[:, b, :], in0=psY[c][0:T, 0:D],
                                                 scalar=comb[e.par][:, b:b + 1], in1=core.x[:, b, :],
                                                 op0=ALU.mult, op1=ALU.add).then_inc(y_taken.sem, 1)

                def body(e):
                    dve.tensor_copy(comb[e.par][:, :],
                                    core.comb[:, :, bass.ds(e.n, 1)].rearrange("t b a -> t (b a)"))
                    dve.drain()
                    for g in range(NG):
                        mix(e, g)
                        if g:
                            add(e, g - 1)
                    add(e, NG - 1)

                pair_loop(dve, body, NE)

        for i in range(2):
            w_here[i].stage_over(48 * NE // 2)
        for s in (g_made, g_taken, u_made, u_taken):
            s.stage_over(NG * NE)
        y_made.stage_over(B * NE)
        y_taken.stage_over(B * NE)


def relu_attention(nc, core, name, ctx_in, w):
    scale = float(D) ** -0.5
    ctx = ExitStack()
    with ctx:
        def sb(n, shape, dt=F32):
            return ctx.enter_context(nc.sbuf_tensor(f"{name}_{n}", shape, dt))

        wq, wk, wv = (sb(n, [P, DC, D]) for n in ("wq", "wk", "wv"))
        bq, bk, bv = sb("bq", [P, DC]), sb("bk", [P, DC]), sb("bv", [1, D])
        maskT = sb("maskT", [SJ, J, T])
        ctxT = [sb(f"ctxT{i}", [P, DC, S]) for i in range(2)]
        stats = sb("stats", [T, 16])
        normed = sb("normed", [T, D])
        hT = sb("hT", [P, DC, T])
        q = [sb(f"q{i}", [P, DC, T]) for i in range(2)]
        kT = [sb(f"kT{i}", [P, DC, S]) for i in range(2)]
        v = [sb(f"v{i}", [SJ, J, D]) for i in range(2)]
        weightsT = sb("weightsT", [SJ, J, T])
        weights = core.counter("weights")
        ctx_here = [core.counter(f"ctx_here{i}") for i in range(2)]
        var_ready = core.counter("var_ready")
        rstd_ready = core.counter("rstd_ready")
        normed_ready = core.counter("normed_ready")
        scored = core.counter("scored")
        mixed = core.counter("probsT_ready")
        made = {c: core.counter(f"made_{c}") for c in "LQKVY"}
        taken = {c: core.counter(f"taken_{c}") for c in "LQKVY"}
        loads = [(wq, w["wq"]), (wk, w["wk"]), (wv, w["wv"]), (bq, w["bq"]), (bk, w["bk"]), (bv, w["bv"]),
                 (maskT, w["maskT"])]
        psL, psQ, psK, psV, psS, psY = (core.bank[0], core.bank[1], core.bank[2:4], core.bank[4:6], core.bank[6],
                                        core.bank[7])

        def run(engine, first, heads):
            first(Batch(0, 0))
            heads(Batch(0, 0), False)
            with engine.Fori(0, (B - 2) // 2) as i:
                heads(Batch(i, 1), False)
                heads(Batch(i, 2), False)
            heads(Batch(0, B - 1), True)

        with nc.Block() as block:

            @block.sync
            def _(sp):
                for dst, s in loads:
                    sp.dma_start(dst[tuple([slice(None)] * len(dst.shape))], s).then_inc(weights.sem, 16)

                def load(b):
                    sp.dma_start(ctxT[b.par][:, :, :], ctx_in[bass.ds(b.n, 1)].rearrange("a p c s -> p (a c) s"))\
                        .then_inc(ctx_here[b.par].sem, 16)

                load(Batch(0, 0))
                load(Batch(0, 1))
                with sp.Fori(0, (B - 2) // 2) as i:
                    for k in (2, 3):
                        b = Batch(i, k)
                        sp.wait_ge(made["V"].sem, made["V"].at(J * (b.n - 1)))
                        load(b)

            @block.gpsimd
            def _(pool):
                with pool.Fori(0, B) as i:
                    pool.wait_ge(var_ready.sem, var_ready.at(i + 1))
                    pool.tensor_tensor(stats[:, 9:10], stats[:, 8:9], core.neg_half[0:T, :], ALU.pow)\
                        .then_inc(rstd_ready.sem, 1)

            @block.tensor
            def _(pe):
                pe.wait_ge(weights.sem, weights.at(16 * len(loads)))

                def keys(b):
                    pe.wait_ge(ctx_here[b.par].sem, ctx_here[b.par].at(16 * b.half + 16))
                    pe.wait_ge(taken["K"].sem, taken["K"].at(DC * b.n))
                    for c in range(DC):
                        for k in range(DC):
                            ins = pe.matmul(psK[c][:, 0:S], wk[:, k, c * P:(c + 1) * P], ctxT[b.par][:, k, :],
                                            start=(k == 0), stop=(k == DC - 1))
                        ins.then_inc(made["K"].sem, 1)

                def queries(b):
                    pe.wait_ge(normed_ready.sem, normed_ready.at(b.n + 1))
                    for k in range(DC):
                        ins = pe.transpose(psL[:, k * T:(k + 1) * T], normed[:, k * P:(k + 1) * P], core.ident[0:T, 0:T])
                    ins.then_inc(made["L"].sem, 1)

                def queries_end(b):
                    pe.wait_ge(taken["L"].sem, taken["L"].at(b.n + 1))
                    pe.wait_ge(taken["Q"].sem, taken["Q"].at(b.n))
                    for c in range(DC):
                        for k in range(DC):
                            ins = pe.matmul(psQ[:, c * T:(c + 1) * T], wq[:, k, c * P:(c + 1) * P], hT[:, k, :],
                                            start=(k == 0), stop=(k == DC - 1))
                    ins.then_inc(made["Q"].sem, 1)

                def values(b, j):
                    pe.wait_ge(taken["V"].sem, taken["V"].at(J * b.n + (j - 1)))
                    for k in range(DC):
                        pe.matmul(psV[(b.par * J + j) % 2][0:SJ, 0:D], ctxT[b.par][:, k, j * SJ:(j + 1) * SJ],
                                  wv[:, k, :], start=(k == 0), stop=False)
                    pe.matmul(psV[(b.par * J + j) % 2][0:SJ, 0:D], core.ones[0:1, 0:SJ], bv[0:1, :],
                              start=False, stop=True).then_inc(made["V"].sem, 1)

                def first(b):
                    keys(b)
                    queries(b)
                    for j in range(J):
                        values(b, j)
                    queries_end(b)

                def heads(b, last):
                    pe.wait_ge(taken["Q"].sem, taken["Q"].at(b.n + 1))
                    pe.wait_ge(taken["K"].sem, taken["K"].at(DC * b.n + DC))
                    for j in range(J):
                        for k in range(DC):
                            ins = pe.matmul(psS[0:SJ, j * T:(j + 1) * T], kT[b.par][:, k, j * SJ:(j + 1) * SJ],
                                            q[b.par][:, k, :], start=(k == 0), stop=(k == DC - 1))
                    ins.then_inc(scored.sem, 1)
                    if not last:
                        keys(b + 1)
                        queries(b + 1)
                        values(b + 1, 0)
                        queries_end(b + 1)
                        values(b + 1, 1)
                        values(b + 1, 2)
                    pe.wait_ge(mixed.sem, mixed.at(b.n + 1))
                    pe.wait_ge(taken["V"].sem, taken["V"].at(J * b.n + J))
                    pe.wait_ge(taken["Y"].sem, taken["Y"].at(b.n))
                    for j in range(J):
                        ins = pe.matmul(psY[0:T, 0:D], weightsT[:, j, :], v[b.par][:, j, :],
                                        start=(j == 0), stop=(j == J - 1))
                    ins.then_inc(made["Y"].sem, 1)

                run(pe, first, heads)

            @block.scalar
            def _(act):
                act.preload_act_table(ACT.Relu)
                act.wait_ge(weights.sem, weights.at(16 * len(loads)))

                def take(b):
                    for c in range(DC):
                        act.wait_ge(made["K"].sem, made["K"].at(DC * b.n + (c + 1)))
                        act.activation(kT[b.par][:, c, :], psK[c][:, 0:S], ACT.Relu, bias=bk[:, c:c + 1])\
                            .then_inc(taken["K"].sem, 1)
                    act.wait_ge(made["L"].sem, made["L"].at(b.n + 1))
                    act.activation(hT[:, :, :], psL[:, 0:DC * T].rearrange("p (k t) -> p k t", t=T), ACT.Copy)\
                        .then_inc(taken["L"].sem, 1)

                def take_values(b, j):
                    act.wait_ge(made["V"].sem, made["V"].at(J * b.n + (j + 1)))
                    act.activation(v[b.par][:, j, :], psV[(b.par * J + j) % 2][0:SJ, 0:D], ACT.Relu)\
                        .then_inc(taken["V"].sem, 1)

                def take_queries(b):
                    act.wait_ge(made["Q"].sem, made["Q"].at(b.n + 1))
                    for c in range(DC):
                        ins = act.activation(q[b.par][:, c, :], psQ[:, c * T:(c + 1) * T], ACT.Relu, bias=bq[:, c:c + 1])
                    ins.then_inc(taken["Q"].sem, 1)

                def first(b):
                    take(b)
                    for j in range(J):
                        take_values(b, j)
                    take_queries(b)

                def heads(b, last):
                    if not last:
                        take(b + 1)
                        take_values(b + 1, 0)
                        take_queries(b + 1)
                        take_values(b + 1, 1)
                        take_values(b + 1, 2)

                run(act, first, heads)

            @block.vector
            def _(dve):
                dve.wait_ge(weights.sem, weights.at(16 * len(loads)))

                def normalise_end(b):
                    dve.wait_ge(rstd_ready.sem, rstd_ready.at(b.n + 1))
                    dve.tensor_scalar(normed[:, :], batch_row(core.x, b), stats[:, 6:7], stats[:, 9:10],
                                      ALU.subtract, ALU.mult).then_inc(normed_ready.sem, 1)

                def first(b):
                    normalise_start(dve, stats, batch_row(core.x, b), var_ready)
                    normalise_end(b)

                def heads(b, last):
                    if not last:
                        normalise_start(dve, stats, batch_row(core.x, b + 1), var_ready)
                    dve.wait_ge(scored.sem, scored.at(b.n + 1))
                    if not last:
                        normalise_end(b + 1)
                    src = psS[0:SJ, 0:J * T].rearrange("p (j t) -> p j t", t=T)
                    dve.tensor_scalar(weightsT[:, :, :], src, scale, 0.0, ALU.mult, ALU.max)
                    dve.drain()
                    dve.tensor_tensor(weightsT[:, :, :], weightsT[:, :, :], maskT[:, :, :], ALU.add)\
                        .then_inc(mixed.sem, 1)
                    dve.wait_ge(made["Y"].sem, made["Y"].at(b.n + 1))
                    dve.scalar_tensor_tensor(out=batch_row(core.x, b), in0=psY[0:T, 0:D], scalar=0.0,
                                             in1=batch_row(core.x, b), op0=ALU.max, op1=ALU.add)\
                        .then_inc(taken["Y"].sem, 1)

                run(dve, first, heads)

        weights.stage_over(16 * len(loads))
        for s in ctx_here:
            s.stage_over(16 * B // 2)
        for s in (var_ready, rstd_ready, normed_ready, scored, mixed, made["L"], taken["L"], made["Q"], taken["Q"],
                  made["Y"], taken["Y"]):
            s.stage_over(B)
        for s, n in ((made["K"], DC), (taken["K"], DC), (made["V"], J), (taken["V"], J)):
            s.stage_over(B * n)


def self_attention(nc, core, name, w):
    HG, G = 4, 4
    ctx = ExitStack()
    with ctx:
        def sb(n, shape, dt=F32):
            return ctx.enter_context(nc.sbuf_tensor(f"{name}_{n}", shape, dt))

        wqkv, wo = sb("wqkv", [P, DC, 3 * D]), sb("wo", [P, DC, D])
        gain, shift = sb("gain", [P, DC]), sb("shift", [P, DC])
        cos, sin, causal = sb("cos", [T, 16]), sb("sin", [T, 16]), sb("causal", [T, T])
        headmask = sb("headmask", [P, 8])
        stats = sb("stats", [T, 16])
        normed = sb("normed", [T, D])
        hT = sb("hT", [P, DC, T])
        turned_by, turned_q = sb("turned_by", [T, 2 * H, 16]), sb("turned_q", [T, 2 * H, 16])
        qT = sb("qT", [P, DC, T])
        keys = sb("keys", [P, H, T])
        v = [sb(f"v{i}", [T, D]) for i in range(2)]
        masked = [sb(f"masked{i}", [T, G, T]) for i in range(2)]
        probs = [sb(f"probs{i}", [T, G, T]) for i in range(2)]
        probsT = [sb(f"probsT{i}", [T, G, T]) for i in range(2)]
        negmax = [sb(f"negmax{i}", [T, H]) for i in range(2)]
        sums = [sb(f"sums{i}", [T, H]) for i in range(2)]
        inverse = sb("inverse", [T, H])
        o, oT = sb("o", [T, D]), sb("oT", [P, DC, T])
        weights = core.counter("weights")
        var_ready = core.counter("var_ready")
        rstd_ready = core.counter("rstd_ready")
        normed_ready = core.counter("normed_ready")
        scored, maxed = core.counter("scored"), core.counter("maxed")
        exped, turned = core.counter("exped"), core.counter("turned")
        probsT_ready, pv_done = core.counter("probsT_ready"), core.counter("pv_done")
        o_ready = core.counter("o_ready")
        qk_made, rope_done = core.counter("qkv_made"), core.counter("rope_done")
        r_made = core.counter("made_K")
        keys_ready, q_ready = core.counter("taken_K"), core.counter("taken_Q")
        made = {c: core.counter(f"made_{c}") for c in "LVOY"}
        taken = {c: core.counter(f"taken_{c}") for c in "LVOY"}
        loads = [(wqkv, w["wqkv"]), (wo, w["wo"]), (gain, w["g"]), (shift, w["b"]), (cos, w["cos"]), (sin, w["sin"]),
                 (causal, w["causal"]), (headmask, w["headmask"])]
        psL, psQK, psV, psR = core.bank[0], core.bank[1], core.bank[2], core.bank[3]
        psS, psT, psO = core.bank[4:6], core.bank[6], core.bank[7]

        def run(engine, first, heads):
            first()
            heads(Batch(0, 0), False, True, True)
            with engine.Fori(0, (B - 4) // 2) as i:
                heads(Batch(i, 1), True, True, True)
                heads(Batch(i, 2), True, True, True)
            heads(Batch(0, B - 3), True, True, True)
            heads(Batch(0, B - 2), True, True, False)
            heads(Batch(0, B - 1), True, False, False)

        with nc.Block() as block:

            @block.sync
            def _(sp):
                for dst, s in loads:
                    sp.dma_start(dst[tuple([slice(None)] * len(dst.shape))], s).then_inc(weights.sem, 16)

            @block.gpsimd
            def _(pool):
                with pool.Fori(0, 2 * B) as i:
                    pool.wait_ge(var_ready.sem, var_ready.at(i + 1))
                    pool.tensor_tensor(stats[:, 9:10], stats[:, 8:9], core.neg_half[0:T, :], ALU.pow)\
                        .then_inc(rstd_ready.sem, 1)

            @block.tensor
            def _(pe):
                pe.wait_ge(weights.sem, weights.at(16 * len(loads)))

                def turn_tokens(b, before_):
                    pe.wait_ge(normed_ready.sem, normed_ready.at(b.n + 1))
                    if before_:
                        pe.wait_ge(taken["O"].sem, taken["O"].at(b.n - 2))
                    pe.wait_ge(taken["L"].sem, taken["L"].at(b.n))
                    for k in range(DC):
                        ins = pe.transpose(psL[:, k * T:(k + 1) * T], normed[:, k * P:(k + 1) * P], core.ident[0:T, 0:T])
                    ins.then_inc(made["L"].sem, 1)

                def project(b):
                    pe.wait_ge(taken["L"].sem, taken["L"].at(b.n + 1))
                    pe.wait_ge(rope_done.sem, rope_done.at(b.n))
                    for k in range(DC):
                        ins = pe.matmul(psQK[0:T, 0:2 * D], hT[:, k, :], wqkv[:, k, 0:2 * D],
                                        start=(k == 0), stop=(k == DC - 1))
                    ins.then_inc(qk_made.sem, 1)
                    pe.wait_ge(taken["V"].sem, taken["V"].at(b.n))
                    for k in range(DC):
                        ins = pe.matmul(psV[0:T, 0:D], hT[:, k, :], wqkv[:, k, 2 * D:3 * D],
                                        start=(k == 0), stop=(k == DC - 1))
                    ins.then_inc(made["V"].sem, 1)

                def turn_rotated(b, before_):
                    pe.wait_ge(rope_done.sem, rope_done.at(b.n + 1))
                    if before_:
                        pe.wait_ge(taken["Y"].sem, taken["Y"].at(b.n - 1))
                    for c in range(2 * DC):
                        ins = pe.transpose(psR[:, c * T:(c + 1) * T],
                                           turned_q[:, c * 8:(c + 1) * 8, :].rearrange("t h e -> t (h e)"),
                                           core.ident[0:T, 0:T])
                    ins.then_inc(r_made.sem, 1)

                def scores(b, g):
                    if g == 0:
                        pe.wait_ge(q_ready.sem, q_ready.at(b.n + 1))
                        pe.wait_ge(keys_ready.sem, keys_ready.at(b.n + 1))
                    pe.matmul(psS[g % 2][0:T, 0:G * T], qT[:, g // 2, :], keys[:, G * g:G * g + G, :],
                              start=True, stop=True).then_inc(scored.sem, 1)

                def turn(b, g):
                    pe.wait_ge(exped.sem, exped.at(HG * b.n + (g + 1)))
                    for h in range(G):
                        ins = pe.transpose(psT[0:T, h * T:(h + 1) * T], probs[g % 2][:, h, :], core.ident[0:T, 0:T])
                    ins.then_inc(turned.sem, 1)

                def values(b, g):
                    pe.wait_ge(probsT_ready.sem, probsT_ready.at(HG * b.n + (g + 1)))
                    if g == 0:
                        pe.wait_ge(taken["V"].sem, taken["V"].at(b.n + 1))
                    for h in range(G):
                        at = (G * g + h) * 16
                        ins = pe.matmul(psO[0:T, at:at + 16], probsT[g % 2][:, h, :], v[b.par][:, at:at + 16],
                                        start=True, stop=True)
                    ins.then_inc(pv_done.sem, 1)

                def turn_outputs(b, after):
                    pe.wait_ge(o_ready.sem, o_ready.at(b.n + 1))
                    if after:
                        pe.wait_ge(taken["L"].sem, taken["L"].at(b.n + 3))
                    for c in range(DC):
                        ins = pe.transpose(psL[:, (2 + c) * T:(3 + c) * T], o[:, c * P:(c + 1) * P], core.ident[0:T, 0:T])
                    ins.then_inc(made["O"].sem, 1)

                def output(b):
                    pe.wait_ge(taken["O"].sem, taken["O"].at(b.n + 1))
                    for c in range(DC):
                        ins = pe.matmul(psR[0:T, 0:D], oT[:, c, :], wo[:, c, :], start=(c == 0), stop=(c == DC - 1))
                    ins.then_inc(made["Y"].sem, 1)

                def first():
                    turn_tokens(Batch(0, 0), False)
                    project(Batch(0, 0))
                    turn_rotated(Batch(0, 0), False)

                def heads(b, prior, after, after2):
                    scores(b, 0)
                    if after:
                        turn_tokens(b + 1, prior)
                    scores(b, 1)
                    turn(b, 0)
                    if prior:
                        turn_outputs(b + -1, after)
                    values(b, 0)
                    if after:
                        project(b + 1)
                    scores(b, 2)
                    turn(b, 1)
                    if prior:
                        output(b + -1)
                    values(b, 1)
                    scores(b, 3)
                    turn(b, 2)
                    values(b, 2)
                    if after:
                        turn_rotated(b + 1, prior)
                    turn(b, 3)
                    values(b, 3)

                run(pe, first, heads)
                turn_outputs(Batch(0, B - 1), None)
                output(Batch(0, B - 1))

            @block.scalar
            def _(act):
                act.preload_act_table(ACT.Exp)
                act.wait_ge(weights.sem, weights.at(16 * len(loads)))

                def take_tokens(b):
                    act.wait_ge(made["L"].sem, made["L"].at(b.n + 1))
                    for k in range(DC):
                        ins = act.activation(hT[:, k, :], psL[:, k * T:(k + 1) * T], ACT.Identity,
                                             bias=shift[:, k:k + 1], scale=gain[:, k:k + 1])
                    ins.then_inc(taken["L"].sem, 1)

                def take_values(b):
                    act.wait_ge(made["V"].sem, made["V"].at(b.n + 1))
                    act.activation(v[b.par][:, :], psV[0:T, 0:D], ACT.Copy).then_inc(taken["V"].sem, 1)

                def take_queries(b):
                    act.wait_ge(r_made.sem, r_made.at(b.n + 1))
                    act.activation(qT[:, :, :], psR[:, 0:DC * T].rearrange("p (c t) -> p c t", t=T), ACT.Copy)\
                        .then_inc(q_ready.sem, 1)

                def take_outputs(b):
                    act.wait_ge(made["O"].sem, made["O"].at(b.n + 1))
                    act.activation(oT[:, :, :], psL[:, 2 * T:4 * T].rearrange("p (c t) -> p c t", t=T), ACT.Copy)\
                        .then_inc(taken["O"].sem, 1)

                def exps(b, g):
                    act.wait_ge(maxed.sem, maxed.at(HG * b.n + (g + 1)))
                    for h in range(G):
                        at = G * g + h
                        ins = act.activation(probs[g % 2][:, h, :], masked[g % 2][:, h, :], ACT.Exp,
                                             bias=negmax[b.par][:, at:at + 1], accum_out=sums[b.par][:, at:at + 1])
                    ins.then_inc(exped.sem, 1)

                def take_probsT(b, g):
                    act.wait_ge(turned.sem, turned.at(HG * b.n + (g + 1)))
                    act.activation(probsT[g % 2][:, :, :], psT[0:T, 0:G * T].rearrange("p (h t) -> p h t", t=T),
                                   ACT.Copy).then_inc(probsT_ready.sem, 1)

                def first():
                    take_tokens(Batch(0, 0))
                    take_values(Batch(0, 0))
                    take_queries(Batch(0, 0))

                def heads(b, prior, after, after2):
                    exps(b, 0)
                    if after:
                        take_tokens(b + 1)
                    exps(b, 1)
                    take_probsT(b, 0)
                    if prior:
                        take_outputs(b + -1)
                    if after:
                        take_values(b + 1)
                    exps(b, 2)
                    take_probsT(b, 1)
                    exps(b, 3)
                    take_probsT(b, 2)
                    if after:
                        take_queries(b + 1)
                    take_probsT(b, 3)

                run(act, first, heads)
                take_outputs(Batch(0, B - 1))

            @block.vector
            def _(dve):
                dve.wait_ge(weights.sem, weights.at(16 * len(loads)))

                def normalised(b, n, dst, src):
                    dve.wait_ge(rstd_ready.sem, rstd_ready.at(2 * b.n + n))
                    return dve.tensor_scalar(dst, src, stats[:, 6:7], stats[:, 9:10], ALU.subtract, ALU.mult)

                def norm_1(b):
                    normalise_start(dve, stats, batch_row(core.x, b), var_ready)

                def norm_2(b):
                    y = batch_row(core.y, b)
                    normalised(b, 1, y, batch_row(core.x, b))
                    dve.drain()
                    normalise_start(dve, stats, y, var_ready)

                def norm_3(b):
                    normalised(b, 2, normed[:, :], batch_row(core.y, b)).then_inc(normed_ready.sem, 1)

                def rotate(b):
                    dve.wait_ge(qk_made.sem, qk_made.at(b.n + 1))
                    qk = psQK[0:T, 0:2 * D].rearrange("t (h e) -> t h e", e=16)

                    def all_heads(t, lo, hi):
                        return t[:, lo:hi].unsqueeze(1).broadcast_to([T, 2 * H, hi - lo])

                    dve.tensor_tensor(turned_by[:, :, 0:8], qk[:, :, 8:16], all_heads(sin, 0, 8), ALU.mult)
                    dve.tensor_tensor(turned_by[:, :, 8:16], qk[:, :, 0:8], all_heads(sin, 8, 16), ALU.mult)
                    dve.tensor_tensor(turned_q[:, :, :], qk, all_heads(cos, 0, 16), ALU.mult)
                    dve.drain()
                    dve.tensor_tensor(turned_q[:, :, :], turned_q[:, :, :], turned_by[:, :, :], ALU.add)\
                        .then_inc(rope_done.sem, 1)

                def spread_keys(b):
                    dve.wait_ge(r_made.sem, r_made.at(b.n + 1))
                    dve.wait_ge(q_ready.sem, q_ready.at(b.n + 1))
                    for c in range(DC):
                        ins = dve.tensor_tensor(keys[:, 8 * c:8 * c + 8, :],
                                                psR[:, (DC + c) * T:(DC + c + 1) * T].unsqueeze(1).broadcast_to([P, 8, T]),
                                                headmask[:, :].unsqueeze(2).broadcast_to([P, 8, T]), ALU.mult)
                    ins.then_inc(keys_ready.sem, 1)

                def group_max(b, g):
                    dve.wait_ge(scored.sem, scored.at(HG * b.n + (g + 1)))
                    dve.tensor_tensor(masked[g % 2][:, :, :], psS[g % 2][0:T, 0:G * T].rearrange("p (h t) -> p h t", t=T),
                                      causal[:, :].unsqueeze(1).broadcast_to([T, G, T]), ALU.add)
                    dve.drain()
                    dve.tensor_reduce(negmax[b.par][:, G * g:G * g + G], masked[g % 2][:, :, :], AX, ALU.max,
                                      negate=True).then_inc(maxed.sem, 1)

                def divide(b):
                    dve.wait_ge(pv_done.sem, pv_done.at(HG * b.n + HG))
                    dve.reciprocal(inverse[:, :], sums[b.par][:, :])
                    dve.drain()
                    dve.tensor_tensor(o[:, :].rearrange("t (h e) -> t h e", e=16),
                                      psO[0:T, 0:D].rearrange("t (h e) -> t h e", e=16),
                                      inverse[:, :].unsqueeze(2).broadcast_to([T, H, 16]), ALU.mult)\
                        .then_inc(o_ready.sem, 1)

                def add(b):
                    dve.wait_ge(made["Y"].sem, made["Y"].at(b.n + 1))
                    y, x = batch_row(core.y, b), batch_row(core.x, b)
                    dve.tensor_tensor(y, psR[0:T, 0:D], y, ALU.add).then_inc(taken["Y"].sem, 1)
                    dve.drain()
                    dve.tensor_tensor(x, x, y, ALU.add)

                def first():
                    for b in (Batch(0, 0), Batch(0, 1)):
                        norm_1(b)
                        norm_2(b)
                        if b.n == 1:
                            dve.wait_ge(made["L"].sem, made["L"].at(1))
                        norm_3(b)
                    rotate(Batch(0, 0))
                    spread_keys(Batch(0, 0))

                def heads(b, prior, after, after2):
                    group_max(b, 0)
                    if prior:
                        divide(b + -1)
                    group_max(b, 1)
                    if after:
                        rotate(b + 1)
                    group_max(b, 2)
                    if prior:
                        add(b + -1)
                    if after2:
                        norm_1(b + 2)
                    group_max(b, 3)
                    if after2:
                        norm_2(b + 2)
                    if after:
                        spread_keys(b + 1)
                    if after2:
                        norm_3(b + 2)

                run(dve, first, heads)
                divide(Batch(0, B - 1))
                add(Batch(0, B - 1))

        weights.stage_over(16 * len(loads))
        for s in (var_ready, rstd_ready):
            s.stage_over(2 * B)
        for s in (normed_ready, o_ready, qk_made, rope_done, r_made, keys_ready, q_ready, *made.values(), *taken.values()):
            s.stage_over(B)
        for s in (scored, maxed, exped, turned, probsT_ready, pv_done):
            s.stage_over(HG * B)


def decoder(nc, a, out):
    with ExitStack() as ctx:
        core = Core(nc, ctx)
        core.start_sem = ctx.enter_context(nc.semaphore("start_sem"))
        core.x = core.keep("x", [T, B, D])
        core.ident = core.keep("ident", [P, P])
        core.neg_half = core.keep("neg_half", [P, 1])
        core.ones = core.keep("ones", [P, P])
        core.h_all = core.keep("h_all", [T, B, D])
        core.gate = core.keep("gate", [T, 2, B])
        core.slot_in, core.slot_out = core.keep("slot_in", [T, 2, B], U32), core.keep("slot_out", [T, 2, B], U32)
        core.eid = core.keep("eid", [1, 32], I32)
        core.y = core.keep("y", [T, B, D])
        core.hT_all = core.keep("hT_all", [P, DC, B * T])
        core.comb = core.keep("comb", [T, B, 18])
        core.filled_sem = ctx.enter_context(nc.semaphore("filled_sem"))
        core.zeroed_sem = ctx.enter_context(nc.semaphore("zeroed_sem"))
        core.slots_in = nc.dram_tensor("slots_in", [4 * B * T, D], F32, kind="Internal").ap()
        core.slots_out = nc.dram_tensor("slots_out", [TILES["L0"] * TILE, D], F32, kind="Internal").ap()
        core.consts, core.tiles = a, TILES
        for n in SIGNALS:
            core.counter(n)
        load_start(nc, core, a["x"], a["ident"])
        known = set(core.counters)
        stages = STAGES(nc, core, a)
        for n, stage in enumerate(stages):
            if n < LAYERS:
                stage()
        store_end(nc, core, out)
        assert set(core.counters) == known, set(core.counters) - known


TILE = 256
CAPACITY = 2 * B * T // 8
TILES = {"L0": (2 * B * T - 8) // TILE + 8, "L1": 8, "L2": (B * T - 8) // TILE + 8}

BY_POOL_DMA = ["scattered"] + [f"gathered{r}" for r in range(8)]
SIGNALS = (["start_loaded", "stored", "weights", "ctx_here0", "ctx_here1", "var_ready", "rstd_ready", "normed_ready",
            "scored", "maxed", "exped", "turned", "probsT_ready", "pv_done", "o_ready", "setup_done", "cums",
            "kept_copy", "scattered", "w_here0", "w_here1", "y_stored0", "y_stored1"]
           + [f"{m}_{c}" for m in ("made", "taken") for c in "LQKVOYGH"] + [f"gathered{r}" for r in range(8)]
           + ["qkv_made", "rope_done"])


def STAGES(nc, core, a):
    l0 = {n: a["L0_" + n] for n in ("wq", "wk", "wv", "wo", "bq", "bk", "bv", "bo")}
    l2 = {n: a["L2_" + n] for n in ("wq", "wk", "wv", "wo")}
    l3 = {n: a["L3_" + n] for n in ("wq", "wk", "wv", "wo", "bq", "bk", "bv", "bo")}
    m = {n: a[n] for n in ("steps", "upto", "keys", "headmask")}
    f0 = {n: a["F0_" + n] for n in ("wg", "w1", "b1", "w2", "b2")}
    f1 = {n: a["F1_" + n] for n in ("wg", "w1", "b1", "w2", "b2", "g", "b")}
    f2 = {n: a["F2_" + n] for n in ("wg", "bg", "w1", "b1", "w2", "b2")}
    f3 = {"wg": a["F3_router"], "bg": a["F3_bg"]}
    d3 = {n: a["F3_" + n] for n in ("wg", "wu", "wd")}
    x1 = {n: a["X1_" + n] for n in ("wq", "wk", "wv", "bq", "bk", "bv", "maskT")}
    s1 = {n: a["S1_" + n] for n in ("g", "b", "wqkv", "wo", "cos", "sin", "causal")}
    s1["headmask"] = a["headmask"]
    return [
        lambda: cross_attention(nc, core, "L0", a["ctxT"], l0, 16, m),
        lambda: (route(nc, core, "L0", f0, 8, 2, "pair", TILE),
                 expert_tiles(nc, core, "L0t", f0, TILE, TILES["L0"], ACT.Relu, True),
                 combine(nc, core, "L0c", 2)),
        lambda: relu_attention(nc, core, "L1x", a["ctxT"], x1),
        lambda: (self_attention(nc, core, "L1s", s1),
                 route(nc, core, "L1", f1, 8, 2, "cap", CAPACITY),
                 expert_tiles(nc, core, "L1t", f1, CAPACITY, TILES["L1"], ACT.Gelu, False),
                 combine(nc, core, "L1c", 2)),
        lambda: cross_attention(nc, core, "L2", a["ctxT"], l2, 64),
        lambda: (route(nc, core, "L2", f2, 8, 1, "all", TILE),
                 expert_tiles(nc, core, "L2t", f2, TILE, TILES["L2"], ACT.Relu, True),
                 combine(nc, core, "L2c", 1)),
        lambda: cross_attention(nc, core, "L3", a["ctxT"], l3, 64),
        lambda: (route(nc, core, "L3", f3, 16, 2, "dense", None),
                 dense_experts(nc, core, "L3d", d3, 18)),
    ]


def lay_out(inputs):
    import numpy as np

    def rows(w):
        w = np.asarray(w)
        return np.ascontiguousarray(w.reshape(w.shape[0] // P, P, w.shape[1]).transpose(1, 0, 2))

    def cols(v):
        return np.ascontiguousarray(np.asarray(v).reshape(-1, P).T)

    def row(v):
        return np.ascontiguousarray(np.asarray(v).reshape(1, -1))

    i = {k: np.asarray(v) for k, v in inputs.items()}
    a = {"x": np.ascontiguousarray(i["x"]), "ident": np.eye(P, dtype=np.float32)}
    a["ctxT"] = np.ascontiguousarray(i["ctx_1024"].reshape(B, S, DC, P).transpose(0, 3, 2, 1))
    a["steps"] = np.ascontiguousarray(i["mask_BxS_ik0"].T)
    a["upto"] = np.triu(np.ones((T, T), np.float32))
    a["keys"] = np.arange(S, dtype=np.float32)
    a["headmask"] = np.where(np.arange(P)[:, None] // 16 == np.arange(8)[None, :], 0.25, 0.0).astype(np.float32)
    for n in ("wq", "wk", "wv", "wo"):
        a["L0_" + n] = rows(i["L0_xattn_" + n].T)
    for n in ("bq", "bk", "bv"):
        a["L0_" + n] = cols(i["L0_xattn_" + n])
    a["L0_bo"] = row(i["L0_xattn_bo"])
    for n in ("wq", "wk", "wv", "wo"):
        a["L2_" + n] = rows(i["L2_xattn_W" + n[1]])
    for n, m in (("q", "Query"), ("k", "Key"), ("v", "Value"), ("o", "Output")):
        a["L3_w" + n] = rows(i["L3_xattn_W_" + m])
        a["L3_b" + n] = (row if n == "o" else cols)(i["L3_xattn_B_" + m])

    def experts(w):
        w = np.asarray(w)
        return np.ascontiguousarray(w.reshape(w.shape[0], w.shape[1] // P, P, w.shape[2]).transpose(0, 2, 1, 3))

    for f, l, g in (("F0", "L0", "Wg"), ("F1", "L1", "Wgate"), ("F2", "L2", "w_gate")):
        l += "_ffn_"
        a[f + "_wg"] = rows(i[l + g])
        a[f + "_w1"], a[f + "_w2"] = experts(i[l + "W1"]), experts(i[l + "W2"])
        a[f + "_b1"] = np.ascontiguousarray(i[l + "b1"].reshape(8, -1, P).transpose(0, 2, 1))
        a[f + "_b2"] = np.ascontiguousarray(i[l + "b2"])
    a["F1_g"], a["F1_b"] = i["L1_ffn_ln2_g"], i["L1_ffn_ln2_b"]
    a["F2_bg"] = i["L2_ffn_b_gate"]
    a["F3_router"], a["F3_bg"] = rows(i["L3_ffn_router_w"].T), i["L3_ffn_router_bias"]
    for n, e, sh in (("wg", "gate_proj", "sh_gate"), ("wu", "up_proj", "sh_up")):
        shared = i["L3_ffn_" + sh].reshape(2, P, D).transpose(0, 2, 1)
        a["F3_" + n] = experts(np.concatenate([i["L3_ffn_" + e], shared]))
    a["F3_wd"] = np.ascontiguousarray(np.concatenate([i["L3_ffn_down_proj"], i["L3_ffn_sh_down"].T.reshape(2, P, D)]))
    for n in "qkv":
        a["X1_w" + n] = rows(i["L1_xattn_kernel_" + n][0, 0])
        a["X1_b" + n] = (row if n == "v" else cols)(i["L1_xattn_bias_" + n])
    a["X1_maskT"] = np.ascontiguousarray(i["mask_1xSxS2_ff0"][0].T.reshape(J, SJ, T).transpose(1, 0, 2))
    a["S1_g"], a["S1_b"] = cols(i["L1_ffn_ln1_g"]), cols(i["L1_ffn_ln1_b"])
    wqkv = i["L1_ffn_Wqkv"].reshape(D, H, 3, 16).transpose(0, 2, 1, 3).reshape(D, 3 * D)
    a["S1_wqkv"], a["S1_wo"] = rows(wqkv), rows(i["L1_ffn_Wproj"])
    angle = np.arange(T, dtype=np.float32)[:, None] * (np.float32(1) / np.float32(10000) ** (np.arange(0, 16, 2, dtype=np.float32) / np.float32(16)))
    cos, sin = np.cos(angle.astype(np.float64)), np.sin(angle.astype(np.float64))
    a["S1_cos"] = np.concatenate([cos, cos], 1).astype(np.float32)
    a["S1_sin"] = np.concatenate([-sin, sin], 1).astype(np.float32)
    a["S1_causal"] = np.where(np.arange(T)[:, None] >= np.arange(T)[None, :], 0.0, NEG).astype(np.float32)
    a["at_expert8"] = np.arange(8, dtype=np.float32) - 64
    a["at_expert16"] = np.arange(16, dtype=np.float32) - 64
    a["keepgoing"] = np.tile((np.arange(B) > 0).astype(np.float32), (8, 1))
    a["spare"] = (2 * B * T + np.arange(2 * B * T, dtype=np.float32)).reshape(T, 2, B)
    a["cap_starts"] = np.arange(8, dtype=np.float32) * CAPACITY
    for n in ("L0", "L2"):
        a["steps_" + n] = np.tile(np.arange(-(-B * T // TILE), dtype=np.float32) * TILE, (8, 1))
        a["tiles_" + n] = np.repeat(np.arange(TILES[n], dtype=np.float32)[:, None], 8, 1)
    return a


def kernel(**inputs):
    import numpy as _np
    import concourse.bacc as _bacc
    from concourse import mybir as _mybir
    from concourse.bass_utils import run_bass_kernel_spmd as _run

    nc = _bacc.Bacc("TRN2", target_bir_lowering=False, num_devices=1)
    arrays = {f"in_{k}": v for k, v in lay_out(inputs).items()}
    a = {k[3:]: nc.dram_tensor(k, v.shape, _mybir.dt.from_np(v.dtype), kind="ExternalInput").ap()
         for k, v in arrays.items()}
    out = nc.dram_tensor("out_0", (B, T, D), F32, kind="ExternalOutput").ap()
    decoder(nc, a, out)
    r = _run(nc, [arrays], core_ids=[0])
    return r.results[0]["out_0"]
```

```python
from contextlib import ExitStack

import concourse.bass as bass
from concourse import mybir

F32 = mybir.dt.float32
I32 = mybir.dt.int32
U32 = mybir.dt.uint32
BF16 = mybir.dt.bfloat16
F32R = mybir.dt.float32r
ALU = mybir.AluOpType
ACT = mybir.ActivationFunctionType
AX = mybir.AxisListType.X

B, T, D = 16, 112, 256
S, SJ, J = 375, 125, 3
SP = 376
P = 128
DC = D // P
H = 16
HALF = 512
CREDIT = 64
NEG = -1e30
LAYERS = 99


class Counter:

    def __init__(self, sem, start):
        self.sem, self.start = sem, start

    def at(self, n):
        return n + self.start

    def stage_over(self, n):
        self.start += n


class Batch:

    def __init__(self, i, k):
        self.n = 2 * i + k
        self.half = i + k // 2
        self.par = k % 2
        self.i, self.k = i, k

    def __add__(self, d):
        return Batch(self.i, self.k + d)


def before(b, h, d):
    return (b, h - d) if h >= d else (b + -1, h - d + H)


class Core:

    def __init__(self, nc, ctx):
        self.nc, self.ctx, self.counters = nc, ctx, {}
        self.held, self.times_held = {}, 0
        self.bank = [ctx.enter_context(nc.psum_tensor(f"bank{i}", [P, HALF], F32)) for i in range(8)]

    def keep(self, name, shape, dt=F32):
        return self.ctx.enter_context(self.nc.sbuf_tensor(name, shape, dt))

    def counter(self, name):
        if name not in self.counters:
            start = 0 if name in BY_POOL_DMA else CREDIT
            self.counters[name] = Counter(self.ctx.enter_context(self.nc.semaphore(name)), start)
        return self.counters[name]


def load_start(nc, core, x_in, ident_in):
    loaded = core.counter("start_loaded")
    with nc.Block() as block:

        @block.gpsimd
        def _(pool):
            for s in core.counters.values():
                if s.start:
                    pool.sem_inc(s.sem, s.start)
            pool.memset(core.neg_half[:, :], -0.5)
            pool.memset(core.ones[:, :], 1.0)
            pool.memset(core.held["zeros"][:, :, :], 0.0).then_inc(core.filled_sem, 1)

        @block.sync
        def _(sp):
            sp.dma_start(core.ident[:, :], ident_in).then_inc(core.start_sem, 16)
            sp.dma_start(core.x[:, :, :], x_in.rearrange("b t d -> t b d")).then_inc(core.start_sem, 16)
            sp.wait_ge(core.filled_sem, 1)
            for r in range(core.slots_in.shape[0] // (B * T)):
                sp.dma_start(core.slots_in[r * B * T:(r + 1) * B * T, :].rearrange("(t b) d -> t b d", b=B),
                             core.held["zeros"][:, :, :]).then_inc(core.zeroed_sem, 16)
            sp.wait_ge(core.start_sem, 32)

        @block.vector
        def _(dve):
            dve.wait_ge(core.start_sem, 32)
            dve.tensor_copy(core.ident_b[:, :], core.ident[:, :])


def store_end(nc, core, out):
    stored = core.counter("stored")
    with nc.Block() as block:

        @block.sync
        def _(sp):
            sp.dma_start(out.rearrange("b t d -> t b d"), core.x[:, :, :]).then_inc(stored.sem, 16)
            sp.wait_ge(stored.sem, stored.at(16))


def cross_attention(nc, core, name, ctx_in, w, dh, mask=None):
    E = H * dh
    EC = E // P
    NQ = -(-EC // 4)
    VW = min(E, HALF)
    NV = J * E // VW
    NOT = -(-EC // 4)
    NY = 2 if EC > 2 else 1
    YW = D // NY
    G = min(H, HALF // dh)
    NG = H // G
    scale = float(dh) ** -0.5
    biased = "bk" in w
    wide = EC > 2
    if wide:
        order = {0: ["V0"], 1: ["V1"], 2: ["V2"], 3: ["K0"], 4: ["O0", "K1"], 5: ["O1", "K2"], 6: ["Y0"],
                 7: ["L0", "L1", "K3"], 8: ["Y1"], 9: ["V3"], 10: ["Q0"], 11: ["K4", "K5"], 12: ["Q1"],
                 13: ["K6", "K7"], 14: ["V4"], 15: ["V5"]}
    else:
        order = {0: ["K0"], 2: ["K1"], 5: ["O0"], 7: ["Y0", "L0", "L1"], 9: ["Q0"], 10: ["V0"],
                 12: ["V1"], 14: ["V2"]}
    first_pieces = ["L0", "L1", "Q0", "Q1", "K0", "K1", "K2", "K3", "K4", "K5", "K6", "K7",
                    "V0", "V1", "V2", "V3", "V4", "V5"]
    every = [p for ps in order.values() for p in ps]
    first_pieces = [p for p in first_pieces if p in every]
    per_batch = {"L": 2, "Q": NQ, "K": EC, "V": NV, "O": NOT, "Y": NY}

    ctx = ExitStack()
    with ctx:
        def sb(n, shape, dt=F32):
            return ctx.enter_context(nc.sbuf_tensor(f"{name}_{n}", shape, dt))

        if wide:
            wq, wo, v = core.held["wq"], core.held["wo"], (core.held["v0"], core.held["v1"])
            wk, wv = v[0][:, 0:DC, :], v[1][:, 0:DC, :]
            wk_hi, wk_lo, wv_hi, wv_lo = (sb(n, [P, DC, E], F32R) for n in ("wk_hi", "wk_lo", "wv_hi", "wv_lo"))
            ctxT = sb("ctxT", [P, DC, SP])
            ctx_hi = [sb(f"ctx_hi{i}", [P, DC, SP], F32R) for i in range(2)]
            ctx_lo = [sb(f"ctx_lo{i}", [P, DC, SP], F32R) for i in range(2)]
            keys_hl = [sb(f"keys_hl{i}", [P, H, SP], F32R) for i in range(2)]
            q_hh = [sb(f"q_hh{i}", [P, H, T], F32R) for i in range(2)]
            q_lo = [sb(f"q_lo{i}", [P, EC, T], F32R) for i in range(2)]
            q = sb("q", [P, 4, T])
            w_split = core.counter("w_split")
            ctx_split = core.counter("ctx_split")
            k_high = core.counter("k_high")
            q_split = core.counter("q_split")
        else:
            wq, wk, wv = (sb(n, [P, DC, E]) for n in ("wq", "wk", "wv"))
            wo = sb("wo", [P, EC, D])
            v = [sb(f"v{i}", [P, J, E]) for i in range(2)]
            ctxT = [sb(f"ctxT{i}", [P, DC, S]) for i in range(2)]
            q = [sb(f"q{i}", [P, H, T]) for i in range(2)]
            kT = [sb(f"kT{i}", [P, EC, S]) for i in range(2)]
        stats = sb("stats", [T, 16])
        normed = sb("normed", [T, D])
        hT = sb("hT", [P, DC, T])
        probs = [sb(f"probs{i}", [T, S]) for i in range(2)]
        probsT = [sb(f"probsT{i}", [SJ, J, T]) for i in range(2)]
        negmax = [sb(f"negmax{i}", [T, H]) for i in range(2)]
        sums = [sb(f"sums{i}", [T, H]) for i in range(2)]
        inverse = sb("inverse", [T, H])
        o = sb("o", [T, E])
        oT = sb("oT", [P, EC, T])
        if biased:
            bq, bk, bv = (sb(n, [P, EC]) for n in ("bq", "bk", "bv"))
            bo = sb("bo", [1, D])
        if mask:
            steps = sb("steps", [T, B], I32)
            stepsf = sb("stepsf", [T, B])
            upto = sb("upto", [T, T])
            last_key = sb("last_key", [T, B])
            keys = sb("keys", [T, S])
            headmask = sb("headmask", [P, P // dh])
            barred = [sb(f"barred{i}", [T, S], BF16) for i in range(2)]
            barred_ready = core.counter("barred_ready")
        weights = core.counter("weights")
        ctx_here = [core.counter(f"ctx_here{i}") for i in range(2)]
        var_ready = core.counter("var_ready")
        rstd_ready = core.counter("rstd_ready")
        normed_ready = core.counter("normed_ready")
        scored = core.counter("scored")
        maxed = core.counter("maxed")
        exped = core.counter("exped")
        turned = core.counter("turned")
        probsT_ready = core.counter("probsT_ready")
        pv_done = core.counter("pv_done")
        o_ready = core.counter("o_ready")
        setup_done = core.counter("setup_done")
        cums = core.counter("cums")
        made = {c: core.counter(f"made_{c}") for c in "LQKVOY"}
        taken = {c: core.counter(f"taken_{c}") for c in "LQKVOY"}
        nweights = 4 + (4 if biased else 0) + (4 if mask else 0)
        psS, psT, psO, ring = core.bank[0:2], core.bank[2:4], core.bank[4:6], core.bank[6:8]

        def count(piece, b):
            n = per_batch[piece[0]]
            return b.n * n + (int(piece[1]) + 1)

        def pieces_at(h, b_first, b_last):
            for p in order.get(h, []):
                if p[0] in "OY":
                    if not b_first:
                        yield p, -1
                elif not b_last:
                    yield p, 1

        def slots(b_first):
            before_ = [("V%d" % (NV - 2), 0), ("V%d" % (NV - 1), 0)]
            if NV == 1:
                raise ValueError
            out, n = {}, 0
            for h in range(H):
                for p, d in pieces_at(h, b_first, False):
                    out[p] = (n % 2, before_[n % 2])
                    before_[n % 2] = (p, d)
                    n += 1
            assert n % 2 == 0
            return out

        def first_slots():
            out, before_ = {}, [None, None]
            for n, p in enumerate(first_pieces):
                out[p] = (n % 2, before_[n % 2])
                before_[n % 2] = (p, 0)
            assert len(first_pieces) % 2 == 0
            return out

        def last_slots():
            tail = [p for p in every if p[0] in "OY"]
            lasts = [p for p in every if p[0] in "OY"]
            before_ = [(lasts[-2], -1), (lasts[-1], -1)]
            out = {}
            for n, p in enumerate(tail):
                out[p] = (n % 2, before_[n % 2])
                before_[n % 2] = (p, 0)
            return out

        def run(heads, first, last, tail, engine):
            first(Batch(0, 0))
            heads(Batch(0, 0), True, False)
            with engine.Fori(0, (B - 4) // 2) as i:
                heads(Batch(i, 1), False, False)
                heads(Batch(i, 2), False, False)
            heads(Batch(0, B - 3), False, False)
            heads(Batch(0, B - 2), False, False, False)
            heads(Batch(0, B - 1), False, True, False)
            tail(Batch(0, B - 1))

        with nc.Block() as block:

            @block.sync
            def _(sp):
                if not wide:
                    for dst, src in ((wq, w["wq"]), (wk, w["wk"]), (wv, w["wv"]), (wo, w["wo"])):
                        sp.dma_start(dst[:, :, :], src).then_inc(weights.sem, 16)
                if biased:
                    for dst, src in ((bq, w["bq"]), (bk, w["bk"]), (bv, w["bv"]), (bo, w["bo"])):
                        sp.dma_start(dst[:, :], src).then_inc(weights.sem, 16)
                if mask:
                    sp.dma_start(steps[:, :], mask["steps"]).then_inc(weights.sem, 16)
                    sp.dma_start(upto[:, :], mask["upto"]).then_inc(weights.sem, 16)
                    sp.dma_start(keys[:, :], mask["keys"].partition_broadcast(T)).then_inc(weights.sem, 16)
                    sp.dma_start(headmask[:, :], mask["headmask"]).then_inc(weights.sem, 16)

                def load(b):
                    sp.dma_start(ctxT[b.par][:, :, :], ctx_in[bass.ds(b.n, 1)].rearrange("a p c s -> p (a c) s"))\
                        .then_inc(ctx_here[b.par].sem, 16)

                if wide:
                    def load_wide(b):
                        sp.dma_start(ctxT[:, :, 0:S], ctx_in[bass.ds(b.n, 1)].rearrange("a p c s -> p (a c) s"))\
                            .then_inc(ctx_here[0].sem, 16)

                    load_wide(Batch(0, 0))
                    with sp.Fori(0, B - 1) as i:
                        sp.wait_ge(ctx_split.sem, ctx_split.at(i + 1))
                        sp.dma_start(ctxT[:, :, 0:S], ctx_in[bass.ds(i + 1, 1)].rearrange("a p c s -> p (a c) s"))\
                            .then_inc(ctx_here[0].sem, 16)
                    return
                load(Batch(0, 0))
                load(Batch(0, 1))
                with sp.Fori(0, (B - 2) // 2) as i:
                    for k in (2, 3):
                        b = Batch(i, k)
                        sp.wait_ge(made["V"].sem, made["V"].at(count("V%d" % (NV - 1), b + -2)))
                        load(b)
                sp.wait_ge(core.zeroed_sem, 16 * (core.slots_in.shape[0] // (B * T)))

            @block.tensor
            def _(pe):
                def piece(p, b, slot):
                    at, prior = slot
                    if prior:
                        kind = prior[0]
                        pe.wait_ge(taken[kind[0]].sem, taken[kind[0]].at(count(kind, prior[1])))
                    bank, m = ring[at], int(p[1])
                    if p[0] == "L":
                        pe.wait_ge(normed_ready.sem, normed_ready.at(b.n + 1))
                        ins = pe.transpose(bank[:, 0:T], normed[:, m * P:(m + 1) * P], core.ident[0:T, 0:T])
                    elif p[0] == "Q":
                        pe.wait_ge(taken["L"].sem, taken["L"].at(count("L1", b)))
                        cs = range(4 * m, min(4 * m + 4, EC))
                        for c in cs:
                            for k in range(DC):
                                ins = pe.matmul(bank[:, (c - 4 * m) * T:(c - 4 * m + 1) * T],
                                                wq[:, k, c * P:(c + 1) * P], hT[:, k, :],
                                                start=(k == 0), stop=(k == DC - 1))
                    elif p[0] == "K" and wide:
                        pe.wait_ge(ctx_split.sem, ctx_split.at(b.n + 1))
                        for n, (wt, c) in enumerate(((wk_hi, ctx_hi), (wk_hi, ctx_lo), (wk_lo, ctx_hi))):
                            for k in range(DC):
                                ins = pe.matmul(bank[:, 0:SP], wt[:, k, m * P:(m + 1) * P], c[b.par][:, k, :],
                                                start=(n + k == 0), stop=(n + k == DC + 1))
                    elif p[0] == "V" and wide:
                        pe.wait_ge(ctx_split.sem, ctx_split.at(b.n + 1))
                        j, vn = m // (E // VW), m % (E // VW)
                        for n, (wt, c) in enumerate(((wv_hi, ctx_hi), (wv_lo, ctx_hi), (wv_hi, ctx_lo))):
                            for k in range(DC):
                                ins = pe.matmul(bank[0:SJ, 0:VW], c[b.par][:, k, j * SJ:(j + 1) * SJ],
                                                wt[:, k, vn * VW:(vn + 1) * VW],
                                                start=(n + k == 0), stop=(n + k == DC + 1))
                    elif p[0] == "K":
                        pe.wait_ge(ctx_here[b.par].sem, ctx_here[b.par].at(16 * b.half + 16))
                        for k in range(DC):
                            ins = pe.matmul(bank[:, 0:S], wk[:, k, m * P:(m + 1) * P], ctxT[b.par][:, k, :],
                                            start=(k == 0), stop=(k == DC - 1))
                    elif p[0] == "V":
                        pe.wait_ge(ctx_here[b.par].sem, ctx_here[b.par].at(16 * b.half + 16))
                        j, n = m // (E // VW), m % (E // VW)
                        for k in range(DC):
                            ins = pe.matmul(bank[0:SJ, 0:VW], ctxT[b.par][:, k, j * SJ:(j + 1) * SJ],
                                            wv[:, k, n * VW:(n + 1) * VW], start=(k == 0), stop=(k == DC - 1))
                    elif p[0] == "O":
                        pe.wait_ge(o_ready.sem, o_ready.at(NG * b.n + NG))
                        cs = range(4 * m, min(4 * m + 4, EC))
                        for c in cs:
                            ins = pe.transpose(bank[:, (c - 4 * m) * T:(c - 4 * m + 1) * T],
                                               o[:, c * P:(c + 1) * P], core.ident[0:T, 0:T])
                    else:
                        pe.wait_ge(taken["O"].sem, taken["O"].at(count("O%d" % (NOT - 1), b)))
                        for c in range(EC):
                            ins = pe.matmul(bank[0:T, 0:YW], oT[:, c, :], wo[:, c, m * YW:(m + 1) * YW],
                                            start=(c == 0), stop=(c == EC - 1 and not biased))
                        if biased:
                            ins = pe.matmul(bank[0:T, 0:YW], core.ones[0:1, 0:T], bo[0:1, m * YW:(m + 1) * YW],
                                            start=False, stop=True)
                    ins.then_inc(made[p[0]].sem, 1)

                def scores(b, h):
                    if wide:
                        at, c = h * dh % P, h * dh // P
                        if c % 4 == 0 and at == 0:
                            pe.wait_ge(q_split.sem, q_split.at(NQ * b.n + (c // 4 + 1)))
                        if at == 0:
                            pe.wait_ge(taken["K"].sem, taken["K"].at(EC * b.n + (c + 1)))
                        pe.matmul(psS[h % 2][0:T, 0:SP], q_hh[b.par][:, h, :], keys_hl[b.par][:, h, :],
                                  start=True, stop=False)
                        pe.matmul(psS[h % 2][0:T, 0:SP], q_lo[b.par][at:at + dh, c, :],
                                  keys_hl[b.par][at:at + dh, h, :], start=False, stop=True).then_inc(scored.sem, 1)
                        return
                    if h == 0:
                        pe.wait_ge(taken["Q"].sem, taken["Q"].at(NQ * b.n + NQ))
                        pe.wait_ge(taken["K"].sem, taken["K"].at(EC * b.n + EC))
                        pe.wait_ge(barred_ready.sem, barred_ready.at(b.n + 1))
                    pe.matmul(psS[h % 2][0:T, 0:S], core.ident_b[0:T, 0:T], barred[b.par][:, :],
                              start=True, stop=False)
                    pe.matmul(psS[h % 2][0:T, 0:S], q[b.par][:, h, :], kT[b.par][:, h * dh // P, :],
                              start=False, stop=True).then_inc(scored.sem, 1)

                def turn(b, h):
                    pe.wait_ge(exped.sem, exped.at(H * b.n + h + 1))
                    for j in range(J):
                        ins = pe.transpose(psT[h % 2][0:SJ, j * T:(j + 1) * T],
                                           probs[h % 2][:, j * SJ:(j + 1) * SJ], core.ident[0:T, 0:T])
                    ins.then_inc(turned.sem, 1)

                def values(b, h):
                    pe.wait_ge(probsT_ready.sem, probsT_ready.at(H * b.n + h + 1))
                    if h == 0:
                        pe.wait_ge(taken["V"].sem, taken["V"].at(NV * b.n + NV))
                    if h % G == 0:
                        pe.wait_ge(o_ready.sem, o_ready.at(NG * b.n + h // G - 1))
                    bank = psO[(b.par * NG + h // G) % 2]
                    for j in range(J):
                        ins = pe.matmul(bank[0:T, h % G * dh:(h % G + 1) * dh], probsT[h % 2][:, j, :],
                                        v[b.par][0:SJ, j, h * dh:(h + 1) * dh], start=(j == 0), stop=(j == J - 1))
                    ins.then_inc(pv_done.sem, 1)

                def heads(b, b_first, b_last, split_next=True):
                    where = slots(b_first)
                    for h in range(H):
                        scores(b, h)
                        if not (b_first and h < 1):
                            turn(*before(b, h, 1))
                        if not (b_first and h < 2):
                            values(*before(b, h, 2))
                        for p, d in pieces_at(h, b_first, b_last):
                            at, (prior, pd) = where[p] if not b_last else last_where[p]
                            piece(p, b + d, (at, (prior, b + pd)))

                def first(b):
                    where = first_slots()
                    for p in first_pieces:
                        if wide and p in ("K0", "V0"):
                            pe.wait_ge(w_split.sem, w_split.at("KV".index(p[0]) + 1))
                        at, prior = where[p]
                        piece(p, b, (at, prior and (prior[0], b)))

                def tail(b):
                    turn(b, H - 1)
                    values(b, H - 2)
                    values(b, H - 1)
                    where = last_slots()
                    for p in [p for p in every if p[0] in "OY"]:
                        at, (prior, d) = where[p]
                        piece(p, b, (at, (prior, b + d)))

                last_where, prior_ = {}, [("V%d" % (NV - 2), 0), ("V%d" % (NV - 1), 0)]
                for n, p in enumerate([p for p in every if p[0] in "OY"]):
                    last_where[p] = (n % 2, prior_[n % 2])
                    prior_[n % 2] = (p, -1)

                pe.wait_ge(weights.sem, weights.at(16 * nweights))
                if mask:
                    pe.wait_ge(setup_done.sem, setup_done.at(1))
                    pe.matmul(psS[0][0:T, 0:B], upto[:, :], stepsf[:, :], start=True, stop=True)\
                        .then_inc(cums.sem, 1)
                    pe.wait_ge(setup_done.sem, setup_done.at(2))
                run(heads, first, lambda *_: None, tail, pe)

            @block.scalar
            def _(act):
                act.preload_act_table(ACT.Exp)
                act.wait_ge(weights.sem, weights.at(16 * nweights))

                def take(p, b, at):
                    bank, m = ring[at], int(p[1])
                    if p[0] in "YQ":
                        return
                    act.wait_ge(made[p[0]].sem, made[p[0]].at(count(p, b)))
                    if p[0] == "L":
                        ins = act.activation(hT[:, m, :], bank[:, 0:T], ACT.Copy)
                    elif p[0] == "K" and wide:
                        for i in range(2):
                            rows = slice(i * dh, (i + 1) * dh)
                            ins = act.activation(keys_hl[b.par][rows, 2 * m + i, :], bank[rows, 0:SP], ACT.Identity,
                                                 bias=bk[rows, m:m + 1] if biased else 0.0)
                        ins.then_inc(k_high.sem, 1)
                        return
                    elif p[0] == "K":
                        if biased:
                            ins = act.activation(kT[b.par][:, m, :], bank[:, 0:S], ACT.Identity, bias=bk[:, m:m + 1])
                        else:
                            ins = act.activation(kT[b.par][:, m, :], bank[:, 0:S], ACT.Copy)
                    elif p[0] == "V":
                        j, n = m // (E // VW), m % (E // VW)
                        ins = act.activation(v[b.par][0:SJ, j, n * VW:(n + 1) * VW], bank[0:SJ, 0:VW], ACT.Copy)
                    else:
                        cs = range(4 * m, min(4 * m + 4, EC))
                        if biased:
                            for c in cs:
                                ins = act.activation(oT[:, c, :], bank[:, (c - 4 * m) * T:(c - 4 * m + 1) * T],
                                                     ACT.Identity, bias=bv[:, c:c + 1])
                        else:
                            ins = act.activation(oT[:, cs[0]:cs[-1] + 1, :],
                                                 bank[:, 0:len(cs) * T].rearrange("p (c t) -> p c t", t=T), ACT.Copy)
                    ins.then_inc(taken[p[0]].sem, 1)

                def heads(b, b_first, b_last, split_next=True):
                    where = slots(b_first)
                    tails = [p for p in every if p[0] in "OY"]
                    for h in range(H):
                        act.wait_ge(maxed.sem, maxed.at(H * b.n + h + 1))
                        act.activation(probs[h % 2][:, :], psS[h % 2][0:T, 0:S],
                                       ACT.Exp, bias=negmax[b.par][:, h:h + 1],
                                       accum_out=sums[b.par][:, h:h + 1]).then_inc(exped.sem, 1)
                        for p, d in pieces_at(h, b_first, b_last):
                            take(p, b + d, where[p][0] if not b_last else tails.index(p) % 2)

                def first(b):
                    where = first_slots()
                    for p in first_pieces:
                        take(p, b, where[p][0])

                def tail(b):
                    where = last_slots()
                    for p in [p for p in every if p[0] in "OY"]:
                        take(p, b, where[p][0])

                run(heads, first, None, tail, act)

            @block.gpsimd
            def _(pool):
                def rstd(b):
                    pool.wait_ge(var_ready.sem, var_ready.at(b.n + 1))
                    pool.tensor_tensor(stats[:, 9:10], stats[:, 8:9], core.neg_half[0:T, :], ALU.pow)\
                        .then_inc(rstd_ready.sem, 1)

                rstd(Batch(0, 0))
                with pool.Fori(0, B - 1) as i:
                    pool.wait_ge(var_ready.sem, var_ready.at(i + 2))
                    pool.tensor_tensor(stats[:, 9:10], stats[:, 8:9], core.neg_half[0:T, :], ALU.pow)\
                        .then_inc(rstd_ready.sem, 1)

            @block.vector
            def _(dve):
                def x_of(b):
                    return core.x[:, bass.ds(b.n, 1), :].rearrange("t a d -> t (a d)")

                def normalise_start(b):
                    dve.bn_stats(stats[:, 0:6], x_of(b))
                    dve.drain()
                    dve.bn_aggr(stats[:, 6:8], stats[:, 0:6])
                    dve.drain()
                    dve.tensor_scalar(stats[:, 8:9], stats[:, 7:8], 1e-5, None, ALU.add).then_inc(var_ready.sem, 1)

                def normalise_end(b):
                    dve.wait_ge(rstd_ready.sem, rstd_ready.at(b.n + 1))
                    dve.tensor_scalar(normed[:, :], x_of(b), stats[:, 6:7], stats[:, 9:10], ALU.subtract, ALU.mult)\
                        .then_inc(normed_ready.sem, 1)

                def bar(b):
                    dve.tensor_scalar(barred[b.par][:, :], keys[:, :], last_key[:, bass.ds(b.n, 1)], NEG,
                                      ALU.is_gt, ALU.mult).then_inc(barred_ready.sem, 1)

                def take(p, b, at):
                    bank, m = ring[at], int(p[1])
                    if p[0] not in ("YQK" if wide else "YQ"):
                        return
                    if p[0] == "K":
                        dve.wait_ge(k_high.sem, k_high.at(count(p, b)))
                        for i in range(2):
                            rows, other = slice(i * dh, (i + 1) * dh), slice((1 - i) * dh, (2 - i) * dh)
                            ins = dve.scalar_tensor_tensor(
                                out=keys_hl[b.par][other, 2 * m + i, :], in0=bank[rows, 0:SP],
                                scalar=bk[rows, m:m + 1] if biased else 0.0,
                                in1=keys_hl[b.par][rows, 2 * m + i, :].bitcast(F32), op0=ALU.add, op1=ALU.subtract)
                        ins.then_inc(taken["K"].sem, 1)
                        return
                    dve.wait_ge(made[p[0]].sem, made[p[0]].at(count(p, b)))
                    if p[0] == "Y":
                        xb = core.x[:, bass.ds(b.n, 1), m * YW:(m + 1) * YW].rearrange("t a d -> t (a d)")
                        ins = dve.tensor_tensor(xb, bank[0:T, 0:YW], xb, ALU.add)
                    elif EC > 2:
                        cs = range(4 * m, min(4 * m + 4, EC))
                        src = bank[:, 0:len(cs) * T].rearrange("p (c t) -> p c t", t=T)
                        dst = q[:, :, :]
                        if biased:
                            ins = dve.scalar_tensor_tensor(
                                out=dst, in0=src, scalar=scale,
                                in1=bq[:, cs[0]:cs[-1] + 1].unsqueeze(2).broadcast_to([P, len(cs), T]),
                                op0=ALU.mult, op1=ALU.add)
                        else:
                            ins = dve.tensor_scalar(dst, src, scale, None, ALU.mult)
                    else:
                        HC = P // dh
                        for c in range(EC):
                            ins = dve.scalar_tensor_tensor(
                                out=q[b.par][:, c * HC:(c + 1) * HC, :],
                                in0=bank[:, c * T:(c + 1) * T].unsqueeze(1).broadcast_to([P, HC, T]),
                                scalar=bq[:, c:c + 1], in1=headmask[:, :].unsqueeze(2).broadcast_to([P, HC, T]),
                                op0=ALU.add, op1=ALU.mult)
                    ins.then_inc(taken[p[0]].sem, 1)

                def split_ctx(b):
                    dve.wait_ge(ctx_here[0].sem, ctx_here[0].at(16 * b.n + 16))
                    dve.tensor_copy(ctx_hi[b.par][:, :, :], ctxT[:, :, :])
                    dve.drain()
                    dve.tensor_tensor(ctx_lo[b.par][:, :, :], ctxT[:, :, :], ctx_hi[b.par][:, :, :].bitcast(F32),
                                      ALU.subtract).then_inc(ctx_split.sem, 1)

                def high_queries(b, m):
                    dve.drain()
                    for i in range(2):
                        rows, other = slice(i * dh, (i + 1) * dh), slice((1 - i) * dh, (2 - i) * dh)
                        for to in (rows, other):
                            dve.tensor_copy(q_hh[b.par][to, 8 * m + i:8 * m + 8:2, :],
                                            q[rows, :, :])

                def low_queries(b, m):
                    dve.drain()
                    for i in range(2):
                        rows = slice(i * dh, (i + 1) * dh)
                        ins = dve.tensor_tensor(q_lo[b.par][rows, 4 * m:4 * m + 4, :], q[rows, :, :],
                                                q_hh[b.par][rows, 8 * m + i:8 * m + 8:2, :].bitcast(F32), ALU.subtract)
                    ins.then_inc(q_split.sem, 1)

                def head_max(b, h):
                    dve.wait_ge(scored.sem, scored.at(H * b.n + h + 1))
                    dve.tensor_reduce(negmax[b.par][:, h:h + 1], psS[h % 2][0:T, 0:S], AX, ALU.max,
                                      negate=True).then_inc(maxed.sem, 1)

                def take_probsT(b, h):
                    dve.wait_ge(turned.sem, turned.at(H * b.n + h + 1))
                    dve.tensor_copy(probsT[h % 2][:, :, :],
                                    psT[h % 2][0:SJ, 0:J * T].rearrange("p (j t) -> p j t", t=T))\
                        .then_inc(probsT_ready.sem, 1)

                def divide(b, g):
                    dve.wait_ge(pv_done.sem, pv_done.at(H * b.n + (g + 1) * G))
                    dve.reciprocal(inverse[:, g * G:(g + 1) * G], sums[b.par][:, g * G:(g + 1) * G])
                    dve.drain()
                    bank = psO[(b.par * NG + g) % 2]
                    dve.tensor_tensor(o[:, g * G * dh:(g + 1) * G * dh].rearrange("t (h e) -> t h e", e=dh),
                                      bank[0:T, 0:G * dh].rearrange("t (h e) -> t h e", e=dh),
                                      inverse[:, g * G:(g + 1) * G].unsqueeze(2).broadcast_to([T, G, dh]),
                                      ALU.mult).then_inc(o_ready.sem, 1)

                def heads(b, b_first, b_last, split_next=True):
                    where = slots(b_first)
                    tails = [p for p in every if p[0] in "OY"]
                    for h in range(H):
                        head_max(b, h)
                        if not (b_first and h < 1):
                            take_probsT(*before(b, h, 1))
                        if h == 1 and not b_last:
                            normalise_start(b + 1)
                        if h == 3 and not b_first:
                            divide(b + -1, NG - 1)
                        if h == 4 and not b_last:
                            normalise_end(b + 1)
                        if h == 6 and mask and not b_last:
                            bar(b + 1)
                        if wide and not b_last and h in (12, 14):
                            low_queries(b + 1, (h - 12) // 2)
                            dve.drain()
                        if NG == 2 and h == 11:
                            divide(b, 0)
                        for p, d in pieces_at(h, b_first, b_last):
                            take(p, b + d, where[p][0] if not b_last else tails.index(p) % 2)
                        if wide and not b_last:
                            if h == 8 and split_next:
                                split_ctx(b + 2)
                            if h in (11, 13):
                                high_queries(b + 1, (h - 11) // 2)

                def first(b):
                    if wide:
                        split_ctx(b)
                        split_ctx(b + 1)
                    normalise_start(b)
                    normalise_end(b)
                    if mask:
                        bar(b)
                    where = first_slots()
                    for p in first_pieces:
                        take(p, b, where[p][0])
                        if wide and p[0] == "Q":
                            high_queries(b, int(p[1]))
                            low_queries(b, int(p[1]))
                            dve.drain()

                def tail(b):
                    take_probsT(b, H - 1)
                    divide(b, NG - 1)
                    where = last_slots()
                    for p in [p for p in every if p[0] in "OY"]:
                        take(p, b, where[p][0])

                dve.wait_ge(weights.sem, weights.at(16 * nweights))
                if wide:
                    for whole, low, high in ((wk, wk_lo, wk_hi), (wv, wv_lo, wv_hi)):
                        dve.tensor_copy(high[:, :, :], whole)
                        dve.drain()
                        dve.tensor_tensor(low[:, :, :], whole, high[:, :, :].bitcast(F32), ALU.subtract)\
                            .then_inc(w_split.sem, 1)
                    dve.memset(ctxT[:, :, S:SP], 0.0)
                    dve.drain()
                if biased and EC > 2:
                    dve.tensor_scalar(bq[:, :], bq[:, :], scale, None, ALU.mult)
                if mask:
                    dve.tensor_copy(stepsf[:, :], steps[:, :]).then_inc(setup_done.sem, 1)
                    dve.wait_ge(cums.sem, cums.at(1))
                    dve.tensor_copy(last_key[:, :], psS[0][0:T, 0:B]).then_inc(setup_done.sem, 1)
                dve.drain()
                run(heads, first, None, tail, dve)

        weights.stage_over(16 * nweights)
        if wide:
            ctx_here[0].stage_over(16 * B)
            w_split.stage_over(2)
            ctx_split.stage_over(B)
            k_high.stage_over(B * EC)
            q_split.stage_over(B * NQ)
        else:
            for s in ctx_here:
                s.stage_over(16 * B // 2)
        for s in (var_ready, rstd_ready, normed_ready):
            s.stage_over(B)
        for s in (scored, maxed, exped, turned, probsT_ready, pv_done):
            s.stage_over(B * H)
        o_ready.stage_over(B * NG)
        if mask:
            barred_ready.stage_over(B)
            setup_done.stage_over(2)
            cums.stage_over(1)
        for c in "LQKVOY":
            made[c].stage_over(B * per_batch[c])
            taken[c].stage_over(B * per_batch[c])


def normalise_start(dve, stats, src, var_ready):
    dve.bn_stats(stats[:, 0:6], src)
    dve.drain()
    dve.bn_aggr(stats[:, 6:8], stats[:, 0:6])
    dve.drain()
    dve.tensor_scalar(stats[:, 8:9], stats[:, 7:8], 1e-5, None, ALU.add).then_inc(var_ready.sem, 1)


def batch_row(t, b):
    return t[:, bass.ds(b.n, 1), :].rearrange("t a d -> t (a d)")


def pair_loop(engine, body, n):
    with engine.Fori(0, n // 2) as i:
        body(Batch(i, 0))
        body(Batch(i, 1))


def route(nc, core, name, w, E, topk, how, tile):
    affine = "g" in w
    src = core.held["y"] if affine else core.x
    biased = "bg" in w
    BE = B * E
    NT = core.tiles[name] if tile else 0
    M = -(-B * T // tile) if tile else 0
    slots = core.slots_in

    ctx = ExitStack()
    with ctx:
        def sb(n, shape, dt=F32):
            return ctx.enter_context(nc.sbuf_tensor(f"{name}_route_{n}", shape, dt))

        wg = sb("wg", [P, DC, E])
        stats = sb("stats", [T, 16])
        normed = [sb(f"normed{i}", [T, D]) for i in range(2)]
        hT = [sb(f"hT{i}", [P, DC, T]) for i in range(2)]
        logits, logits2, eq1, eq2, both, scratch = (sb(n, [T, B, E]) for n in
                                                    ("logits", "logits2", "eq1", "eq2", "both", "scratch"))
        at_expert = sb("at_expert", [T, E])
        m1, m2, i1, i2, total, kept, place = (sb(n, [T, B]) for n in ("m1", "m2", "i1", "i2", "total", "kept", "place"))
        if affine:
            gain, shift = sb("gain", [T, D]), sb("shift", [T, D])
        if biased:
            bg = sb("bg", [T, E])
        if tile:
            upto = sb("upto", [T, T])
            sums_eb, scan, keepgoing = (sb(n, [T, E, B]) for n in ("sums_eb", "scan", "keepgoing"))
            base = sb("base", [T, E, B])
            steps = sb("steps", [T, E, M])
            over = sb("over", [T, E, M])
            ntiles, ends, starts = (sb(n, [T, E]) for n in ("ntiles", "ends", "starts"))
            tiles = sb("tiles", [1, NT, E])
            tiles_cmp = sb("tiles_cmp", [1, NT, E])
            eidf = sb("eidf", [1, NT])
            spare = sb("spare", [T, topk, B])
        weights = core.counter("weights")
        var_ready = core.counter("var_ready")
        rstd_ready = core.counter("rstd_ready")
        normed_ready = core.counter("normed_ready")
        made_L, taken_L = core.counter("made_L"), core.counter("taken_L")
        made_G, taken_G = core.counter("made_G"), core.counter("taken_G")
        kept_copy = core.counter("kept_copy")
        to_exp, exped = core.counter("maxed"), core.counter("exped")
        to_count, counted = core.counter("setup_done"), core.counter("cums")
        slots_ready = core.counter("o_ready")
        scattered = core.counter("scattered")
        loads = [(wg, w["wg"])]
        if affine:
            loads += [(gain, w["g"].partition_broadcast(T)), (shift, w["b"].partition_broadcast(T))]
        if biased:
            loads += [(bg, w["bg"].partition_broadcast(T))]
        loads += [(at_expert, core.consts["at_expert%d" % E].partition_broadcast(T))]
        if tile:
            loads += [(upto, core.consts["upto"]), (keepgoing, core.consts["keepgoing"].partition_broadcast(T)),
                      (spare, core.consts["spare"][:, 0:topk, :])]
            if how == "cap":
                loads += [(starts, core.consts["cap_starts"].partition_broadcast(T))]
            else:
                loads += [(steps, core.consts[f"steps_{name}"].partition_broadcast(T)),
                          (tiles, core.consts[f"tiles_{name}"].unsqueeze(0))]
        psL, psG = core.bank[0:2], core.bank[2:4]
        pos, tot = core.bank[4], core.bank[5]

        with nc.Block() as block:

            @block.sync
            def _(sp):
                for dst, s in loads:
                    sp.dma_start(dst[tuple([slice(None)] * len(dst.shape))], s).then_inc(weights.sem, 16)

            @block.gpsimd
            def _(pool):
                with pool.Fori(0, B) as i:
                    pool.wait_ge(var_ready.sem, var_ready.at(i + 1))
                    pool.tensor_tensor(stats[:, 9:10], stats[:, 8:9], core.neg_half[0:T, :], ALU.pow)\
                        .then_inc(rstd_ready.sem, 1)
                if tile:
                    pool.wait_ge(slots_ready.sem, slots_ready.at(1))
                    for b in range(B):
                        for k in range(topk):
                            pool.indirect_dma_start(
                                out=slots[:, :],
                                out_offset=bass.IndirectOffsetOnAxis(ap=core.slot_in[:, k, b:b + 1], axis=0),
                                in_=core.held["h_all"][:, b, :], in_offset=None).then_inc(scattered.sem, 16)
                    pool.wait_ge(scattered.sem, scattered.at(16 * B * topk))

            @block.tensor
            def _(pe):
                pe.wait_ge(weights.sem, weights.at(16 * len(loads)))

                def body(b):
                    pe.wait_ge(normed_ready.sem, normed_ready.at(b.n + 1))
                    pe.wait_ge(taken_L.sem, taken_L.at(b.n - 1))
                    for k in range(DC):
                        ins = pe.transpose(psL[b.par][:, k * T:(k + 1) * T], normed[b.par][:, k * P:(k + 1) * P],
                                           core.ident[0:T, 0:T])
                    ins.then_inc(made_L.sem, 1)
                    pe.wait_ge(taken_L.sem, taken_L.at(b.n + 1))
                    pe.wait_ge(taken_G.sem, taken_G.at(b.n - 1))
                    for k in range(DC):
                        ins = pe.matmul(psG[b.par][0:T, 0:E], hT[b.par][:, k, :], wg[:, k, :],
                                        start=(k == 0), stop=(k == DC - 1))
                    ins.then_inc(made_G.sem, 1)

                pair_loop(pe, body, B)
                if tile:
                    pe.wait_ge(to_count.sem, to_count.at(1))
                    pe.matmul(pos[0:T, 0:BE], upto[:, :], both[:, :, :].rearrange("t b e -> t (b e)"),
                              start=True, stop=True)
                    pe.matmul(tot[0:T, 0:BE], core.ones[0:T, 0:T], both[:, :, :].rearrange("t b e -> t (b e)"),
                              start=True, stop=True).then_inc(counted.sem, 1)

            @block.scalar
            def _(act):
                act.preload_act_table(ACT.Exp)

                def body(b):
                    act.wait_ge(made_L.sem, made_L.at(b.n + 1))
                    src_ = psL[b.par][:, 0:DC * T].rearrange("p (k t) -> p k t", t=T)
                    act.activation(hT[b.par][:, :, :], src_, ACT.Copy).then_inc(taken_L.sem, 1)
                    if tile:
                        act.activation(batch_row(core.held["h_all"], b), normed[b.par][:, :], ACT.Copy).then_inc(kept_copy.sem, 1)
                    else:
                        act.activation(core.held["hT_all"][:, :, bass.ds(b.n * T, T)], src_, ACT.Copy).then_inc(kept_copy.sem, 1)

                pair_loop(act, body, B)
                act.wait_ge(to_exp.sem, to_exp.at(1))
                act.activation(scratch[:, :, :], scratch[:, :, :], ACT.Exp).then_inc(exped.sem, 1)

            @block.vector
            def _(dve):
                v = dve
                v.wait_ge(weights.sem, weights.at(16 * len(loads)))

                def take_logits(b):
                    v.wait_ge(made_G.sem, made_G.at(b.n + 1))
                    dst = logits[:, bass.ds(b.n, 1), :].rearrange("t a e -> t (a e)")
                    if biased:
                        v.tensor_tensor(dst, psG[b.par][0:T, 0:E], bg[:, :], ALU.add).then_inc(taken_G.sem, 1)
                    else:
                        v.tensor_copy(dst, psG[b.par][0:T, 0:E]).then_inc(taken_G.sem, 1)

                def body(b):
                    normalise_start(v, stats, batch_row(src, b), var_ready)
                    v.wait_ge(kept_copy.sem, kept_copy.at(b.n - 1))
                    v.wait_ge(rstd_ready.sem, rstd_ready.at(b.n + 1))
                    n = normed[b.par][:, :]
                    ins = v.tensor_scalar(n, batch_row(src, b), stats[:, 6:7], stats[:, 9:10], ALU.subtract, ALU.mult)
                    if affine:
                        v.drain()
                        v.tensor_tensor(n, n, gain[:, :], ALU.mult)
                        v.drain()
                        ins = v.tensor_tensor(n, n, shift[:, :], ALU.add)
                    ins.then_inc(normed_ready.sem, 1)
                    take_logits(b)

                pair_loop(v, body, B)

                def over_e(t):
                    return t[:, :].unsqueeze(2).broadcast_to([T, B, E])

                def over_b(t):
                    return t[:, :].unsqueeze(1).broadcast_to([T, B, E])

                v.drain()

                def first_best(l, m, i, eq):
                    v.tensor_reduce(m[:, :], l[:, :, :], AX, ALU.max)
                    v.drain()
                    v.tensor_tensor(eq[:, :, :], l[:, :, :], over_e(m), ALU.is_equal)
                    v.drain()
                    v.tensor_tensor(eq[:, :, :], eq[:, :, :], over_b(at_expert), ALU.mult)
                    v.drain()
                    v.tensor_reduce(i[:, :], eq[:, :, :], AX, ALU.min)
                    v.drain()
                    v.tensor_tensor(eq[:, :, :], over_b(at_expert), over_e(i), ALU.is_equal)
                    v.drain()

                first_best(logits, m1, i1, eq1)
                v.tensor_tensor(scratch[:, :, :], logits[:, :, :], over_e(m1), ALU.subtract).then_inc(to_exp.sem, 1)
                if topk == 2:
                    v.scalar_tensor_tensor(out=logits2[:, :, :], in0=eq1[:, :, :], scalar=NEG, in1=logits[:, :, :],
                                           op0=ALU.mult, op1=ALU.add)
                    v.drain()
                    first_best(logits2, m2, i2, eq2)
                    v.tensor_tensor(both[:, :, :], eq1[:, :, :], eq2[:, :, :], ALU.add).then_inc(to_count.sem, 1)
                else:
                    v.tensor_copy(both[:, :, :], eq1[:, :, :]).then_inc(to_count.sem, 1)
                v.wait_ge(exped.sem, exped.at(1))
                v.drain()
                if how in ("pair", "dense"):
                    v.tensor_tensor(scratch[:, :, :], scratch[:, :, :], both[:, :, :], ALU.mult)
                    v.drain()
                v.tensor_reduce(total[:, :], scratch[:, :, :], AX, ALU.add)
                v.drain()
                v.reciprocal(total[:, :], total[:, :])
                v.drain()
                if how == "dense":
                    v.memset(core.held["comb"][:, :, E:], 1.0)
                    v.tensor_tensor(core.held["comb"][:, :, 0:E], scratch[:, :, :], over_e(total), ALU.mult)
                    v.drain()
                if tile:
                    gate = core.gate
                    for k, eq in enumerate((eq1, eq2)[:topk]):
                        v.tensor_tensor(logits2[:, :, :], scratch[:, :, :], eq[:, :, :], ALU.mult)
                        v.drain()
                        v.tensor_reduce(m1[:, :], logits2[:, :, :], AX, ALU.add)
                        v.drain()
                        v.tensor_tensor(gate[:, k, :], m1[:, :], total[:, :], ALU.mult)
                        v.drain()
                    v.wait_ge(counted.sem, counted.at(1))
                    v.tensor_copy(sums_eb[:, :, :].rearrange("t e b -> t b e"),
                                  tot[0:T, 0:BE].rearrange("t (b e) -> t b e", e=E))
                    v.drain()
                    flat = "t e b -> t (e b)"
                    v.tensor_tensor_scan(scan[:, :, :].rearrange(flat), keepgoing[:, :, :].rearrange(flat),
                                         sums_eb[:, :, :].rearrange(flat), 0.0, ALU.mult, ALU.add)
                    v.drain()
                    if how != "cap":
                        v.tensor_tensor(over[:, :, :], scan[:, :, B - 1:B].broadcast_to([T, E, M]), steps[:, :, :], ALU.is_gt)
                        v.drain()
                        v.tensor_reduce(ntiles[:, :], over[:, :, :], AX, ALU.add)
                        v.drain()
                        v.tensor_tensor_scan(ends[:, :], core.ones[0:T, 0:E], ntiles[:, :], 0.0, ALU.mult, ALU.add)
                        v.drain()
                        v.tensor_tensor(starts[:, :], ends[:, :], ntiles[:, :], ALU.subtract)
                        v.drain()
                        v.tensor_scalar(starts[:, :], starts[:, :], float(tile), None, ALU.mult)
                        v.drain()
                        v.tensor_tensor(tiles_cmp[:, :, :], tiles[:, :, :],
                                        ends[0:1, :].unsqueeze(1).broadcast_to([1, NT, E]), ALU.is_ge)
                        v.drain()
                        v.tensor_reduce(eidf[:, :], tiles_cmp[:, :, :], AX, ALU.add)
                        v.drain()
                        v.tensor_scalar(eidf[:, :], eidf[:, :], float(E - 1), None, ALU.min)
                        v.drain()
                        v.tensor_copy(core.eid[0:1, 0:NT], eidf[:, :])
                    v.tensor_tensor(base[:, :, :], scan[:, :, :], sums_eb[:, :, :], ALU.subtract)
                    v.drain()
                    v.tensor_tensor(both[:, :, :], pos[0:T, 0:BE].rearrange("t (b e) -> t b e", e=E),
                                    base[:, :, :].rearrange("t e b -> t b e"), ALU.add)
                    v.drain()
                    for k, eq in enumerate((eq1, eq2)[:topk]):
                        v.tensor_tensor(scratch[:, :, :], both[:, :, :], eq[:, :, :], ALU.mult)
                        v.tensor_tensor(logits2[:, :, :], over_b(starts), eq[:, :, :], ALU.mult)
                        v.drain()
                        v.tensor_reduce(m1[:, :], scratch[:, :, :], AX, ALU.add)
                        v.tensor_reduce(m2[:, :], logits2[:, :, :], AX, ALU.add)
                        v.drain()
                        v.tensor_tensor(place[:, :], m1[:, :], m2[:, :], ALU.add)
                        v.drain()
                        v.tensor_scalar(place[:, :], place[:, :], -1.0, None, ALU.add)
                        v.drain()
                        if how == "cap":
                            v.tensor_scalar(kept[:, :], m1[:, :], float(tile), None, ALU.is_le)
                            v.drain()
                            v.tensor_tensor(gate[:, k, :], gate[:, k, :], kept[:, :], ALU.mult)
                            v.tensor_tensor(place[:, :], place[:, :], kept[:, :], ALU.mult)
                            v.tensor_tensor(m2[:, :], spare[:, k, :], kept[:, :], ALU.mult)
                            v.drain()
                            v.tensor_copy(core.slot_out[:, k, :], place[:, :])
                            v.tensor_tensor(m2[:, :], spare[:, k, :], m2[:, :], ALU.subtract)
                            v.drain()
                            v.tensor_tensor(place[:, :], place[:, :], m2[:, :], ALU.add)
                            v.drain()
                        else:
                            v.tensor_copy(core.slot_out[:, k, :], place[:, :])
                        v.tensor_copy(core.slot_in[:, k, :], place[:, :])
                        v.drain()
                    v.wait_ge(kept_copy.sem, kept_copy.at(B))
                    v.tensor_copy(place[:, :], m1[:, :]).then_inc(slots_ready.sem, 1)

        weights.stage_over(16 * len(loads))
        for s in (var_ready, rstd_ready, normed_ready, made_L, taken_L, made_G, taken_G, kept_copy):
            s.stage_over(B)
        to_exp.stage_over(1)
        exped.stage_over(1)
        to_count.stage_over(1)
        if tile:
            counted.stage_over(1)
            slots_ready.stage_over(1)
            scattered.stage_over(16 * B * topk)


def expert_tiles(nc, core, name, w, tile, NT, func, dynamic):
    CH = -(-tile // P)
    CW = tile // CH
    F = w["w1"].shape[3] // P
    ctx = ExitStack()
    with ctx:
        def sb(n, shape, dt=F32):
            return ctx.enter_context(nc.sbuf_tensor(f"{name}_{n}", shape, dt))

        w1 = [sb(f"w1_{i}", [P, DC, F * P]) for i in range(2)]
        w2 = [sb(f"w2_{i}", [P, F, D]) for i in range(2)]
        b1 = [sb(f"b1_{i}", [P, F]) for i in range(2)]
        b2 = [sb(f"b2_{i}", [CW, D]) for i in range(2)]
        xs = [sb(f"xs{i}", [CW, CH, D]) for i in range(2)]
        xT = sb("xT", [P, DC, tile])
        hidden = sb("hidden", [P, F, tile])
        ys = [sb(f"ys{i}", [CW, CH, D]) for i in range(2)]
        x_here = [core.counter(f"ctx_here{i}") for i in range(2)]
        w_here = [core.counter(f"w_here{i}") for i in range(2)]
        xT_made, xT_taken = core.counter("made_L"), core.counter("taken_L")
        h_made, h_taken = core.counter("made_H"), core.counter("taken_H")
        y_made, y_taken = core.counter("made_Y"), core.counter("taken_Y")
        stored = [core.counter(f"y_stored{i}") for i in range(2)]
        slots_in, slots_out = core.slots_in, core.slots_out
        psX, psH, psY = core.bank[0:2], core.bank[2:6], core.bank[6:8]
        eid = core.eid

        def rows(dram, t):
            return dram[bass.ds(t.n * tile, tile), :].rearrange("(c p) d -> p c d", p=CW)

        with nc.Block() as block:

            @block.sync
            def _(sp):
                def store(t):
                    sp.dma_start(rows(slots_out, t), ys[t.par][:, :, :]).then_inc(stored[t.par].sem, 16)

                def load(t, wait):
                    if wait:
                        sp.wait_ge(xT_made.sem, xT_made.at(t.n - 1))
                    sp.dma_start(xs[t.par][:, :, :], rows(slots_in, t)).then_inc(x_here[t.par].sem, 16)
                    if dynamic:
                        e = sp.value_load(eid[0:1, bass.ds(t.n, 1)], min_val=0, max_val=w["w1"].shape[0] - 1)
                    else:
                        e = t.n
                    if wait:
                        sp.wait_ge(h_taken.sem, h_taken.at(F * (t.n - 1)))
                    sp.dma_start(w1[t.par][:, :, :], w["w1"][bass.ds(e, 1)].rearrange("a p k f -> p (a k) f"))\
                        .then_inc(w_here[t.par].sem, 16)
                    sp.dma_start(b1[t.par][:, :], w["b1"][bass.ds(e, 1)].rearrange("a p f -> p (a f)"))\
                        .then_inc(w_here[t.par].sem, 16)
                    if wait:
                        sp.wait_ge(y_taken.sem, y_taken.at(CH * (t.n - 1)))
                        store(t + -2)
                    sp.dma_start(w2[t.par][:, :, :], w["w2"][bass.ds(e, 1)].rearrange("a p f d -> p (a f) d"))\
                        .then_inc(w_here[t.par].sem, 16)
                    sp.dma_start(b2[t.par][:, :], w["b2"][bass.ds(e, 1)].rearrange("a d -> (a d)").partition_broadcast(CW))\
                        .then_inc(w_here[t.par].sem, 16)

                load(Batch(0, 0), False)
                load(Batch(0, 1), False)
                with sp.Fori(0, (NT - 2) // 2) as i:
                    load(Batch(i, 2), True)
                    load(Batch(i, 3), True)
                if NT % 2:
                    load(Batch(0, NT - 1), True)
                for t in (NT - 2, NT - 1):
                    sp.wait_ge(y_taken.sem, y_taken.at(CH * (t + 1)))
                    store(Batch(0, t))
                for i in range(2):
                    sp.wait_ge(stored[i].sem, stored[i].at(16 * ((NT + 1 - i) // 2)))

            def run(engine, body):
                n = (NT - 1) // 2
                with engine.Fori(0, n) as i:
                    body(Batch(i, 0), False)
                    body(Batch(i, 1), False)
                for t in range(2 * n, NT):
                    body(Batch(0, t), t == NT - 1)

            @block.tensor
            def _(pe):
                def turn(t):
                    pe.wait_ge(x_here[t.par].sem, x_here[t.par].at(16 * t.half + 16))
                    pe.wait_ge(xT_taken.sem, xT_taken.at(t.n))
                    for k in range(DC):
                        for c in range(CH):
                            ins = pe.transpose(psX[k][:, c * CW:(c + 1) * CW], xs[t.par][:, c, k * P:(k + 1) * P],
                                               core.ident[0:CW, 0:CW])
                    ins.then_inc(xT_made.sem, 1)

                def body(t, last):
                    pe.wait_ge(w_here[t.par].sem, w_here[t.par].at(64 * t.half + 64))
                    pe.wait_ge(xT_taken.sem, xT_taken.at(t.n + 1))
                    for f in range(F):
                        pe.wait_ge(h_taken.sem, h_taken.at(F * t.n + (f - 3)))
                        for k in range(DC):
                            ins = pe.matmul(psH[f % 4][:, 0:tile], w1[t.par][:, k, f * P:(f + 1) * P], xT[:, k, :],
                                            start=(k == 0), stop=(k == DC - 1))
                        ins.then_inc(h_made.sem, 1)
                    if not last:
                        turn(t + 1)
                    for c in range(CH):
                        pe.wait_ge(y_taken.sem, y_taken.at(CH * t.n + (c - 1)))
                        for f in range(F):
                            if c == 0:
                                pe.wait_ge(h_taken.sem, h_taken.at(F * t.n + (f + 1)))
                            ins = pe.matmul(psY[c % 2][0:CW, 0:D], hidden[:, f, c * CW:(c + 1) * CW], w2[t.par][:, f, :],
                                            start=(f == 0), stop=(f == F - 1))
                        ins.then_inc(y_made.sem, 1)

                turn(Batch(0, 0))
                run(pe, body)

            @block.scalar
            def _(act):
                act.preload_act_table(func)

                def take_xT(t):
                    act.wait_ge(xT_made.sem, xT_made.at(t.n + 1))
                    act.activation(xT[:, 0, :], psX[0][:, 0:tile], ACT.Copy)
                    act.activation(xT[:, 1, :], psX[1][:, 0:tile], ACT.Copy).then_inc(xT_taken.sem, 1)

                def body(t, last):
                    act.wait_ge(w_here[t.par].sem, w_here[t.par].at(64 * t.half + 64))
                    for f in range(F):
                        act.wait_ge(h_made.sem, h_made.at(F * t.n + (f + 1)))
                        act.activation(hidden[:, f, :], psH[f % 4][:, 0:tile], func, bias=b1[t.par][:, f:f + 1])\
                            .then_inc(h_taken.sem, 1)
                    if not last:
                        take_xT(t + 1)

                take_xT(Batch(0, 0))
                run(act, body)

            @block.vector
            def _(dve):
                def body(t, last):
                    dve.wait_ge(w_here[t.par].sem, w_here[t.par].at(64 * t.half + 64))
                    dve.wait_ge(stored[t.par].sem, stored[t.par].at(16 * t.half))
                    for c in range(CH):
                        dve.wait_ge(y_made.sem, y_made.at(CH * t.n + (c + 1)))
                        dve.tensor_tensor(ys[t.par][:, c, :], psY[c % 2][0:CW, 0:D], b2[t.par][:, :], ALU.add)\
                            .then_inc(y_taken.sem, 1)

                run(dve, body)

        for i in range(2):
            x_here[i].stage_over(16 * ((NT + 1 - i) // 2))
            w_here[i].stage_over(64 * ((NT + 1 - i) // 2))
            stored[i].stage_over(16 * ((NT + 1 - i) // 2))
        xT_made.stage_over(NT)
        xT_taken.stage_over(NT)
        h_made.stage_over(F * NT)
        h_taken.stage_over(F * NT)
        y_made.stage_over(CH * NT)
        y_taken.stage_over(CH * NT)


def combine(nc, core, name, topk, next_loads=()):
    R = 8
    with ExitStack() as ctx:
        got = [ctx.enter_context(nc.sbuf_tensor(f"{name}_got{r}", [T, topk, D], F32)) for r in range(R)]
        gathered = [core.counter(f"gathered{r}") for r in range(R)]
        added = core.counter("taken_Y")
        with nc.Block() as block:

            @block.sync
            def _(sp):
                for dst, src in next_loads:
                    sp.dma_start(dst, src).then_inc(core.counter("weights").sem, 16)

            @block.gpsimd
            def _(pool):
                for b in range(B):
                    if b >= R:
                        pool.wait_ge(added.sem, added.at(b - R + 1))
                    for k in range(topk):
                        pool.indirect_dma_start(
                            out=got[b % R][:, k, :], out_offset=None, in_=core.slots_out[:, :],
                            in_offset=bass.IndirectOffsetOnAxis(ap=core.slot_out[:, k, b:b + 1], axis=0))\
                            .then_inc(gathered[b % R].sem, 16)

            @block.vector
            def _(dve):
                for b in range(B):
                    dve.wait_ge(gathered[b % R].sem, gathered[b % R].at(16 * topk * (b // R + 1)))
                    for k in range(topk):
                        ins = dve.scalar_tensor_tensor(out=core.x[:, b, :], in0=got[b % R][:, k, :],
                                                       scalar=core.gate[:, k, b:b + 1], in1=core.x[:, b, :],
                                                       op0=ALU.mult, op1=ALU.add)
                        if k < topk - 1:
                            dve.drain()
                    ins.then_inc(added.sem, 1)

        for r in range(R):
            gathered[r].stage_over(16 * topk * (B // R))
        added.stage_over(B)


def dense_experts(nc, core, name, w, NE):
    GT, GB = 4 * T, 4
    NG = B // GB
    ctx = ExitStack()
    with ctx:
        def sb(n, shape, dt=F32):
            return ctx.enter_context(nc.sbuf_tensor(f"{name}_{n}", shape, dt))

        wu = [sb(f"wu{i}", [P, DC, P]) for i in range(2)]
        wg = [sb(f"wg{i}", [P, DC, P]) for i in range(2)]
        wd = [sb(f"wd{i}", [P, D]) for i in range(2)]
        silu = [sb(f"silu{i}", [P, GT]) for i in range(2)]
        hidden = [sb(f"hidden{i}", [P, GT]) for i in range(2)]
        comb = [sb(f"comb{i}", [T, B]) for i in range(2)]
        w_here = [core.counter(f"w_here{i}") for i in range(2)]
        g_made, g_taken = core.counter("made_G"), core.counter("taken_G")
        u_made, u_taken = core.counter("made_H"), core.counter("taken_H")
        y_made, y_taken = core.counter("made_Y"), core.counter("taken_Y")
        psG, psU, psY = core.bank[0:2], core.bank[2:4], core.bank[4:8]

        with nc.Block() as block:

            @block.sync
            def _(sp):
                def load(e, wait):
                    if wait:
                        sp.wait_ge(y_made.sem, y_made.at(B * (e.n - 1)))
                    for dst, src in ((wg, "wg"), (wu, "wu")):
                        sp.dma_start(dst[e.par][:, :, :], w[src][bass.ds(e.n, 1)].rearrange("a p k f -> p (a k) f"))\
                            .then_inc(w_here[e.par].sem, 16)
                    sp.dma_start(wd[e.par][:, :], w["wd"][bass.ds(e.n, 1)].rearrange("a p d -> p (a d)"))\
                        .then_inc(w_here[e.par].sem, 16)

                load(Batch(0, 0), False)
                load(Batch(0, 1), False)
                with sp.Fori(0, (NE - 2) // 2) as i:
                    load(Batch(i, 2), True)
                    load(Batch(i, 3), True)

            @block.tensor
            def _(pe):
                def up(e, g):
                    n = NG * e.n + g
                    if g == 0:
                        pe.wait_ge(w_here[e.par].sem, w_here[e.par].at(48 * e.half + 48))
                    h = core.held["hT_all"][:, :, g * GT:(g + 1) * GT]
                    pe.wait_ge(g_taken.sem, g_taken.at(n - 1))
                    for k in range(DC):
                        ins = pe.matmul(psG[g % 2][:, 0:GT], wg[e.par][:, k, :], h[:, k, :],
                                        start=(k == 0), stop=(k == DC - 1))
                    ins.then_inc(g_made.sem, 1)
                    pe.wait_ge(u_taken.sem, u_taken.at(n - 1))
                    for k in range(DC):
                        ins = pe.matmul(psU[g % 2][:, 0:GT], wu[e.par][:, k, :], h[:, k, :],
                                        start=(k == 0), stop=(k == DC - 1))
                    ins.then_inc(u_made.sem, 1)

                def down(e, g):
                    pe.wait_ge(u_taken.sem, u_taken.at(NG * e.n + (g + 1)))
                    for c in range(GB):
                        pe.wait_ge(y_taken.sem, y_taken.at(B * e.n + (GB * g + c - 3)))
                        pe.matmul(psY[c][0:T, 0:D], hidden[g % 2][:, c * T:(c + 1) * T], wd[e.par][:, :],
                                  start=True, stop=True).then_inc(y_made.sem, 1)

                def body(e):
                    for g in range(NG):
                        up(e, g)
                        if g:
                            down(e, g - 1)
                    down(e, NG - 1)

                pair_loop(pe, body, NE)

            @block.scalar
            def _(act):
                act.preload_act_table(ACT.Silu)

                def body(e):
                    for g in range(NG):
                        act.wait_ge(g_made.sem, g_made.at(NG * e.n + (g + 1)))
                        act.wait_ge(u_taken.sem, u_taken.at(NG * e.n + (g - 1)))
                        act.activation(silu[g % 2][:, :], psG[g % 2][:, 0:GT], ACT.Silu).then_inc(g_taken.sem, 1)

                pair_loop(act, body, NE)

            @block.vector
            def _(dve):
                def mix(e, g):
                    dve.wait_ge(g_taken.sem, g_taken.at(NG * e.n + (g + 1)))
                    dve.wait_ge(u_made.sem, u_made.at(NG * e.n + (g + 1)))
                    dve.tensor_tensor(hidden[g % 2][:, :], silu[g % 2][:, :], psU[g % 2][:, 0:GT], ALU.mult)\
                        .then_inc(u_taken.sem, 1)

                def add(e, g):
                    for c in range(GB):
                        b = GB * g + c
                        dve.wait_ge(y_made.sem, y_made.at(B * e.n + (b + 1)))
                        dve.scalar_tensor_tensor(out=core.x[:, b, :], in0=psY[c][0:T, 0:D],
                                                 scalar=comb[e.par][:, b:b + 1], in1=core.x[:, b, :],
                                                 op0=ALU.mult, op1=ALU.add).then_inc(y_taken.sem, 1)

                def body(e):
                    dve.tensor_copy(comb[e.par][:, :],
                                    core.held["comb"][:, :, bass.ds(e.n, 1)].rearrange("t b a -> t (b a)"))
                    dve.drain()
                    for g in range(NG):
                        mix(e, g)
                        if g:
                            add(e, g - 1)
                    add(e, NG - 1)

                pair_loop(dve, body, NE)

        for i in range(2):
            w_here[i].stage_over(48 * NE // 2)
        for s in (g_made, g_taken, u_made, u_taken):
            s.stage_over(NG * NE)
        y_made.stage_over(B * NE)
        y_taken.stage_over(B * NE)


def relu_attention(nc, core, name, ctx_in, w):
    scale = float(D) ** -0.5
    ctx = ExitStack()
    with ctx:
        def sb(n, shape, dt=F32):
            return ctx.enter_context(nc.sbuf_tensor(f"{name}_{n}", shape, dt))

        wq, wk, wv = (sb(n, [P, DC, D]) for n in ("wq", "wk", "wv"))
        bq, bk, bv = sb("bq", [P, DC]), sb("bk", [P, DC]), sb("bv", [1, D])
        maskT = sb("maskT", [SJ, J, T])
        ctxT = [sb(f"ctxT{i}", [P, DC, S]) for i in range(2)]
        stats = sb("stats", [T, 16])
        normed = sb("normed", [T, D])
        hT = sb("hT", [P, DC, T])
        q = [sb(f"q{i}", [P, DC, T]) for i in range(2)]
        kT = [sb(f"kT{i}", [P, DC, S]) for i in range(2)]
        v = [sb(f"v{i}", [SJ, J, D]) for i in range(2)]
        weightsT = sb("weightsT", [SJ, J, T])
        weights = core.counter("weights")
        ctx_here = [core.counter(f"ctx_here{i}") for i in range(2)]
        var_ready = core.counter("var_ready")
        rstd_ready = core.counter("rstd_ready")
        normed_ready = core.counter("normed_ready")
        scored = core.counter("scored")
        mixed = core.counter("probsT_ready")
        made = {c: core.counter(f"made_{c}") for c in "LQKVY"}
        taken = {c: core.counter(f"taken_{c}") for c in "LQKVY"}
        loads = [(wq, w["wq"]), (wk, w["wk"]), (wv, w["wv"]), (bq, w["bq"]), (bk, w["bk"]), (bv, w["bv"]),
                 (maskT, w["maskT"])]
        psL, psQ, psK, psV, psS, psY = (core.bank[0], core.bank[1], core.bank[2:4], core.bank[4:6], core.bank[6],
                                        core.bank[7])

        def run(engine, first, heads):
            first(Batch(0, 0))
            heads(Batch(0, 0), False)
            with engine.Fori(0, (B - 2) // 2) as i:
                heads(Batch(i, 1), False)
                heads(Batch(i, 2), False)
            heads(Batch(0, B - 1), True)

        with nc.Block() as block:

            @block.sync
            def _(sp):
                for dst, s in loads:
                    sp.dma_start(dst[tuple([slice(None)] * len(dst.shape))], s).then_inc(weights.sem, 16)

                def load(b):
                    sp.dma_start(ctxT[b.par][:, :, :], ctx_in[bass.ds(b.n, 1)].rearrange("a p c s -> p (a c) s"))\
                        .then_inc(ctx_here[b.par].sem, 16)

                load(Batch(0, 0))
                load(Batch(0, 1))
                with sp.Fori(0, (B - 2) // 2) as i:
                    for k in (2, 3):
                        b = Batch(i, k)
                        sp.wait_ge(made["V"].sem, made["V"].at(J * (b.n - 1)))
                        load(b)

            @block.gpsimd
            def _(pool):
                with pool.Fori(0, B) as i:
                    pool.wait_ge(var_ready.sem, var_ready.at(i + 1))
                    pool.tensor_tensor(stats[:, 9:10], stats[:, 8:9], core.neg_half[0:T, :], ALU.pow)\
                        .then_inc(rstd_ready.sem, 1)

            @block.tensor
            def _(pe):
                pe.wait_ge(weights.sem, weights.at(16 * len(loads)))

                def keys(b):
                    pe.wait_ge(ctx_here[b.par].sem, ctx_here[b.par].at(16 * b.half + 16))
                    pe.wait_ge(taken["K"].sem, taken["K"].at(DC * b.n))
                    for c in range(DC):
                        for k in range(DC):
                            ins = pe.matmul(psK[c][:, 0:S], wk[:, k, c * P:(c + 1) * P], ctxT[b.par][:, k, :],
                                            start=(k == 0), stop=(k == DC - 1))
                        ins.then_inc(made["K"].sem, 1)

                def queries(b):
                    pe.wait_ge(normed_ready.sem, normed_ready.at(b.n + 1))
                    for k in range(DC):
                        ins = pe.transpose(psL[:, k * T:(k + 1) * T], normed[:, k * P:(k + 1) * P], core.ident[0:T, 0:T])
                    ins.then_inc(made["L"].sem, 1)

                def queries_end(b):
                    pe.wait_ge(taken["L"].sem, taken["L"].at(b.n + 1))
                    pe.wait_ge(taken["Q"].sem, taken["Q"].at(b.n))
                    for c in range(DC):
                        for k in range(DC):
                            ins = pe.matmul(psQ[:, c * T:(c + 1) * T], wq[:, k, c * P:(c + 1) * P], hT[:, k, :],
                                            start=(k == 0), stop=(k == DC - 1))
                    ins.then_inc(made["Q"].sem, 1)

                def values(b, j):
                    pe.wait_ge(taken["V"].sem, taken["V"].at(J * b.n + (j - 1)))
                    for k in range(DC):
                        pe.matmul(psV[(b.par * J + j) % 2][0:SJ, 0:D], ctxT[b.par][:, k, j * SJ:(j + 1) * SJ],
                                  wv[:, k, :], start=(k == 0), stop=False)
                    pe.matmul(psV[(b.par * J + j) % 2][0:SJ, 0:D], core.ones[0:1, 0:SJ], bv[0:1, :],
                              start=False, stop=True).then_inc(made["V"].sem, 1)

                def first(b):
                    keys(b)
                    queries(b)
                    for j in range(J):
                        values(b, j)
                    queries_end(b)

                def heads(b, last):
                    pe.wait_ge(taken["Q"].sem, taken["Q"].at(b.n + 1))
                    pe.wait_ge(taken["K"].sem, taken["K"].at(DC * b.n + DC))
                    for j in range(J):
                        for k in range(DC):
                            ins = pe.matmul(psS[0:SJ, j * T:(j + 1) * T], kT[b.par][:, k, j * SJ:(j + 1) * SJ],
                                            q[b.par][:, k, :], start=(k == 0), stop=(k == DC - 1))
                    ins.then_inc(scored.sem, 1)
                    if not last:
                        keys(b + 1)
                        queries(b + 1)
                        values(b + 1, 0)
                        queries_end(b + 1)
                        values(b + 1, 1)
                        values(b + 1, 2)
                    pe.wait_ge(mixed.sem, mixed.at(b.n + 1))
                    pe.wait_ge(taken["V"].sem, taken["V"].at(J * b.n + J))
                    pe.wait_ge(taken["Y"].sem, taken["Y"].at(b.n))
                    for j in range(J):
                        ins = pe.matmul(psY[0:T, 0:D], weightsT[:, j, :], v[b.par][:, j, :],
                                        start=(j == 0), stop=(j == J - 1))
                    ins.then_inc(made["Y"].sem, 1)

                run(pe, first, heads)

            @block.scalar
            def _(act):
                act.preload_act_table(ACT.Relu)
                act.wait_ge(weights.sem, weights.at(16 * len(loads)))

                def take(b):
                    for c in range(DC):
                        act.wait_ge(made["K"].sem, made["K"].at(DC * b.n + (c + 1)))
                        act.activation(kT[b.par][:, c, :], psK[c][:, 0:S], ACT.Relu, bias=bk[:, c:c + 1])\
                            .then_inc(taken["K"].sem, 1)
                    act.wait_ge(made["L"].sem, made["L"].at(b.n + 1))
                    act.activation(hT[:, :, :], psL[:, 0:DC * T].rearrange("p (k t) -> p k t", t=T), ACT.Copy)\
                        .then_inc(taken["L"].sem, 1)

                def take_values(b, j):
                    act.wait_ge(made["V"].sem, made["V"].at(J * b.n + (j + 1)))
                    act.activation(v[b.par][:, j, :], psV[(b.par * J + j) % 2][0:SJ, 0:D], ACT.Relu)\
                        .then_inc(taken["V"].sem, 1)

                def take_queries(b):
                    act.wait_ge(made["Q"].sem, made["Q"].at(b.n + 1))
                    for c in range(DC):
                        ins = act.activation(q[b.par][:, c, :], psQ[:, c * T:(c + 1) * T], ACT.Relu, bias=bq[:, c:c + 1])
                    ins.then_inc(taken["Q"].sem, 1)

                def first(b):
                    take(b)
                    for j in range(J):
                        take_values(b, j)
                    take_queries(b)

                def heads(b, last):
                    if not last:
                        take(b + 1)
                        take_values(b + 1, 0)
                        take_queries(b + 1)
                        take_values(b + 1, 1)
                        take_values(b + 1, 2)

                run(act, first, heads)

            @block.vector
            def _(dve):
                dve.wait_ge(weights.sem, weights.at(16 * len(loads)))

                def normalise_end(b):
                    dve.wait_ge(rstd_ready.sem, rstd_ready.at(b.n + 1))
                    dve.tensor_scalar(normed[:, :], batch_row(core.x, b), stats[:, 6:7], stats[:, 9:10],
                                      ALU.subtract, ALU.mult).then_inc(normed_ready.sem, 1)

                def first(b):
                    normalise_start(dve, stats, batch_row(core.x, b), var_ready)
                    normalise_end(b)

                def heads(b, last):
                    if not last:
                        normalise_start(dve, stats, batch_row(core.x, b + 1), var_ready)
                    dve.wait_ge(scored.sem, scored.at(b.n + 1))
                    if not last:
                        normalise_end(b + 1)
                    src = psS[0:SJ, 0:J * T].rearrange("p (j t) -> p j t", t=T)
                    dve.tensor_scalar(weightsT[:, :, :], src, scale, 0.0, ALU.mult, ALU.max)
                    dve.drain()
                    dve.tensor_tensor(weightsT[:, :, :], weightsT[:, :, :], maskT[:, :, :], ALU.add)\
                        .then_inc(mixed.sem, 1)
                    dve.wait_ge(made["Y"].sem, made["Y"].at(b.n + 1))
                    dve.scalar_tensor_tensor(out=batch_row(core.x, b), in0=psY[0:T, 0:D], scalar=0.0,
                                             in1=batch_row(core.x, b), op0=ALU.max, op1=ALU.add)\
                        .then_inc(taken["Y"].sem, 1)

                run(dve, first, heads)

        weights.stage_over(16 * len(loads))
        for s in ctx_here:
            s.stage_over(16 * B // 2)
        for s in (var_ready, rstd_ready, normed_ready, scored, mixed, made["L"], taken["L"], made["Q"], taken["Q"],
                  made["Y"], taken["Y"]):
            s.stage_over(B)
        for s, n in ((made["K"], DC), (taken["K"], DC), (made["V"], J), (taken["V"], J)):
            s.stage_over(B * n)


def self_attention(nc, core, name, w):
    HG, G = 4, 4
    ctx = ExitStack()
    with ctx:
        def sb(n, shape, dt=F32):
            return ctx.enter_context(nc.sbuf_tensor(f"{name}_{n}", shape, dt))

        wqkv, wo = sb("wqkv", [P, DC, 3 * D]), sb("wo", [P, DC, D])
        gain, shift = sb("gain", [P, DC]), sb("shift", [P, DC])
        cos, sin, causal = sb("cos", [T, 16]), sb("sin", [T, 16]), sb("causal", [T, T])
        headmask = sb("headmask", [P, 8])
        stats = sb("stats", [T, 16])
        normed = sb("normed", [T, D])
        hT = sb("hT", [P, DC, T])
        turned_by, turned_q = sb("turned_by", [T, 2 * H, 16]), sb("turned_q", [T, 2 * H, 16])
        qT = [sb(f"qT{i}", [P, DC, T]) for i in range(2)]
        keys = [sb(f"keys{i}", [P, H, T]) for i in range(2)]
        causal_b = sb("causal_b", [T, T], BF16)
        v = [sb(f"v{i}", [T, D]) for i in range(2)]
        probs = [sb(f"probs{i}", [T, G, T]) for i in range(2)]
        probsT = [sb(f"probsT{i}", [T, G, T]) for i in range(2)]
        negmax = [sb(f"negmax{i}", [T, H]) for i in range(2)]
        sums = [sb(f"sums{i}", [T, H]) for i in range(2)]
        inverse = sb("inverse", [T, H])
        o, oT = sb("o", [T, D]), sb("oT", [P, DC, T])
        mask_ready = core.counter("barred_ready")
        weights = core.counter("weights")
        var_ready = core.counter("var_ready")
        rstd_ready = core.counter("rstd_ready")
        normed_ready = core.counter("normed_ready")
        scored, maxed = core.counter("scored"), core.counter("maxed")
        exped, turned = core.counter("exped"), core.counter("turned")
        probsT_ready, pv_done = core.counter("probsT_ready"), core.counter("pv_done")
        o_ready = core.counter("o_ready")
        qk_made, rope_done = core.counter("qkv_made"), core.counter("rope_done")
        r_made = core.counter("made_K")
        keys_ready, q_ready = core.counter("taken_K"), core.counter("taken_Q")
        made = {c: core.counter(f"made_{c}") for c in "LVOY"}
        taken = {c: core.counter(f"taken_{c}") for c in "LVOY"}
        loads = [(wqkv, w["wqkv"]), (wo, w["wo"]), (gain, w["g"]), (shift, w["b"]), (cos, w["cos"]), (sin, w["sin"]),
                 (causal, w["causal"]), (headmask, w["headmask"])]
        psL, psQK, psV, psR = core.bank[0], core.bank[1], core.bank[2], core.bank[3]
        psS, psT, psO = core.bank[4:6], core.bank[6], core.bank[7]

        def run(engine, first, heads):
            first()
            heads(Batch(0, 0), False, True, True, True)
            with engine.Fori(0, (B - 4) // 2) as i:
                heads(Batch(i, 1), True, True, True, True)
                heads(Batch(i, 2), True, True, True, True)
            for n in range(B - 3, B):
                heads(Batch(0, n), True, n + 1 < B, n + 2 < B, n + 3 < B)

        with nc.Block() as block:

            @block.sync
            def _(sp):
                for dst, s in loads:
                    sp.dma_start(dst[tuple([slice(None)] * len(dst.shape))], s).then_inc(weights.sem, 16)

            @block.gpsimd
            def _(pool):
                with pool.Fori(0, 2 * B) as i:
                    pool.wait_ge(var_ready.sem, var_ready.at(i + 1))
                    pool.tensor_tensor(stats[:, 9:10], stats[:, 8:9], core.neg_half[0:T, :], ALU.pow)\
                        .then_inc(rstd_ready.sem, 1)

            @block.tensor
            def _(pe):
                pe.wait_ge(weights.sem, weights.at(16 * len(loads)))

                def turn_tokens(b, before_):
                    pe.wait_ge(normed_ready.sem, normed_ready.at(b.n + 1))
                    if before_:
                        pe.wait_ge(taken["O"].sem, taken["O"].at(b.n - 2))
                    pe.wait_ge(taken["L"].sem, taken["L"].at(b.n))
                    for k in range(DC):
                        ins = pe.transpose(psL[:, k * T:(k + 1) * T], normed[:, k * P:(k + 1) * P], core.ident[0:T, 0:T])
                    ins.then_inc(made["L"].sem, 1)

                def project_qk(b):
                    pe.wait_ge(taken["L"].sem, taken["L"].at(b.n + 1))
                    pe.wait_ge(rope_done.sem, rope_done.at(b.n))
                    for k in range(DC):
                        ins = pe.matmul(psQK[0:T, 0:2 * D], hT[:, k, :], wqkv[:, k, 0:2 * D],
                                        start=(k == 0), stop=(k == DC - 1))
                    ins.then_inc(qk_made.sem, 1)

                def project_v(b):
                    pe.wait_ge(taken["V"].sem, taken["V"].at(b.n))
                    for k in range(DC):
                        ins = pe.matmul(psV[0:T, 0:D], hT[:, k, :], wqkv[:, k, 2 * D:3 * D],
                                        start=(k == 0), stop=(k == DC - 1))
                    ins.then_inc(made["V"].sem, 1)

                def turn_rotated(b, before_):
                    pe.wait_ge(rope_done.sem, rope_done.at(b.n + 1))
                    if before_:
                        pe.wait_ge(taken["Y"].sem, taken["Y"].at(b.n - 2))
                    for c in range(2 * DC):
                        ins = pe.transpose(psR[:, c * T:(c + 1) * T],
                                           turned_q[:, c * 8:(c + 1) * 8, :].rearrange("t h e -> t (h e)"),
                                           core.ident[0:T, 0:T])
                    ins.then_inc(r_made.sem, 1)

                def scores(b, g):
                    if g == 0:
                        pe.wait_ge(q_ready.sem, q_ready.at(b.n + 1))
                        pe.wait_ge(keys_ready.sem, keys_ready.at(b.n + 1))
                    pe.wait_ge(exped.sem, exped.at(HG * b.n + (g - 1)))
                    pe.matmul(psS[g % 2][0:T, 0:G * T], core.ident_b[0:T, 0:T],
                              causal_b[:, :].unsqueeze(1).broadcast_to([T, G, T]), start=True, stop=False)
                    pe.matmul(psS[g % 2][0:T, 0:G * T], qT[b.par][:, g // 2, :], keys[b.par][:, G * g:G * g + G, :],
                              start=False, stop=True).then_inc(scored.sem, 1)

                def turn(b, g):
                    pe.wait_ge(exped.sem, exped.at(HG * b.n + (g + 1)))
                    for h in range(G):
                        ins = pe.transpose(psT[0:T, h * T:(h + 1) * T], probs[g % 2][:, h, :], core.ident[0:T, 0:T])
                    ins.then_inc(turned.sem, 1)

                def values(b, g):
                    pe.wait_ge(probsT_ready.sem, probsT_ready.at(HG * b.n + (g + 1)))
                    if g == 0:
                        pe.wait_ge(taken["V"].sem, taken["V"].at(b.n + 1))
                        pe.wait_ge(o_ready.sem, o_ready.at(b.n))
                    for h in range(G):
                        at = (G * g + h) * 16
                        ins = pe.matmul(psO[0:T, at:at + 16], probsT[g % 2][:, h, :], v[b.par][:, at:at + 16],
                                        start=True, stop=True)
                    ins.then_inc(pv_done.sem, 1)

                def turn_outputs(b, after):
                    pe.wait_ge(o_ready.sem, o_ready.at(b.n + 1))
                    if after:
                        pe.wait_ge(taken["L"].sem, taken["L"].at(b.n + 3))
                    for c in range(DC):
                        ins = pe.transpose(psL[:, (2 + c) * T:(3 + c) * T], o[:, c * P:(c + 1) * P], core.ident[0:T, 0:T])
                    ins.then_inc(made["O"].sem, 1)

                def output(b):
                    pe.wait_ge(taken["O"].sem, taken["O"].at(b.n + 1))
                    pe.wait_ge(taken["Y"].sem, taken["Y"].at(b.n))
                    for c in range(DC):
                        ins = pe.matmul(psR[0:T, 0:D], oT[:, c, :], wo[:, c, :], start=(c == 0), stop=(c == DC - 1))
                    ins.then_inc(made["Y"].sem, 1)

                def first():
                    pe.wait_ge(mask_ready.sem, mask_ready.at(1))
                    b = Batch(0, 0)
                    turn_tokens(b, False)
                    project_qk(b)
                    project_v(b)
                    turn_tokens(b + 1, False)
                    turn_rotated(b, False)
                    project_qk(b + 1)
                    project_v(b + 1)
                    scores(b, 0)
                    scores(b, 1)

                def heads(b, prior, after, after2, after3):
                    scores(b, 2)
                    turn(b, 0)
                    if after:
                        turn_rotated(b + 1, prior)
                    values(b, 0)
                    if prior:
                        turn_outputs(b + -1, after)
                    scores(b, 3)
                    turn(b, 1)
                    if after2:
                        turn_tokens(b + 2, prior)
                    values(b, 1)
                    if after:
                        scores(b + 1, 0)
                    turn(b, 2)
                    if after2:
                        project_qk(b + 2)
                    values(b, 2)
                    if after:
                        scores(b + 1, 1)
                    turn(b, 3)
                    if prior:
                        output(b + -1)
                    values(b, 3)
                    if after2:
                        project_v(b + 2)

                run(pe, first, heads)
                turn_outputs(Batch(0, B - 1), None)
                output(Batch(0, B - 1))

            @block.scalar
            def _(act):
                act.preload_act_table(ACT.Exp)
                act.wait_ge(weights.sem, weights.at(16 * len(loads)))

                def take_tokens(b):
                    act.wait_ge(made["L"].sem, made["L"].at(b.n + 1))
                    for k in range(DC):
                        ins = act.activation(hT[:, k, :], psL[:, k * T:(k + 1) * T], ACT.Identity,
                                             bias=shift[:, k:k + 1], scale=gain[:, k:k + 1])
                    ins.then_inc(taken["L"].sem, 1)

                def take_values(b):
                    act.wait_ge(made["V"].sem, made["V"].at(b.n + 1))
                    act.activation(v[b.par][:, :], psV[0:T, 0:D], ACT.Copy).then_inc(taken["V"].sem, 1)

                def take_queries(b):
                    act.wait_ge(r_made.sem, r_made.at(b.n + 1))
                    act.activation(qT[b.par][:, :, :], psR[:, 0:DC * T].rearrange("p (c t) -> p c t", t=T), ACT.Copy)\
                        .then_inc(q_ready.sem, 1)

                def take_outputs(b):
                    act.wait_ge(made["O"].sem, made["O"].at(b.n + 1))
                    act.activation(oT[:, :, :], psL[:, 2 * T:4 * T].rearrange("p (c t) -> p c t", t=T), ACT.Copy)\
                        .then_inc(taken["O"].sem, 1)

                def exps(b, g):
                    act.wait_ge(maxed.sem, maxed.at(HG * b.n + (g + 1)))
                    for h in range(G):
                        at = G * g + h
                        ins = act.activation(probs[g % 2][:, h, :], psS[g % 2][0:T, h * T:(h + 1) * T], ACT.Exp,
                                             bias=negmax[b.par][:, at:at + 1], accum_out=sums[b.par][:, at:at + 1])
                    ins.then_inc(exped.sem, 1)

                def take_probsT(b, g):
                    act.wait_ge(turned.sem, turned.at(HG * b.n + (g + 1)))
                    act.activation(probsT[g % 2][:, :, :], psT[0:T, 0:G * T].rearrange("p (h t) -> p h t", t=T),
                                   ACT.Copy).then_inc(probsT_ready.sem, 1)

                def first():
                    b = Batch(0, 0)
                    take_tokens(b)
                    take_values(b)
                    take_tokens(b + 1)
                    take_queries(b)
                    take_values(b + 1)
                    exps(b, 0)
                    exps(b, 1)

                def heads(b, prior, after, after2, after3):
                    take_probsT(b, 0)
                    exps(b, 2)
                    if after:
                        take_queries(b + 1)
                    take_probsT(b, 1)
                    if prior:
                        take_outputs(b + -1)
                    exps(b, 3)
                    if after2:
                        take_tokens(b + 2)
                    take_probsT(b, 2)
                    if after:
                        exps(b + 1, 0)
                    take_probsT(b, 3)
                    if after:
                        exps(b + 1, 1)
                    if after2:
                        take_values(b + 2)

                run(act, first, heads)
                take_outputs(Batch(0, B - 1))

            @block.vector
            def _(dve):
                dve.wait_ge(weights.sem, weights.at(16 * len(loads)))
                dve.tensor_copy(causal_b[:, :], causal[:, :]).then_inc(mask_ready.sem, 1)

                def normalised(b, n, dst, src):
                    dve.wait_ge(rstd_ready.sem, rstd_ready.at(2 * b.n + n))
                    return dve.tensor_scalar(dst, src, stats[:, 6:7], stats[:, 9:10], ALU.subtract, ALU.mult)

                def norm_1(b):
                    normalise_start(dve, stats, batch_row(core.x, b), var_ready)

                def norm_2(b):
                    y = batch_row(core.held["y"], b)
                    normalised(b, 1, y, batch_row(core.x, b))
                    dve.drain()
                    normalise_start(dve, stats, y, var_ready)

                def norm_3(b):
                    normalised(b, 2, normed[:, :], batch_row(core.held["y"], b)).then_inc(normed_ready.sem, 1)

                def rotate(b):
                    dve.wait_ge(qk_made.sem, qk_made.at(b.n + 1))
                    qk = psQK[0:T, 0:2 * D].rearrange("t (h e) -> t h e", e=16)

                    def all_heads(t, lo, hi):
                        return t[:, lo:hi].unsqueeze(1).broadcast_to([T, 2 * H, hi - lo])

                    dve.tensor_tensor(turned_by[:, :, 0:8], qk[:, :, 8:16], all_heads(sin, 0, 8), ALU.mult)
                    dve.tensor_tensor(turned_by[:, :, 8:16], qk[:, :, 0:8], all_heads(sin, 8, 16), ALU.mult)
                    dve.tensor_tensor(turned_q[:, :, :], qk, all_heads(cos, 0, 16), ALU.mult)
                    dve.drain()
                    dve.tensor_tensor(turned_q[:, :, :], turned_q[:, :, :], turned_by[:, :, :], ALU.add)\
                        .then_inc(rope_done.sem, 1)

                def spread_keys(b):
                    dve.wait_ge(r_made.sem, r_made.at(b.n + 1))
                    dve.wait_ge(q_ready.sem, q_ready.at(b.n + 1))
                    for c in range(DC):
                        ins = dve.tensor_tensor(keys[b.par][:, 8 * c:8 * c + 8, :],
                                                psR[:, (DC + c) * T:(DC + c + 1) * T].unsqueeze(1).broadcast_to([P, 8, T]),
                                                headmask[:, :].unsqueeze(2).broadcast_to([P, 8, T]), ALU.mult)
                    ins.then_inc(keys_ready.sem, 1)

                def group_max(b, g):
                    dve.wait_ge(scored.sem, scored.at(HG * b.n + (g + 1)))
                    dve.tensor_reduce(negmax[b.par][:, G * g:G * g + G],
                                      psS[g % 2][0:T, 0:G * T].rearrange("p (h t) -> p h t", t=T), AX, ALU.max,
                                      negate=True).then_inc(maxed.sem, 1)

                def divide(b):
                    dve.wait_ge(pv_done.sem, pv_done.at(HG * b.n + HG))
                    dve.reciprocal(inverse[:, :], sums[b.par][:, :])
                    dve.drain()
                    dve.tensor_tensor(o[:, :].rearrange("t (h e) -> t h e", e=16),
                                      psO[0:T, 0:D].rearrange("t (h e) -> t h e", e=16),
                                      inverse[:, :].unsqueeze(2).broadcast_to([T, H, 16]), ALU.mult)\
                        .then_inc(o_ready.sem, 1)

                def add(b):
                    dve.wait_ge(made["Y"].sem, made["Y"].at(b.n + 1))
                    y, x = batch_row(core.held["y"], b), batch_row(core.x, b)
                    dve.tensor_tensor(y, psR[0:T, 0:D], y, ALU.add).then_inc(taken["Y"].sem, 1)
                    dve.drain()
                    dve.tensor_tensor(x, x, y, ALU.add)

                def first():
                    b = Batch(0, 0)
                    norm_1(b)
                    norm_2(b)
                    norm_3(b)
                    norm_1(b + 1)
                    norm_2(b + 1)
                    dve.wait_ge(made["L"].sem, made["L"].at(1))
                    norm_3(b + 1)
                    rotate(b)
                    spread_keys(b)
                    rotate(b + 1)
                    group_max(b, 0)
                    group_max(b, 1)
                    norm_1(b + 2)
                    norm_2(b + 2)

                def heads(b, prior, after, after2, after3):
                    if prior:
                        divide(b + -1)
                    group_max(b, 2)
                    if after:
                        spread_keys(b + 1)
                    if after2:
                        norm_3(b + 2)
                    group_max(b, 3)
                    if after3:
                        norm_1(b + 3)
                    if after:
                        group_max(b + 1, 0)
                    if after2:
                        rotate(b + 2)
                    if after:
                        group_max(b + 1, 1)
                    if after3:
                        norm_2(b + 3)
                    if prior:
                        add(b + -1)

                run(dve, first, heads)
                divide(Batch(0, B - 1))
                add(Batch(0, B - 1))

        weights.stage_over(16 * len(loads))
        mask_ready.stage_over(1)
        for s in (var_ready, rstd_ready):
            s.stage_over(2 * B)
        for s in (normed_ready, o_ready, qk_made, rope_done, r_made, keys_ready, q_ready, *made.values(), *taken.values()):
            s.stage_over(B)
        for s in (scored, maxed, exped, turned, probsT_ready, pv_done):
            s.stage_over(HG * B)


def decoder(nc, a, out):
    with ExitStack() as ctx:
        core = Core(nc, ctx)
        core.start_sem = ctx.enter_context(nc.semaphore("start_sem"))
        core.x = core.keep("x", [T, B, D])
        core.ident = core.keep("ident", [P, P])
        core.ident_b = core.keep("ident_b", [P, P], BF16)
        core.neg_half = core.keep("neg_half", [P, 1])
        core.ones = core.keep("ones", [P, P])
        core.gate = core.keep("gate", [T, 2, B])
        core.slot_in, core.slot_out = core.keep("slot_in", [T, 2, B], U32), core.keep("slot_out", [T, 2, B], U32)
        core.eid = core.keep("eid", [1, 32], I32)
        core.filled_sem = ctx.enter_context(nc.semaphore("filled_sem"))
        core.zeroed_sem = ctx.enter_context(nc.semaphore("zeroed_sem"))
        core.slots_in = nc.dram_tensor("slots_in", [4 * B * T, D], F32, kind="Internal").ap()
        core.slots_out = nc.dram_tensor("slots_out", [TILES["L0"] * TILE, D], F32, kind="Internal").ap()
        core.consts, core.tiles = a, TILES
        for n in SIGNALS:
            core.counter(n)
        known = set(core.counters)
        stages = STAGES(nc, core, a)
        for n, stage in enumerate(stages):
            if n < LAYERS:
                stage()
        store_end(nc, core, out)
        assert set(core.counters) == known, set(core.counters) - known


TILE = 256
CAPACITY = 2 * B * T // 8
TILES = {"L0": (2 * B * T - 8) // TILE + 8, "L1": 8, "L2": (B * T - 8) // TILE + 8}

BY_POOL_DMA = ["scattered"] + [f"gathered{r}" for r in range(8)]
SIGNALS = (["start_loaded", "stored", "weights", "ctx_here0", "ctx_here1", "var_ready", "rstd_ready", "normed_ready",
            "scored", "maxed", "exped", "turned", "probsT_ready", "pv_done", "o_ready", "setup_done", "cums",
            "kept_copy", "scattered", "w_here0", "w_here1", "y_stored0", "y_stored1"]
           + [f"{m}_{c}" for m in ("made", "taken") for c in "LQKVOYGH"] + [f"gathered{r}" for r in range(8)]
           + ["qkv_made", "rope_done", "barred_ready", "w_split", "ctx_split", "k_high", "q_split"])


def STAGES(nc, core, a):
    l0 = {n: a["L0_" + n] for n in ("wq", "wk", "wv", "wo", "bq", "bk", "bv", "bo")}
    l2 = {n: a["L2_" + n] for n in ("wq", "wk", "wv", "wo")}
    l3 = {n: a["L3_" + n] for n in ("wq", "wk", "wv", "wo", "bq", "bk", "bv", "bo")}
    m = {n: a[n] for n in ("steps", "upto", "keys", "headmask")}
    f0 = {n: a["F0_" + n] for n in ("wg", "w1", "b1", "w2", "b2")}
    f1 = {n: a["F1_" + n] for n in ("wg", "w1", "b1", "w2", "b2", "g", "b")}
    f2 = {n: a["F2_" + n] for n in ("wg", "bg", "w1", "b1", "w2", "b2")}
    f3 = {"wg": a["F3_router"], "bg": a["F3_bg"]}
    d3 = {n: a["F3_" + n] for n in ("wg", "wu", "wd")}
    x1 = {n: a["X1_" + n] for n in ("wq", "wk", "wv", "bq", "bk", "bv", "maskT")}
    s1 = {n: a["S1_" + n] for n in ("g", "b", "wqkv", "wo", "cos", "sin", "causal")}
    s1["headmask"] = a["headmask"]

    def held(tensors, *steps):
        with ExitStack() as ctx:
            for n, shape in tensors.items():
                core.times_held += 1
                core.held[n] = ctx.enter_context(nc.sbuf_tensor(f"{n}_{core.times_held}", shape, F32))
            for step in steps:
                step()

    def sparse(name, w, topk, how, tile, function, several):
        return (lambda: held({"h_all": [T, B, D]}, lambda: route(nc, core, name, w, 8, topk, how, tile)),
                lambda: expert_tiles(nc, core, name + "t", w, tile, TILES[name], function, several))

    def combine_and_attend(name, topk, next_name, w):
        def steps():
            h = core.held
            combine(nc, core, name + "c", topk,
                    [(h["v0"][:, 0:DC, :], w["wk"]), (h["v1"][:, 0:DC, :], w["wv"]),
                     (h["wq"][:, :, :], w["wq"]), (h["wo"][:, :, :], w["wo"])])
            cross_attention(nc, core, next_name, a["ctxT"], w, 64)
        E = 64 * H
        held({"wq": [P, DC, E], "wo": [P, E // P, D], "v0": [P, J, E], "v1": [P, J, E]}, steps)

    def run_all(*steps):
        for step in steps:
            step()

    route_L1, tiles_L1 = sparse("L1", f1, 2, "cap", CAPACITY, ACT.Gelu, False)
    return [
        lambda: held({"zeros": [T, B, D]},
                     lambda: load_start(nc, core, a["x"], a["ident"]),
                     lambda: cross_attention(nc, core, "L0", a["ctxT"], l0, 16, m)),
        lambda: run_all(*sparse("L0", f0, 2, "pair", TILE, ACT.Relu, True),
                        lambda: combine(nc, core, "L0c", 2)),
        lambda: relu_attention(nc, core, "L1x", a["ctxT"], x1),
        lambda: run_all(lambda: held({"y": [T, B, D]}, lambda: self_attention(nc, core, "L1s", s1), route_L1),
                        tiles_L1, lambda: combine_and_attend("L1", 2, "L2", l2)),
        lambda: run_all(*sparse("L2", f2, 1, "all", TILE, ACT.Relu, True),
                        lambda: combine_and_attend("L2", 1, "L3", l3)),
        lambda: held({"hT_all": [P, DC, B * T], "comb": [T, B, 18]},
                     lambda: route(nc, core, "L3", f3, 16, 2, "dense", None),
                     lambda: dense_experts(nc, core, "L3d", d3, 18)),
    ]


def lay_out(inputs):
    import numpy as np

    def rows(w):
        w = np.asarray(w)
        return np.ascontiguousarray(w.reshape(w.shape[0] // P, P, w.shape[1]).transpose(1, 0, 2))

    def cols(v):
        return np.ascontiguousarray(np.asarray(v).reshape(-1, P).T)

    def row(v):
        return np.ascontiguousarray(np.asarray(v).reshape(1, -1))

    i = {k: np.asarray(v) for k, v in inputs.items()}
    a = {"x": np.ascontiguousarray(i["x"]), "ident": np.eye(P, dtype=np.float32)}
    a["ctxT"] = np.ascontiguousarray(i["ctx_1024"].reshape(B, S, DC, P).transpose(0, 3, 2, 1))
    a["steps"] = np.ascontiguousarray(i["mask_BxS_ik0"].T)
    a["upto"] = np.triu(np.ones((T, T), np.float32))
    a["keys"] = np.arange(S, dtype=np.float32)
    a["headmask"] = np.where(np.arange(P)[:, None] // 16 == np.arange(8)[None, :], 0.25, 0.0).astype(np.float32)
    for n in ("wq", "wk", "wv", "wo"):
        a["L0_" + n] = rows(i["L0_xattn_" + n].T)
    for n in ("bq", "bk", "bv"):
        a["L0_" + n] = cols(i["L0_xattn_" + n])
    a["L0_bo"] = row(i["L0_xattn_bo"])
    for n in ("wq", "wk", "wv", "wo"):
        a["L2_" + n] = rows(i["L2_xattn_W" + n[1]])
    for n, m in (("q", "Query"), ("k", "Key"), ("v", "Value"), ("o", "Output")):
        a["L3_w" + n] = rows(i["L3_xattn_W_" + m])
        a["L3_b" + n] = (row if n == "o" else cols)(i["L3_xattn_B_" + m])

    def experts(w):
        w = np.asarray(w)
        return np.ascontiguousarray(w.reshape(w.shape[0], w.shape[1] // P, P, w.shape[2]).transpose(0, 2, 1, 3))

    for f, l, g in (("F0", "L0", "Wg"), ("F1", "L1", "Wgate"), ("F2", "L2", "w_gate")):
        l += "_ffn_"
        a[f + "_wg"] = rows(i[l + g])
        a[f + "_w1"], a[f + "_w2"] = experts(i[l + "W1"]), experts(i[l + "W2"])
        a[f + "_b1"] = np.ascontiguousarray(i[l + "b1"].reshape(8, -1, P).transpose(0, 2, 1))
        a[f + "_b2"] = np.ascontiguousarray(i[l + "b2"])
    a["F1_g"], a["F1_b"] = i["L1_ffn_ln2_g"], i["L1_ffn_ln2_b"]
    a["F2_bg"] = i["L2_ffn_b_gate"]
    a["F3_router"], a["F3_bg"] = rows(i["L3_ffn_router_w"].T), i["L3_ffn_router_bias"]
    for n, e, sh in (("wg", "gate_proj", "sh_gate"), ("wu", "up_proj", "sh_up")):
        shared = i["L3_ffn_" + sh].reshape(2, P, D).transpose(0, 2, 1)
        a["F3_" + n] = experts(np.concatenate([i["L3_ffn_" + e], shared]))
    a["F3_wd"] = np.ascontiguousarray(np.concatenate([i["L3_ffn_down_proj"], i["L3_ffn_sh_down"].T.reshape(2, P, D)]))
    for n in "qkv":
        a["X1_w" + n] = rows(i["L1_xattn_kernel_" + n][0, 0])
        a["X1_b" + n] = (row if n == "v" else cols)(i["L1_xattn_bias_" + n])
    a["X1_maskT"] = np.ascontiguousarray(i["mask_1xSxS2_ff0"][0].T.reshape(J, SJ, T).transpose(1, 0, 2))
    a["S1_g"], a["S1_b"] = cols(i["L1_ffn_ln1_g"]), cols(i["L1_ffn_ln1_b"])
    wqkv = i["L1_ffn_Wqkv"].reshape(D, H, 3, 16).transpose(0, 2, 1, 3).reshape(D, 3 * D)
    a["S1_wqkv"], a["S1_wo"] = rows(wqkv), rows(i["L1_ffn_Wproj"])
    angle = np.arange(T, dtype=np.float32)[:, None] * (np.float32(1) / np.float32(10000) ** (np.arange(0, 16, 2, dtype=np.float32) / np.float32(16)))
    cos, sin = np.cos(angle.astype(np.float64)), np.sin(angle.astype(np.float64))
    a["S1_cos"] = np.concatenate([cos, cos], 1).astype(np.float32)
    a["S1_sin"] = np.concatenate([-sin, sin], 1).astype(np.float32)
    a["S1_causal"] = np.where(np.arange(T)[:, None] >= np.arange(T)[None, :], 0.0, NEG).astype(np.float32)
    a["at_expert8"] = np.arange(8, dtype=np.float32) - 64
    a["at_expert16"] = np.arange(16, dtype=np.float32) - 64
    a["keepgoing"] = np.tile((np.arange(B) > 0).astype(np.float32), (8, 1))
    a["spare"] = (2 * B * T + np.arange(2 * B * T, dtype=np.float32)).reshape(T, 2, B)
    a["cap_starts"] = np.arange(8, dtype=np.float32) * CAPACITY
    for n in ("L0", "L2"):
        a["steps_" + n] = np.tile(np.arange(-(-B * T // TILE), dtype=np.float32) * TILE, (8, 1))
        a["tiles_" + n] = np.repeat(np.arange(TILES[n], dtype=np.float32)[:, None], 8, 1)
    return a


def kernel(**inputs):
    import numpy as _np
    import concourse.bacc as _bacc
    from concourse import mybir as _mybir
    from concourse.bass_utils import run_bass_kernel_spmd as _run

    nc = _bacc.Bacc("TRN2", target_bir_lowering=False, num_devices=1)
    arrays = {f"in_{k}": v for k, v in lay_out(inputs).items()}
    a = {k[3:]: nc.dram_tensor(k, v.shape, _mybir.dt.from_np(v.dtype), kind="ExternalInput").ap()
         for k, v in arrays.items()}
    out = nc.dram_tensor("out_0", (B, T, D), F32, kind="ExternalOutput").ap()
    decoder(nc, a, out)
    r = _run(nc, [arrays], core_ids=[0])
    return r.results[0]["out_0"]
```
